# Optimizing a Trainium2 kernel written in Bass

```python
import numpy as np
import jax
import jax.numpy as jnp

def _softmax(x, axis=-1):
    return jax.nn.softmax(x, axis=axis)

def _gelu(x):
    return jax.nn.gelu(x, approximate=True)

def _silu(x):
    return jax.nn.silu(x)

def _sigmoid(x):
    return jax.nn.sigmoid(x)

def _layernorm(x, axis=-1, eps=1e-05):
    m = jnp.mean(x, axis=axis, keepdims=True)
    v = jnp.var(x, axis=axis, keepdims=True)
    return (x - m) / jnp.sqrt(v + eps)

def _scatter_add(tgt, idx, src, axis=0):
    return tgt.at[idx].add(src)

def _segment_sum(src, seg, n):
    return jax.ops.segment_sum(src, seg, n)
kernel_name = 'mk_decoder_postln_d1_seqx_r8_15b9f6'

def setup_inputs(seed: int=0):
    np.random.seed(seed)
    _w = jnp.asarray

    def _rec_inputs():
        import jax
        import jax.numpy as jnp
        _rk = jax.random.key(seed)
        x = 2.818e-05 + 1 * jax.random.normal(jax.random.fold_in(_rk, 1), (4, 256, 256), jnp.float32)
        _lenS = 256 - jax.random.randint(jax.random.fold_in(_rk, 7), (4,), 0, max(1, 256 // 4) + 1, jnp.int32)
        _lenS2 = 256 - jax.random.randint(jax.random.fold_in(_rk, 8), (4,), 0, max(1, 256 // 4) + 1, jnp.int32)
        _ctx_1024P = jax.random.normal(jax.random.fold_in(_rk, 11), (4, 16, 128), jnp.float32)
        _ctx_1024c = jax.random.dirichlet(jax.random.fold_in(_rk, 511), 0.3 * jnp.ones((16,), jnp.float32), (4, 256))
        _ctx_1024t = jnp.einsum('bsk,bkd->bsd', _ctx_1024c, _ctx_1024P)
        _ctx_1024t = _ctx_1024t * jax.lax.rsqrt(jnp.mean(jnp.square(_ctx_1024t)) + 1e-12) * 0.953939
        ctx_1024 = 7.22013e-05 + 1.00017 * (_ctx_1024t + 0.3 * jax.random.normal(jax.random.fold_in(_rk, 611), (4, 256, 128), jnp.float32))
        return (x, ctx_1024)
    x, ctx_1024 = _rec_inputs()

    def _L0_attn_setup():
        import jax, jax.numpy as jnp
        import numpy as np
        import math
        D_MODEL = 256
        N_HEADS = 16
        D_HEAD = 128
        BATCH = 2
        SEQ = 256
        key = jax.random.key(seed)
        ks = jax.random.split(key, 5)
        std = 0.02
        x = jax.random.normal(ks[0], (BATCH, SEQ, D_MODEL), dtype=jnp.float32)
        W_Q = std * jax.random.normal(ks[1], (N_HEADS, D_HEAD, D_MODEL), dtype=jnp.float32)
        W_K = std * jax.random.normal(ks[2], (N_HEADS, D_HEAD, D_MODEL), dtype=jnp.float32)
        W_V = std * jax.random.normal(ks[3], (N_HEADS, D_HEAD, D_MODEL), dtype=jnp.float32)
        W_O = std * jax.random.normal(ks[4], (N_HEADS, D_MODEL, D_HEAD), dtype=jnp.float32)
        return {'x': x, 'W_Q': W_Q, 'W_K': W_K, 'W_V': W_V, 'W_O': W_O}
    _L0_attn_all = _L0_attn_setup()
    _L0_attn_in = {k: v for k, v in _L0_attn_all.items() if k in ('W_Q', 'W_K', 'W_V', 'W_O')}
    del _L0_attn_all

    def _L0_xattn_setup():
        import jax, jax.numpy as jnp
        import numpy as np
        B_, L_, D_MODEL = (4, 256, 128)
        D_STATE, D_CONV, EXPAND = (16, 4, 2)
        D_INNER = EXPAND * D_MODEL
        DT_RANK = (D_MODEL + 15) // 16

        def silu(x):
            return x * jax.nn.sigmoid(x)
        key = jax.random.key(seed)
        ks = jax.random.split(key, 10)
        f32 = jnp.float32
        hidden_states = jax.random.normal(ks[0], (B_, L_, D_MODEL), dtype=f32)
        z = jax.random.normal(ks[1], (B_, D_INNER, L_), dtype=f32)
        in_proj_w = jax.random.normal(ks[2], (D_INNER, D_MODEL), dtype=f32) * 0.02
        conv_w = jax.random.normal(ks[3], (D_INNER, 1, D_CONV), dtype=f32) * 0.1
        conv_b = jax.random.normal(ks[4], (D_INNER,), dtype=f32) * 0.02
        x_proj_w = jax.random.normal(ks[5], (DT_RANK + 2 * D_STATE, D_INNER), dtype=f32) * 0.02
        dt_proj_w = jax.random.uniform(ks[6], (D_INNER, DT_RANK), dtype=f32, minval=-DT_RANK ** (-0.5), maxval=DT_RANK ** (-0.5))
        dt = jnp.exp(jax.random.uniform(ks[7], (D_INNER,), dtype=f32, minval=np.log(0.001), maxval=np.log(0.1)))
        dt_proj_b = jnp.log(jnp.expm1(dt))
        A_log = jnp.log(jnp.broadcast_to(jnp.arange(1, D_STATE + 1, dtype=f32), (D_INNER, D_STATE)))
        D = jnp.ones((D_INNER,), f32)
        return {'hidden_states': hidden_states, 'z': z, 'in_proj_w': in_proj_w, 'conv_w': conv_w, 'conv_b': conv_b, 'x_proj_w': x_proj_w, 'dt_proj_w': dt_proj_w, 'dt_proj_b': dt_proj_b, 'A_log': A_log, 'D': D}
    _L0_xattn_all = _L0_xattn_setup()
    _L0_xattn_in = {k: v for k, v in _L0_xattn_all.items() if k in ('in_proj_w', 'conv_w', 'conv_b', 'x_proj_w', 'dt_proj_w', 'dt_proj_b', 'A_log', 'D')}
    del _L0_xattn_all

    def _L0_ffn_setup():
        import jax, jax.numpy as jnp
        import numpy as np
        B, S, H = (4, 256, 256)
        E, I, IS = (16, 176, 704)
        TOP_K = 4
        NORM_TOPK_PROB = False

        def _routing_weights(x, router_w):
            logits = x @ router_w.T
            probs = jax.nn.softmax(logits.astype(jnp.float32), axis=-1)
            vals, idx = jax.lax.top_k(probs, TOP_K)
            if NORM_TOPK_PROB:
                vals = vals / jnp.sum(vals, axis=-1, keepdims=True)
            T = x.shape[0]
            w_dense = jnp.zeros((T, probs.shape[-1]), probs.dtype)
            w_dense = w_dense.at[jnp.arange(T)[:, None], idx].set(vals)
            return w_dense.astype(x.dtype)

        def _moe_experts(x, gate_w, up_w, down_w, w_dense):

            def body(acc, ew):
                gw, uw, dw, w = ew
                h = jax.nn.silu(x @ gw.T) * (x @ uw.T)
                return (acc + w[:, None] * (h @ dw.T), None)
            acc, _ = jax.lax.scan(body, jnp.zeros_like(x), (gate_w, up_w, down_w, w_dense.T))
            return acc
        key = jax.random.key(seed)
        ks = jax.random.split(key, 9)
        s = 0.02
        return {'hidden_states': jax.random.normal(ks[0], (B, S, H), jnp.float32), 'router_w': jax.random.normal(ks[1], (E, H), jnp.float32) * s, 'gate_w': jax.random.normal(ks[2], (E, I, H), jnp.float32) * s, 'up_w': jax.random.normal(ks[3], (E, I, H), jnp.float32) * s, 'down_w': jax.random.normal(ks[4], (E, H, I), jnp.float32) * s, 'shared_gate_w': jax.random.normal(ks[5], (IS, H), jnp.float32) * s, 'shared_up_w': jax.random.normal(ks[6], (IS, H), jnp.float32) * s, 'shared_down_w': jax.random.normal(ks[7], (H, IS), jnp.float32) * s, 'se_gate_w': jax.random.normal(ks[8], (1, H), jnp.float32) * s}
    _L0_ffn_all = _L0_ffn_setup()
    _L0_ffn_in = {k: v for k, v in _L0_ffn_all.items() if k in ('router_w', 'gate_w', 'up_w', 'down_w', 'shared_gate_w', 'shared_up_w', 'shared_down_w', 'se_gate_w')}
    del _L0_ffn_all
    return {'x': x, 'ctx_1024': ctx_1024, 'L0_attn_W_Q': _L0_attn_in['W_Q'], 'L0_attn_W_K': _L0_attn_in['W_K'], 'L0_attn_W_V': _L0_attn_in['W_V'], 'L0_attn_W_O': _L0_attn_in['W_O'], 'L0_xattn_in_proj_w': _L0_xattn_in['in_proj_w'], 'L0_xattn_conv_w': _L0_xattn_in['conv_w'], 'L0_xattn_conv_b': _L0_xattn_in['conv_b'], 'L0_xattn_x_proj_w': _L0_xattn_in['x_proj_w'], 'L0_xattn_dt_proj_w': _L0_xattn_in['dt_proj_w'], 'L0_xattn_dt_proj_b': _L0_xattn_in['dt_proj_b'], 'L0_xattn_A_log': _L0_xattn_in['A_log'], 'L0_xattn_D': _L0_xattn_in['D'], 'L0_ffn_router_w': _L0_ffn_in['router_w'], 'L0_ffn_gate_w': _L0_ffn_in['gate_w'], 'L0_ffn_up_w': _L0_ffn_in['up_w'], 'L0_ffn_down_w': _L0_ffn_in['down_w'], 'L0_ffn_shared_gate_w': _L0_ffn_in['shared_gate_w'], 'L0_ffn_shared_up_w': _L0_ffn_in['shared_up_w'], 'L0_ffn_shared_down_w': _L0_ffn_in['shared_down_w'], 'L0_ffn_se_gate_w': _L0_ffn_in['se_gate_w']}

def reference(x, ctx_1024, L0_attn_W_Q, L0_attn_W_K, L0_attn_W_V, L0_attn_W_O, L0_xattn_in_proj_w, L0_xattn_conv_w, L0_xattn_conv_b, L0_xattn_x_proj_w, L0_xattn_dt_proj_w, L0_xattn_dt_proj_b, L0_xattn_A_log, L0_xattn_D, L0_ffn_router_w, L0_ffn_gate_w, L0_ffn_up_w, L0_ffn_down_w, L0_ffn_shared_gate_w, L0_ffn_shared_up_w, L0_ffn_shared_down_w, L0_ffn_se_gate_w):
    import jax
    import jax.numpy as jnp

    def _L0_attn_ref(x, W_Q, W_K, W_V, W_O):
        import jax, jax.numpy as jnp
        import numpy as np
        import math
        D_MODEL = 256
        N_HEADS = 16
        D_HEAD = 128
        BATCH = 2
        SEQ = 256
        d_head = W_Q.shape[1]
        seq_len = x.shape[1]
        scale = 1.0 / math.sqrt(d_head)
        q = jnp.einsum('bsd,hed->bhse', x, W_Q)
        k = jnp.einsum('bsd,hed->bhse', x, W_K)
        v = jnp.einsum('bsd,hed->bhse', x, W_V)
        scores = jnp.einsum('bhse,bhme->bhsm', q, k) * scale
        causal = jnp.triu(jnp.ones((seq_len, seq_len), dtype=bool), k=1)
        scores = jnp.where(causal, jnp.float32(-1000000000.0), scores)
        pattern = jax.nn.softmax(scores, axis=-1)
        z = jnp.einsum('bhsm,bhme->bhse', pattern, v)
        out = jnp.einsum('bhse,hde->bsd', z, W_O)
        return out

    def _L0_xattn_ref(hidden_states, z, in_proj_w, conv_w, conv_b, x_proj_w, dt_proj_w, dt_proj_b, A_log, D):
        import jax, jax.numpy as jnp
        import numpy as np
        B_, L_, D_MODEL = (4, 256, 128)
        D_STATE, D_CONV, EXPAND = (16, 4, 2)
        D_INNER = EXPAND * D_MODEL
        DT_RANK = (D_MODEL + 15) // 16

        def silu(x):
            return x * jax.nn.sigmoid(x)
        Bsz, L, _ = hidden_states.shape
        d_inner, _, d_conv = conv_w.shape
        dt_rank = dt_proj_w.shape[1]
        d_state = A_log.shape[1]
        x = jnp.einsum('bld,ed->bel', hidden_states, in_proj_w)
        xc = jax.lax.conv_general_dilated(x, conv_w, window_strides=(1,), padding=[(d_conv - 1, 0)], feature_group_count=d_inner, dimension_numbers=('NCH', 'OIH', 'NCH'))
        x = silu(xc + conv_b[None, :, None])
        x_dbl = jnp.einsum('bdl,ed->bel', x, x_proj_w)
        dt_low, Bm, Cm = jnp.split(x_dbl, [dt_rank, dt_rank + d_state], axis=1)
        dt = jnp.einsum('brl,dr->bdl', dt_low, dt_proj_w)
        dt = jax.nn.softplus(dt + dt_proj_b[None, :, None])
        A = -jnp.exp(A_log)
        dt_t = jnp.moveaxis(dt, -1, 0)
        B_t = jnp.moveaxis(Bm, -1, 0)
        C_t = jnp.moveaxis(Cm, -1, 0)
        u_t = jnp.moveaxis(x, -1, 0)

        def step(state, inp):
            d, b, c, u = inp
            dA = jnp.exp(d[..., None] * A)
            state = state * dA + (d * u)[..., None] * b[:, None, :]
            y = jnp.einsum('bdn,bn->bd', state, c)
            return (state, y)
        state0 = jnp.zeros((Bsz, d_inner, d_state), x.dtype)
        _, ys = jax.lax.scan(step, state0, (dt_t, B_t, C_t, u_t))
        y = jnp.moveaxis(ys, 0, 2)
        y = y + D[None, :, None] * x
        y = y * silu(z)
        return jnp.swapaxes(y, 1, 2)

    def _L0_ffn_ref(hidden_states, router_w, gate_w, up_w, down_w, shared_gate_w, shared_up_w, shared_down_w, se_gate_w):
        import jax, jax.numpy as jnp
        import numpy as np
        B, S, H = (4, 256, 256)
        E, I, IS = (16, 176, 704)
        TOP_K = 4
        NORM_TOPK_PROB = False

        def _routing_weights(x, router_w):
            logits = x @ router_w.T
            probs = jax.nn.softmax(logits.astype(jnp.float32), axis=-1)
            vals, idx = jax.lax.top_k(probs, TOP_K)
            if NORM_TOPK_PROB:
                vals = vals / jnp.sum(vals, axis=-1, keepdims=True)
            T = x.shape[0]
            w_dense = jnp.zeros((T, probs.shape[-1]), probs.dtype)
            w_dense = w_dense.at[jnp.arange(T)[:, None], idx].set(vals)
            return w_dense.astype(x.dtype)

        def _moe_experts(x, gate_w, up_w, down_w, w_dense):

            def body(acc, ew):
                gw, uw, dw, w = ew
                h = jax.nn.silu(x @ gw.T) * (x @ uw.T)
                return (acc + w[:, None] * (h @ dw.T), None)
            acc, _ = jax.lax.scan(body, jnp.zeros_like(x), (gate_w, up_w, down_w, w_dense.T))
            return acc
        b, s, h = hidden_states.shape
        x = hidden_states.reshape(-1, h)
        w_dense = _routing_weights(x, router_w)
        moe_out = _moe_experts(x, gate_w, up_w, down_w, w_dense)
        shared = jax.nn.silu(x @ shared_gate_w.T) * (x @ shared_up_w.T) @ shared_down_w.T
        shared = jax.nn.sigmoid(x @ se_gate_w.T) * shared
        return (moe_out + shared).reshape(b, s, h)
    x = _layernorm(x + _L0_attn_ref(x, L0_attn_W_Q, L0_attn_W_K, L0_attn_W_V, L0_attn_W_O), axis=-1)
    x = _layernorm(x + _L0_xattn_ref(ctx_1024, x, L0_xattn_in_proj_w, L0_xattn_conv_w, L0_xattn_conv_b, L0_xattn_x_proj_w, L0_xattn_dt_proj_w, L0_xattn_dt_proj_b, L0_xattn_A_log, L0_xattn_D), axis=-1)
    x = _layernorm(x + _L0_ffn_ref(x, L0_ffn_router_w, L0_ffn_gate_w, L0_ffn_up_w, L0_ffn_down_w, L0_ffn_shared_gate_w, L0_ffn_shared_up_w, L0_ffn_shared_down_w, L0_ffn_se_gate_w), axis=-1)
    return x

_drawn_inputs = setup_inputs


def setup_inputs(seed=0):
    import zlib

    import numpy as np

    out = dict(_drawn_inputs(seed))
    spreads = {'L0_xattn_D': (1.0, 0.6)}
    factors = {'ctx_1024': 4.288,
     'L0_attn_W_Q': 8.0,
     'L0_attn_W_K': 8.0,
     'L0_xattn_in_proj_w': 4.308,
     'L0_xattn_conv_w': 4.494,
     'L0_xattn_conv_b': 8.0,
     'L0_xattn_x_proj_w': 8.0,
     'L0_xattn_dt_proj_w': 8.0,
     'L0_xattn_dt_proj_b': 8.0,
     'L0_xattn_A_log': 8.0,
     'L0_ffn_router_w': 8.0,
     'L0_ffn_gate_w': 8.0,
     'L0_ffn_up_w': 8.0,
     'L0_ffn_down_w': 8.0,
     'L0_ffn_shared_gate_w': 3.997,
     'L0_ffn_shared_up_w': 3.978,
     'L0_ffn_shared_down_w': 3.967,
     'L0_ffn_se_gate_w': 8.0}
    for name, (base, spread) in spreads.items():
        noise = np.random.default_rng([zlib.crc32(name.encode()), seed]).standard_normal(out[name].shape)
        drawn = base * np.exp(spread * noise) if base else spread * noise
        out[name] = jnp.asarray(drawn.astype(out[name].dtype))
    for name, factor in factors.items():
        out[name] = (out[name] * factor).astype(out[name].dtype)
    return out
```

```python
from contextlib import ExitStack

import concourse.bass as bass
from concourse import mybir

F32 = mybir.dt.float32
F32R = mybir.dt.float32r
BF16 = mybir.dt.bfloat16
ALU = mybir.AluOpType
ACT = mybir.ActivationFunctionType
AX = mybir.AxisListType

P = 128
BATCH, SEQ, D = 4, 256, 256
TOK = BATCH * SEQ
NT = TOK // P
DK = D // P
CH = 512
NC = TOK // CH
HEADS, HD = 16, 128
PAIRS = HEADS // 2
QSCALE = -1.0 / float(HD) ** 0.5
MASKED = 1.0e30
CTX = 128
DI = 256
DM = DI // P
STATES, TAPS, RANK = 16, 4, 8
XDBL = RANK + 2 * STATES
EXPERTS, EI, SI = 16, 176, 704
GROUPS = (EXPERTS * EI + SI) // EI
HID = GROUPS * EI
HT = -(-HID // P)
TOPK = 4
NR = EXPERTS + 2
NSEL = 96
EPS = 1e-5
ATANH = (2.000000007681758, 0.6666632164140144, 0.40024595229818943, 0.2796515775679465, 0.28157778313522575)

PRE_UNITS = 22
PRE_ATTN = 12
PAIR_UNITS, HALF_UNITS = 32, 14
Q_U, P_U, K_U, Z_U, S_U, V_U = 0, 2, 6, 8, 10, 28
PRE_HI, PAIR_HI, HALF_HI = 8, 24, 10


def decoder_layer(nc, ins, out):
    with ExitStack() as ctx:
        def sb(name, shape, dt=F32):
            return ctx.enter_context(nc.sbuf_tensor(name, shape, dt))

        def sem(name):
            return ctx.enter_context(nc.semaphore(name))

        xT_hi = sb("xT_hi", [P, DK, TOK], F32R)
        xT_lo = sb("xT_lo", [P, DK, TOK], F32R)
        x_res = sb("x_res", [P, NT, D])
        stage = sb("stage", [P, DK, TOK])
        wqk_raw = sb("wqk_raw", [P, 4 * P])
        wv_raw = sb("wv_raw", [P, 4 * P])
        wo_raw = sb("wo_raw", [P, D])
        wqk_hi = [sb(f"wqk_hi{i}", [P, 4 * P], F32R) for i in range(2)]
        wqk_lo = [sb(f"wqk_lo{i}", [P, 4 * P], F32R) for i in range(2)]
        wv_hi = sb("wv_hi", [P, 4 * P], F32R)
        wv_lo = sb("wv_lo", [P, 4 * P], F32R)
        wo_hi = [sb(f"wo_hi{i}", [P, D], F32R) for i in range(2)]
        wo_lo = [sb(f"wo_lo{i}", [P, D], F32R) for i in range(2)]
        q_hi, q_lo = sb("q_hi", [P, TOK], F32R), sb("q_lo", [P, TOK], F32R)
        k_hi, k_lo = sb("k_hi", [P, TOK], F32R), sb("k_lo", [P, TOK], F32R)
        z_hi, z_lo = sb("z_hi", [P, TOK], F32R), sb("z_lo", [P, TOK], F32R)
        v_hi = sb("v_hi", [P, NT, 2 * HD], F32R)
        v_lo = sb("v_lo", [P, NT, 2 * HD], F32R)
        prob = sb("prob", [P, BATCH, 3 * P])
        pT_hi = sb("pT_hi", [P, BATCH, 3 * P], F32R)
        pT_lo = sb("pT_lo", [P, BATCH, 3 * P], F32R)
        smin = sb("smin", [P, BATCH, 2])
        ssum = sb("ssum", [P, BATCH, 2])
        sinv = sb("sinv", [P, BATCH, 2])
        mask = sb("mask", [P, 2 * P])
        ident = sb("ident", [P, P])
        ident_b = sb("ident_b", [P, P], BF16)
        inw = sb("inw", [P, DI])
        xw = sb("xw", [P, DM, XDBL])
        dtw = sb("dtw", [RANK, DI])
        chan = sb("chan", [P, DM, TAPS + 3 + STATES])
        bc = sb("bc", [P, 4 * TOK])
        b_all = bc[:, 0:2 * TOK].rearrange("p (i t) -> p i t", t=TOK)
        c_all = bc[:, 2 * TOK:].rearrange("p (i t) -> p i t", t=TOK)
        n_pad = DM * BATCH * (SEQ + TAPS - 1)
        padded = bc[:, 0:n_pad].rearrange("p (m b s) -> p m b s", m=DM, b=BATCH)
        ctxT = bc[:, n_pad:n_pad + TOK]
        conv = stage
        u = sb("u", [P, DM, TOK])
        xdbl = sb("xdbl", [XDBL, TOK])
        dt = sb("dt", [P, DM, TOK])
        dtu = sb("dtu", [P, DM, TOK])
        y = sb("y", [P, DM, TOK])
        a_neg = sb("a_neg", [P, DM, STATES])
        da = sb("da", [P, DM, BATCH, SEQ])
        dbu = sb("dbu", [P, DM, TOK])
        state = sb("state", [P, DM, TOK])
        stats = sb("stats", [P, NT, 6])
        mv = sb("mv", [P, NT, 2])
        veps = sb("veps", [P, NT])
        rstd = sb("rstd", [P, NT])
        mhalf = sb("mhalf", [P, NT])
        rw_raw = sb("rw_raw", [P, DK, NR])
        rw_hi, rw_lo = sb("rw_hi", [P, DK, NR], F32R), sb("rw_lo", [P, DK, NR], F32R)
        lmax = sb("lmax", [P, NT])
        lsub = sb("lsub", [P, NT, EXPERTS])
        lsum = sb("lsum", [P, NT])
        linv = sb("linv", [P, NT])
        probs = sb("probs", [P, NT, EXPERTS + 8])
        picked = sb("picked", [P, NT, EXPERTS + 8])
        top = sb("top", [P, NT, 8])
        gate = sb("gate", [P, NT])
        wr = sb("wr", [P, NT, GROUPS])
        wpart = sb("wpart", [P, NT, NSEL], BF16)
        wT = sb("wT", [NSEL, TOK], BF16)
        sel = sb("sel", [NSEL, HT * P], BF16)
        h_hi, h_lo = [q_hi, k_hi], [q_lo, k_lo]
        f_raw = [prob[:, 2 * i:2 * i + 2, :].rearrange("p b s -> p (b s)") for i in range(2)]
        gu_hi, gu_lo = wqk_hi, wqk_lo
        dn_hi, dn_lo = wo_hi, wo_lo
        silu_g, hid = da[:, 0].rearrange("p b s -> p (b s)"), dbu[:, 0, :]
        hidw = state[:, 0, :]
        pre = stage[:, :, :].rearrange("p a t -> p (a t)").rearrange("p (t d) -> p t d", d=D)
        soft_v, soft_e, soft_s, soft_2 = da, dbu, state, conv

        acc = ctx.enter_context(nc.psum_tensor("acc", [P, NT * D], F32))
        ring = ctx.enter_context(nc.psum_tensor("ring", [P, 4, CH], F32))
        acc_t = acc[:, :].rearrange("p (t d) -> p t d", d=D)

        def bank(g):
            return ring[:, g % 4, :]

        bc_dram = nc.dram_tensor("bc_dram", [2 * STATES, TOK], F32, kind="Internal").ap()

        filled = sem("filled")
        pre_read = sem("pre_read")
        bank_read = sem("bank_read")
        hi_done = sem("hi_done")
        exp_done = sem("exp_done")
        inv_done = sem("inv_done")
        probs_ready = sem("probs_ready")
        ld_x, ld_xres, ld_ctx = sem("ld_x"), sem("ld_xres"), sem("ld_ctx")
        ld_chan, ld_xw, ld_rw = sem("ld_chan"), sem("ld_xw"), sem("ld_rw")
        ld_wqk, ld_wv, ld_wo = sem("ld_wqk"), sem("ld_wv"), sem("ld_wo")
        x_hi_s, x_lo_s = sem("x_hi_s"), sem("x_lo_s")
        wqk_h, wv_h, wo_h = sem("wqk_h"), sem("wv_h"), sem("wo_h")
        wqk_s, wv_s, wo_s = sem("wqk_s"), sem("wv_s"), sem("wo_s")
        consts = sem("consts")
        pad_zero, acc_zero = sem("pad_zero"), sem("acc_zero")
        convd, u_done, a_exp, a_done = sem("convd"), sem("u_done"), sem("a_exp"), sem("a_done")
        bc_stored, soft, soft_x, dt_done, dtu_done = (sem("bc_stored"), sem("soft"), sem("soft_x"),
                                                      sem("dt_done"), sem("dtu_done"))
        bc_load = [sem("bc_load0"), sem("bc_load1")]
        da_done, dbu_done = sem("da_done"), sem("dbu_done")
        scanned, cmul, y_added = sem("scanned"), sem("cmul"), sem("y_added")
        out_proj = sem("out_proj")
        ln_in, ln_stat, ln_mv, ln_eps, ln_rstd, ln_out = (sem("ln_in"), sem("ln_stat"), sem("ln_mv"),
                                                          sem("ln_eps"), sem("ln_rstd"), sem("ln_out"))
        silu_z, gated, turned = sem("silu_z"), sem("gated"), sem("turned")
        x2_turned, x2_hi, x2_lo = sem("x2_turned"), sem("x2_hi"), sem("x2_lo")
        rw_h, rw_s, logit = sem("rw_h"), sem("rw_s"), sem("logit")
        route, route_e = sem("route"), sem("route_e")
        wt_turned, wt_done = sem("wt_turned"), sem("wt_done")
        ld_f = [sem("ld_f0"), sem("ld_f1")]
        gu_h, gu_s, dn_h, dn_s = sem("gu_h"), sem("gu_s"), sem("dn_h"), sem("dn_s")
        gate_f, up_f, wb_f = sem("gate_f"), sem("up_f"), sem("wb_f")
        silu_d, hid_d, hidw_d = sem("silu_d"), sem("hid_d"), sem("hidw_d")
        hhi_d, hlo_d = sem("hhi_d"), sem("hlo_d")
        down_d = sem("down_d")
        stored = sem("stored")

        block = ctx.enter_context(nc.Block())

        @block.sync
        def _(sp):
            sp.dma_start(ctxT[:, :], ins["ctxT"]).then_inc(ld_ctx, 16)
            sp.dma_start(inw[:, :], ins["inw"]).then_inc(ld_ctx, 16)
            sp.dma_start(chan[:, :, :], ins["chan"]).then_inc(ld_chan, 16)
            sp.dma_start(stage[:, :, :], ins["xT"]).then_inc(ld_x, 16)
            sp.dma_start(wqk_raw[:, :], ins["wqk"][0, :, :]).then_inc(ld_wqk, 16)
            sp.dma_start(wv_raw[:, :], ins["wv"][0, :, :]).then_inc(ld_wv, 16)
            sp.dma_start(xw[:, :, :], ins["xw"]).then_inc(ld_xw, 16)
            sp.dma_start(dtw[:, :], ins["dtw"]).then_inc(ld_xw, 16)
            sp.dma_start(wo_raw[:, :], ins["wo"][0, :, :]).then_inc(ld_wo, 16)
            sp.dma_start(x_res[:, :, :], ins["x"]).then_inc(ld_xres, 16)
            sp.dma_start(rw_raw[:, :, :], ins["rw"]).then_inc(ld_rw, 16)
            sp.wait_ge(wqk_s, 1)
            sp.dma_start(wqk_raw[:, :], ins["wqk"][1, :, :]).then_inc(ld_wqk, 16)
            sp.wait_ge(pre_read, 6)
            sp.dma_start(bc_dram, xdbl[RANK:XDBL, :]).then_inc(bc_stored, 16)
            sp.wait_ge(bc_stored, 16)

            def load_bc(n, i):
                sp.dma_start(b_all[:, i, :], bc_dram[bass.ds(n, 1), :].to_broadcast([P, TOK])).then_inc(bc_load[i], 16)
                sp.dma_start(c_all[:, i, :], bc_dram[bass.ds(n + STATES, 1), :].to_broadcast([P, TOK]))\
                  .then_inc(bc_load[i], 16)

            for i in range(2):
                load_bc(i, i)

            def pair_loads(p, last):
                for i in range(2):
                    a = 2 * p + i
                    if not last:
                        sp.wait_ge(wqk_s, a + 2)
                        sp.dma_start(wqk_raw[:, :], ins["wqk"][bass.ds(a + 2, 1), :, :].rearrange("h p n -> (h p) n"))\
                          .then_inc(ld_wqk, 16)
                    if not (last and i == 1):
                        sp.wait_ge(wo_s, a + 1)
                        sp.dma_start(wo_raw[:, :], ins["wo"][bass.ds(a + 1, 1), :, :].rearrange("h p n -> (h p) n"))\
                          .then_inc(ld_wo, 16)
                    if i == 0 and not last:
                        sp.wait_ge(wv_s, p + 1)
                        sp.dma_start(wv_raw[:, :], ins["wv"][bass.ds(p + 1, 1), :, :].rearrange("h p n -> (h p) n"))\
                          .then_inc(ld_wv, 16)
                    if not last:
                        sp.wait_ge(dbu_done, 4 * p + 2 * i + 2)
                        sp.wait_ge(cmul, 4 * p + 2 * i + 2)
                        load_bc(2 * p + 2 + i, i)

            with sp.Fori(0, PAIRS - 1) as p:
                pair_loads(p, False)
            pair_loads(PAIRS - 1, True)
            sp.wait_ge(filled, PRE_UNITS + PAIR_UNITS * (PAIRS - 1) + HALF_UNITS + BATCH)
            for i in range(2):
                sp.dma_start(f_raw[i], ins["wf"][i, :, :]).then_inc(ld_f[i], 16)

            def mlp_load(j, i):
                sp.wait_ge(dn_s, j - 1)
                sp.dma_start(f_raw[i], ins["wf"][bass.ds(j, 1), :, :].rearrange("h p n -> (h p) n"))\
                  .then_inc(ld_f[i], 16)

            with sp.Fori(0, HT // 2 - 1) as r:
                for i in range(2):
                    mlp_load(2 * r + 2 + i, i)
            for t in range(NT):
                sp.wait_ge(ln_out, 2 * NT + t + 1)
                sp.dma_start(out[t * P:(t + 1) * P, :], pre[:, t, :]).then_inc(stored, 16)
            sp.wait_ge(stored, 16 * NT)

        @block.gpsimd
        def _(pool):
            pool.memset(ident[:, :], 0.0).then_inc(consts, 1)
            pool.memset(mask[:, :], 0.0).then_inc(consts, 1)
            pool.memset(padded[:, :, :, 0:TAPS - 1], 0.0).then_inc(pad_zero, 1)
            pool.wait_ge(consts, 2)
            pool.affine_select(out=ident[:, :], in_=ident[:, :], compare_op=ALU.not_equal, fill=1.0,
                               base=0, pattern=[[-1, P]], channel_multiplier=1).then_inc(consts, 1)
            pool.affine_select(out=mask[:, P:2 * P], in_=mask[:, P:2 * P], compare_op=ALU.is_ge,
                               fill=MASKED, base=0, pattern=[[-1, P]], channel_multiplier=1).then_inc(consts, 1)
            pool.wait_ge(consts, 4)
            pool.tensor_scalar(ident_b[:, :], ident[:, :], 1.0, 0.0, ALU.mult, ALU.add).then_inc(consts, 1)

            def split(raw, hi, lo, hi_sem, lo_sem, n):
                pool.nop(nofuse=True)
                pool.tensor_scalar(hi, raw, 1.0, 0.0, ALU.mult, ALU.add).then_inc(hi_sem, 1)
                pool.wait_ge(hi_sem, n)
                pool.tensor_tensor(lo, raw, hi.bitcast(F32), ALU.subtract).then_inc(lo_sem, 1)

            pool.wait_ge(ld_wqk, 16)
            split(wqk_raw[:, :], wqk_hi[0][:, :], wqk_lo[0][:, :], wqk_h, wqk_s, 1)
            pool.wait_ge(ld_wv, 16)
            split(wv_raw[:, :], wv_hi[:, :], wv_lo[:, :], wv_h, wv_s, 1)
            pool.wait_ge(ld_wqk, 32)
            split(wqk_raw[:, :], wqk_hi[1][:, :], wqk_lo[1][:, :], wqk_h, wqk_s, 2)
            pool.wait_ge(ld_wo, 16)
            split(wo_raw[:, :], wo_hi[0][:, :], wo_lo[0][:, :], wo_h, wo_s, 1)
            pool.wait_ge(ld_rw, 16)
            split(rw_raw[:, :, :], rw_hi[:, :, :], rw_lo[:, :, :], rw_h, rw_s, 1)
            pool.memset(mhalf[:, :], -0.5).then_inc(consts, 1)
            pool.memset(probs[:, :, EXPERTS:EXPERTS + 8], -1.0).then_inc(consts, 1)
            pool.memset(wpart[:, :, :], 0.0).then_inc(consts, 1)
            pool.memset(sel[:, :], 1.0).then_inc(consts, 1)
            for n, r in enumerate(range(0, NSEL, 32)):
                pool.wait_ge(consts, 9 + n)
                pool.affine_select(out=sel[r:r + 32, :], in_=sel[r:r + 32, :], compare_op=ALU.is_ge, fill=0.0,
                                   base=0, pattern=[[1, HT * P]], channel_multiplier=-EI).then_inc(consts, 1)
            for n, r in enumerate(range(0, NSEL, 32)):
                pool.wait_ge(consts, 12 + n)
                pool.affine_select(out=sel[r:r + 32, :], in_=sel[r:r + 32, :], compare_op=ALU.is_ge, fill=0.0,
                                   base=EI - 1, pattern=[[-1, HT * P]], channel_multiplier=EI).then_inc(consts, 1)
            pool.wait_ge(consts, 15)
            for m in range(DM):
                pool.wait_ge(u_done, m + 1)
                pool.tensor_scalar(y[:, m, :], u[:, m, :], chan[:, m, TAPS + 2:TAPS + 3], 1.0,
                                   ALU.mult, ALU.mult).then_inc(y_added, 1)
            for m in range(DM):
                pool.wait_ge(dt_done, m + 1)
                pool.tensor_tensor(dtu[:, m, :], dt[:, m, :], u[:, m, :], ALU.mult).then_inc(dtu_done, 1)
            pool.wait_ge(dtu_done, 2)

            def make_dbu(p, i, m):
                k = 4 * p + 2 * i + m
                pool.wait_ge(bc_load[i], 32 * p + 32)
                pool.wait_ge(scanned, k + 1)
                pool.tensor_tensor(dbu[:, m, :], dtu[:, m, :], b_all[:, i, :], ALU.mult).then_inc(dbu_done, 1)

            def add_y(p, i, m):
                k = 4 * p + 2 * i + m
                pool.wait_ge(cmul, k + 1)
                pool.wait_ge(y_added, k + 1)
                pool.tensor_tensor(y[:, m, :], y[:, m, :], state[:, m, :], ALU.add).then_inc(y_added, 1)

            def pair_pool(p, last):
                for i in range(2):
                    a = 2 * p + i
                    make_dbu(p, i, 0)
                    if not (last and i == 1):
                        pool.wait_ge(filled, PRE_UNITS + PAIR_UNITS * p + HALF_UNITS * i + 1)
                        pool.wait_ge(ld_wo, 16 * (a + 2))
                        split(wo_raw[:, :], wo_hi[1 - i][:, :], wo_lo[1 - i][:, :], wo_h, wo_s, a + 2)
                    make_dbu(p, i, 1)
                    if not last:
                        pool.wait_ge(ld_wqk, 16 * (a + 3))
                        split(wqk_raw[:, :], wqk_hi[i][:, :], wqk_lo[i][:, :], wqk_h, wqk_s, a + 3)
                    add_y(p, i, 0)
                    if i == 0 and not last:
                        pool.wait_ge(ld_wv, 16 * (p + 2))
                        split(wv_raw[:, :], wv_hi[:, :], wv_lo[:, :], wv_h, wv_s, p + 2)
                    add_y(p, i, 1)

            with pool.Fori(0, PAIRS - 1) as p:
                pair_pool(p, False)
            pair_pool(PAIRS - 1, True)

            def norm_scale(n):
                pool.wait_ge(ln_mv, NT * (n + 1))
                if n:
                    pool.wait_ge(ln_out, NT * n)
                pool.tensor_scalar(veps[:, :], mv[:, :, 1], 1.0, EPS, ALU.mult, ALU.add).then_inc(ln_eps, 1)
                pool.wait_ge(ln_eps, n + 1)
                pool.tensor_tensor(rstd[:, :], veps[:, :], mhalf[:, :], ALU.pow).then_inc(ln_rstd, 1)

            def split_gate_up(j, i):
                pool.wait_ge(ld_f[i], 8 * j + 16 - 8 * i)
                split(f_raw[i][:, 0:4 * P], gu_hi[i][:, :], gu_lo[i][:, :], gu_h, gu_s, j + 1)

            def split_down(j, i):
                split(f_raw[i][:, 4 * P:], dn_hi[i][:, :], dn_lo[i][:, :], dn_h, dn_s, j + 1)

            def lo_h(j, i):
                for c in range(NC):
                    s = slice(c * CH, (c + 1) * CH)
                    pool.wait_ge(hhi_d, NC * j + c + 1)
                    pool.tensor_tensor(h_lo[i][:, s], hidw[:, s], h_hi[i][:, s].bitcast(F32), ALU.subtract)\
                        .then_inc(hlo_d, 1)

            norm_scale(0)
            for j in range(2):
                split_gate_up(j, j)
                split_down(j, j)
            norm_scale(1)
            lo_h(0, 0)
            with pool.Fori(0, HT // 2 - 1) as r:
                for i in range(2):
                    j = 2 * r + i
                    pool.wait_ge(up_f, NC * (j + 1))
                    split_gate_up(j + 2, i)
                    lo_h(j + 1, 1 - i)
                    pool.wait_ge(down_d, j + 1)
                    split_down(j + 2, i)
            lo_h(HT - 1, 1)
            norm_scale(2)

        @block.scalar
        def _(act):
            for m in range(DM):
                for c in range(NC):
                    g = NC * m + c
                    act.wait_ge(filled, g + 1)
                    act.activation(padded[:, m, 2 * c:2 * c + 2, TAPS - 1:],
                                   bank(g).rearrange("p (b s) -> p b s", s=SEQ), ACT.Copy).then_inc(pre_read, 1)
            act.wait_ge(ld_x, 16)
            for k in range(DK):
                act.activation(xT_hi[:, k, :], stage[:, k, :], ACT.Copy).then_inc(x_hi_s, 1)

            def hi(dst, g, n_units, scale=1.0, cols=CH):
                act.wait_ge(filled, n_units)
                act.activation(dst, bank(g)[:, 0:cols], ACT.Copy, scale=scale).then_inc(hi_done, 1)

            def hi_qk(dst, g, n, c, scale):
                hi(dst[:, c * CH:(c + 1) * CH], g, n + 1, scale)

            for c in range(NC):
                hi_qk(q_hi, 4 + c, 4 + c, c, QSCALE)
            for m in range(DM):
                act.wait_ge(convd, m + 1)
                act.activation(u[:, m, :], conv[:, m, :], ACT.Silu, bias=chan[:, m, TAPS:TAPS + 1]).then_inc(u_done, 1)
            for c in range(NC):
                hi_qk(k_hi, 6 + c, 6 + c, c, 1.0)
            for t in range(4):
                hi(v_hi[:, 2 * t:2 * t + 2, :].rearrange("p t e -> p (t e)"), 8 + t, 9 + t)
            for c in range(NC):
                act.wait_ge(filled, 13 + c)
                act.activation(xdbl[:, c * CH:(c + 1) * CH], bank(12 + c)[0:XDBL, :], ACT.Copy).then_inc(pre_read, 1)
            act.activation(a_neg[:, :, :], chan[:, :, TAPS + 3:], ACT.Exp).then_inc(a_exp, 1)
            for m in range(DM):
                for c in range(NC):
                    g = 14 + NC * m + c
                    act.wait_ge(filled, g + 1)
                    act.activation(soft_v[:, m, 2 * c:2 * c + 2, :].rearrange("p b s -> p (b s)"), bank(g),
                                   ACT.Identity, bias=chan[:, m, TAPS + 1:TAPS + 2]).then_inc(pre_read, 1)
                act.wait_ge(pre_read, 8 + 2 * m)
                act.activation(soft_e[:, m, :], soft_v[:, m].rearrange("p b s -> p (b s)"), ACT.Abs).then_inc(soft_x, 1)
                act.wait_ge(soft_x, 2 * m + 1)
                act.activation(soft_e[:, m, :], soft_e[:, m, :], ACT.Exp, scale=-1.0).then_inc(soft_x, 1)

            def exps(n):
                for b in range(BATCH):
                    act.wait_ge(bank_read, n + b + 1)
                    act.activation(prob[:, b, 0:P], prob[:, b, 0:P], ACT.Exp, bias=smin[:, b, 0:1], scale=-1.0,
                                   accum_out=ssum[:, b, 0:1]).then_inc(exp_done, 1)
                    act.activation(prob[:, b, P:], prob[:, b, P:], ACT.Exp, bias=smin[:, b, 1:2], scale=-1.0,
                                   accum_out=ssum[:, b, 1:2]).then_inc(exp_done, 1)

            def make_da(p, i, m):
                act.wait_ge(scanned, 4 * p + 2 * i + m + 1)
                act.activation(da[:, m, :, 1:], dt[:, m, :].rearrange("p (b s) -> p b s", s=SEQ)[:, :, 1:],
                               ACT.Exp, scale=a_neg[:, m, bass.ds(2 * p + i, 1)]).then_inc(da_done, 1)

            exps(8)
            act.wait_ge(a_done, 1)
            act.wait_ge(dt_done, 2)

            def pair_act(p, last):
                for i in range(2):
                    base = PRE_UNITS + PAIR_UNITS * p + HALF_UNITS * i
                    gb = PRE_UNITS + HALF_UNITS * i
                    nxt = not (last and i == 1)
                    if last and i == 1:
                        pt, z = P_U - 2, Z_U - 4
                    else:
                        pt, z = P_U, Z_U
                    if nxt:
                        for c in range(NC):
                            hi_qk(q_hi, gb + Q_U + c, base + Q_U + c, c, QSCALE)
                    make_da(p, i, 0)
                    for b in range(BATCH):
                        hi(pT_hi[:, b, :], gb + pt + b, base + pt + b + 1, cols=3 * P)
                    if nxt:
                        for c in range(NC):
                            hi_qk(k_hi, gb + K_U + c, base + K_U + c, c, 1.0)
                    make_da(p, i, 1)
                    for c in range(NC):
                        hi_qk(z_hi, gb + z + c, base + z + c, c, 1.0)
                    if nxt:
                        exps(PRE_ATTN + PAIR_UNITS * p + HALF_UNITS * i + S_U)
                if not last:
                    for t in range(4):
                        hi(v_hi[:, 2 * t:2 * t + 2, :].rearrange("p t e -> p (t e)"),
                           PRE_UNITS + V_U + t, PRE_UNITS + PAIR_UNITS * p + V_U + t + 1)

            with act.Fori(0, PAIRS - 1) as p:
                pair_act(p, False)
            pair_act(PAIRS - 1, True)

            for t in range(NT):
                act.wait_ge(ln_out, t + 1)
                act.activation(da[:, 0].rearrange("p b s -> p (b s)").rearrange("p (t d) -> p t d", d=D)[:, t, :]
                               if t < 4 else
                               da[:, 1].rearrange("p b s -> p (b s)").rearrange("p (t d) -> p t d", d=D)[:, t - 4, :],
                               x_res[:, t, :], ACT.Silu).then_inc(silu_z, 1)
            for n in range(NC * DK):
                act.wait_ge(x2_turned, n + 1)
                act.activation(xT_hi[:, n % DK, (n // DK) * CH:(n // DK + 1) * CH], bank(n), ACT.Copy)\
                   .then_inc(x2_hi, 1)
            act.wait_ge(route, 2)
            act.activation(probs[:, :, 0:EXPERTS], lsub[:, :, :], ACT.Exp).then_inc(route_e, 1)
            act.activation(gate[:, :], gate[:, :], ACT.Exp).then_inc(route_e, 1)
            act.wait_ge(wt_turned, 1)
            act.activation(wT[:, :], bank(1)[0:NSEL, :].bitcast(BF16), ACT.Copy).then_inc(wt_done, 1)

            def mlp_act(j, i, g0, first):
                for c in range(NC):
                    s = slice(c * CH, (c + 1) * CH)
                    act.wait_ge(gate_f, NC * j + c + 1)
                    if not first:
                        act.wait_ge(hid_d, NC * (j - 1) + c + 1)
                    act.activation(silu_g[:, s], bank(g0 + 3 * c), ACT.Silu).then_inc(silu_d, 1)
                for c in range(NC):
                    s = slice(c * CH, (c + 1) * CH)
                    act.wait_ge(hidw_d, NC * j + c + 1)
                    act.activation(h_hi[i][:, s], hidw[:, s], ACT.Copy).then_inc(hhi_d, 1)

            mlp_act(0, 0, 2, True)
            with act.Fori(0, HT // 2 - 1) as r:
                mlp_act(2 * r + 1, 1, 2 + 6, False)
                mlp_act(2 * r + 2, 0, 2, False)
            mlp_act(HT - 1, 1, 2 + 6, False)

        @block.vector
        def _(dve):
            dve.memset(acc[:, :], 0.0).then_inc(acc_zero, 1)
            dve.wait_ge(ld_x, 16)
            dve.wait_ge(ld_chan, 16)
            for k in range(DK):
                dve.wait_ge(x_hi_s, k + 1)
                dve.tensor_tensor(xT_lo[:, k, :], stage[:, k, :], xT_hi[:, k, :].bitcast(F32), ALU.subtract)\
                   .then_inc(x_lo_s, 1)

            def lo(dst, hi_part, g, n_hi, scale=None, cols=CH):
                dve.wait_ge(hi_done, n_hi)
                if scale is None:
                    dve.tensor_tensor(dst, bank(g)[:, 0:cols], hi_part.bitcast(F32), ALU.subtract).then_inc(bank_read, 1)
                else:
                    dve.scalar_tensor_tensor(out=dst, in0=bank(g)[:, 0:cols], scalar=scale, in1=hi_part.bitcast(F32),
                                             op0=ALU.mult, op1=ALU.subtract).then_inc(bank_read, 1)

            def lo_qk(dst, src, g, n, c, scale=None):
                s = slice(c * CH, (c + 1) * CH)
                lo(dst[:, s], src[:, s], g, n + 1, scale)

            def lo_v(t, g, n):
                lo(v_lo[:, 2 * t:2 * t + 2, :].rearrange("p t e -> p (t e)"),
                   v_hi[:, 2 * t:2 * t + 2, :].rearrange("p t e -> p (t e)"), g, n + 1)

            def conv_half(m, base):
                dve.wait_ge(pre_read, NC * (m + 1))
                dve.wait_ge(pad_zero, 1)
                dst = conv[:, m, :].rearrange("p (b s) -> p b s", s=SEQ)
                for k in range(TAPS):
                    src = padded[:, m, :, k:k + SEQ]
                    tap = chan[:, m, k:k + 1]
                    if k == 0:
                        op = dve.tensor_scalar(dst, src, tap, None, ALU.mult)
                    else:
                        dve.wait_ge(soft, base + k)
                        op = dve.scalar_tensor_tensor(out=dst, in0=src, scalar=tap, in1=dst, op0=ALU.mult, op1=ALU.add)
                    op.then_inc(convd if k == TAPS - 1 else soft, 1)

            dve.wait_ge(x_lo_s, DK)
            conv_half(0, 0)
            for c in range(NC):
                lo_qk(q_lo, q_hi, 4 + c, c, c, QSCALE)
            conv_half(1, TAPS - 1)
            for c in range(NC):
                lo_qk(k_lo, k_hi, 6 + c, 2 + c, c)
            for t in range(4):
                lo_v(t, 8 + t, 4 + t)
            dve.wait_ge(a_exp, 1)
            dve.tensor_scalar(a_neg[:, :, :], a_neg[:, :, :], -1.0, None, ALU.mult).then_inc(a_done, 1)

            soft0 = 2 * (TAPS - 1)
            for m in range(DM):
                dve.wait_ge(soft_x, 2 * m + 2)
                e, s, s2, w = soft_e[:, m, :], soft_s[:, m, :], soft_2[:, m, :], dt[:, m, :]
                steps = [
                    lambda: dve.tensor_scalar(w, e, 2.0, None, ALU.add),
                    lambda: dve.reciprocal(s, w),
                    lambda: dve.tensor_tensor(s, s, e, ALU.mult),
                    lambda: dve.tensor_tensor(s2, s, s, ALU.mult),
                    lambda: dve.tensor_scalar(w, s2, ATANH[4], ATANH[3], ALU.mult, ALU.add),
                    lambda: dve.tensor_tensor(w, w, s2, ALU.mult),
                    lambda: dve.scalar_tensor_tensor(out=w, in0=w, scalar=ATANH[2], in1=s2, op0=ALU.add, op1=ALU.mult),
                    lambda: dve.scalar_tensor_tensor(out=w, in0=w, scalar=ATANH[1], in1=s2, op0=ALU.add, op1=ALU.mult),
                    lambda: dve.scalar_tensor_tensor(out=w, in0=w, scalar=ATANH[0], in1=s, op0=ALU.add, op1=ALU.mult),
                ]
                for step in steps:
                    step().then_inc(soft, 1)
                    soft0 += 1
                    dve.wait_ge(soft, soft0)
                dve.scalar_tensor_tensor(out=w, in0=soft_v[:, m].rearrange("p b s -> p (b s)"), scalar=0.0, in1=w,
                                         op0=ALU.max, op1=ALU.add).then_inc(dt_done, 1)
            dve.wait_ge(dt_done, 2)
            dve.memset(da[:, :, :, 0:1], 0.0).then_inc(scanned, 2)

            def mask_scores(b, g, n_units):
                dve.wait_ge(filled, n_units)
                dve.nop(nofuse=True)
                dve.tensor_tensor_reduce(prob[:, b, 0:P], bank(g)[:, 0:P], mask[:, P:], 1.0, 3.0e38, ALU.add, ALU.min,
                                         smin[:, b, 0:1])
                dve.tensor_tensor_reduce(prob[:, b, P:], bank(g)[:, P:3 * P], mask[:, :], 1.0, 3.0e38, ALU.add, ALU.min,
                                         smin[:, b, 1:2]).then_inc(bank_read, 1)

            def normalise(n):
                for b in range(BATCH):
                    dve.wait_ge(exp_done, 8 * n + 2 * b + 2)
                    dve.reciprocal(sinv[:, b, :], ssum[:, b, :]).then_inc(inv_done, 1)
                for b in range(BATCH):
                    dve.wait_ge(inv_done, BATCH * n + b + 1)
                    dve.tensor_scalar(prob[:, b, 0:P], prob[:, b, 0:P], sinv[:, b, 0:1], None, ALU.mult)\
                       .then_inc(probs_ready, 1)
                    dve.tensor_scalar(prob[:, b, P:], prob[:, b, P:], sinv[:, b, 1:2], None, ALU.mult)\
                       .then_inc(probs_ready, 1)

            def scan(p, i, m):
                k = 4 * p + 2 * i + m
                dve.wait_ge(da_done, k + 1)
                dve.wait_ge(dbu_done, k + 1)
                dve.wait_ge(y_added, k + 1)
                dve.tensor_tensor_scan(state[:, m, :], da[:, m].rearrange("p b s -> p (b s)"), dbu[:, m, :], 0.0,
                                       ALU.mult, ALU.add).then_inc(scanned, 1)

            def times_c(p, i, m):
                k = 4 * p + 2 * i + m
                dve.wait_ge(scanned, k + 3)
                dve.wait_ge(bc_load[i], 32 * p + 32)
                dve.tensor_tensor(state[:, m, :], state[:, m, :], c_all[:, i, :], ALU.mult).then_inc(cmul, 1)

            dve.wait_ge(consts, 4)
            for b in range(BATCH):
                mask_scores(b, 18 + b, 19 + b)

            def pair_dve(p, last):
                for i in range(2):
                    base = PRE_UNITS + PAIR_UNITS * p + HALF_UNITS * i
                    hbase = PRE_HI + PAIR_HI * p + HALF_HI * i
                    gb = PRE_UNITS + HALF_UNITS * i
                    nxt = not (last and i == 1)
                    pt, z, hp, hz = (P_U, Z_U, 2, 8) if nxt else (P_U - 2, Z_U - 4, 0, 4)
                    normalise(2 * p + i)
                    if nxt:
                        for c in range(NC):
                            lo_qk(q_lo, q_hi, gb + Q_U + c, hbase + c, c, QSCALE)
                    scan(p, i, 0)
                    for b in range(BATCH):
                        lo(pT_lo[:, b, :], pT_hi[:, b, :], gb + pt + b, hbase + hp + b + 1, cols=3 * P)
                    times_c(p, i, 0)
                    if nxt:
                        for c in range(NC):
                            lo_qk(k_lo, k_hi, gb + K_U + c, hbase + 6 + c, c)
                    scan(p, i, 1)
                    for c in range(NC):
                        lo_qk(z_lo, z_hi, gb + z + c, hbase + hz + c, c)
                    times_c(p, i, 1)
                    if nxt:
                        for b in range(BATCH):
                            mask_scores(b, gb + S_U + b, base + S_U + b + 1)
                if not last:
                    for t in range(4):
                        lo_v(t, PRE_UNITS + V_U + t, PRE_HI + PAIR_HI * p + 20 + t)

            with dve.Fori(0, PAIRS - 1) as p:
                pair_dve(p, False)
            pair_dve(PAIRS - 1, True)

            def layer_norm(n, add, dst):
                for t in range(NT + 2):
                    if t < NT:
                        add(t).then_inc(ln_in, 1)
                    if 1 <= t <= NT:
                        dve.wait_ge(ln_in, NT * n + t)
                        dve.bn_stats(stats[:, t - 1, :], pre[:, t - 1, :]).then_inc(ln_stat, 1)
                    if t >= 2:
                        dve.wait_ge(ln_stat, NT * n + t - 1)
                        dve.bn_aggr(mv[:, t - 2, :], stats[:, t - 2, :]).then_inc(ln_mv, 1)
                dve.wait_ge(ln_mv, NT * (n + 1))
                dve.wait_ge(ln_rstd, n + 1)
                for t in range(NT):
                    dve.tensor_scalar(dst[:, t, :], pre[:, t, :], mv[:, t, 0:1], rstd[:, t:t + 1],
                                      ALU.subtract, ALU.mult).then_inc(ln_out, 1)

            dve.wait_ge(ld_xres, 16)

            def add_attention(t):
                dve.wait_ge(out_proj, t // 2 * 2 + 2)
                return dve.tensor_tensor(pre[:, t, :], acc_t[:, t, :], x_res[:, t, :], ALU.add)

            layer_norm(0, add_attention, x_res)
            dve.wait_ge(y_added, 2 + 2 * STATES)
            dve.wait_ge(ln_out, NT)
            for t in range(NT):
                b, m = t // DM, t % DM
                sz = da[:, t // 4].rearrange("p b s -> p (b s)")[:, (t % 4) * D:(t % 4 + 1) * D]
                dve.wait_ge(silu_z, t + 1)
                dve.tensor_tensor(y[:, m, b * SEQ:(b + 1) * SEQ], y[:, m, b * SEQ:(b + 1) * SEQ], sz, ALU.mult)\
                   .then_inc(gated, 1)
            dve.memset(acc[:, :], 0.0).then_inc(acc_zero, 1)

            def add_scan(t):
                dve.wait_ge(turned, t // 2 * 2 + 2)
                return dve.tensor_tensor(pre[:, t, :], bank(t // 2)[:, (t % 2) * D:(t % 2 + 1) * D], x_res[:, t, :],
                                         ALU.add)

            layer_norm(1, add_scan, x_res)
            for n in range(NC * DK):
                dve.wait_ge(x2_hi, n + 1)
                s = slice((n // DK) * CH, (n // DK + 1) * CH)
                dve.tensor_tensor(xT_lo[:, n % DK, s], bank(n), xT_hi[:, n % DK, s].bitcast(F32), ALU.subtract)\
                   .then_inc(x2_lo, 1)

            dve.wait_ge(logit, 1)
            dve.wait_ge(consts, 9)
            logits = bank(0)[:, 0:NT * NR].rearrange("p (t e) -> p t e", e=NR)
            dve.tensor_reduce(lmax[:, :], logits[:, :, 0:EXPERTS], AX.X, ALU.max).then_inc(soft, 1)
            dve.tensor_scalar(gate[:, :], logits[:, :, EXPERTS], -1.0, 80.0, ALU.mult, ALU.min).then_inc(route, 1)
            dve.wait_ge(soft, soft0 + 1)
            dve.tensor_tensor(lsub[:, :, :], logits[:, :, 0:EXPERTS],
                              lmax[:, :].unsqueeze(2).to_broadcast([P, NT, EXPERTS]), ALU.subtract).then_inc(route, 1)
            dve.wait_ge(route_e, 2)
            dve.tensor_reduce(lsum[:, :], probs[:, :, 0:EXPERTS], AX.X, ALU.add).then_inc(soft, 1)
            dve.tensor_scalar(gate[:, :], gate[:, :], 1.0, None, ALU.add).then_inc(route, 1)
            dve.wait_ge(soft, soft0 + 2)
            dve.reciprocal(linv[:, :], lsum[:, :]).then_inc(soft, 1)
            dve.wait_ge(route, 3)
            for g in range(EXPERTS, GROUPS):
                dve.reciprocal(wr[:, :, g], gate[:, :]).then_inc(route, 1)
            dve.wait_ge(soft, soft0 + 3)
            dve.tensor_tensor(probs[:, :, 0:EXPERTS], probs[:, :, 0:EXPERTS],
                              linv[:, :].unsqueeze(2).to_broadcast([P, NT, EXPERTS]), ALU.mult).then_inc(soft, 1)
            dve.wait_ge(soft, soft0 + 4)
            for t in range(NT):
                dve.max(top[:, t, :], probs[:, t, 0:EXPERTS]).then_inc(soft, 1)
            dve.wait_ge(soft, soft0 + 4 + NT)
            dve.memset(top[:, :, TOPK:], -1.0).then_inc(soft, 1)
            dve.wait_ge(soft, soft0 + 5 + NT)
            for t in range(NT):
                dve.match_replace(picked[:, t, :], top[:, t, :], probs[:, t, :], -2.0).then_inc(soft, 1)
            dve.wait_ge(soft, soft0 + 5 + 2 * NT)
            dve.scalar_tensor_tensor(out=wr[:, :, 0:EXPERTS], in0=picked[:, :, 0:EXPERTS], scalar=-2.0,
                                     in1=probs[:, :, 0:EXPERTS], op0=ALU.is_equal, op1=ALU.mult).then_inc(route, 1)
            s0 = soft0 + 5 + 2 * NT
            dve.wait_ge(route, 3 + (GROUPS - EXPERTS) + 1)
            for part in range(3):
                dst = wpart[:, :, 32 * part:32 * part + GROUPS]
                dve.tensor_copy(dst, wr[:, :, :]).then_inc(soft, 1)
                s0 += 1
                dve.wait_ge(soft, s0)
                if part < 2:
                    dve.tensor_tensor(wr[:, :, :], wr[:, :, :], dst, ALU.subtract).then_inc(soft, 1)
                    s0 += 1
                    dve.wait_ge(soft, s0)

            def mlp_dve(j, g0, first):
                for c in range(NC):
                    s = slice(c * CH, (c + 1) * CH)
                    dve.wait_ge(silu_d, NC * j + c + 1)
                    dve.wait_ge(up_f, NC * j + c + 1)
                    if not first:
                        dve.wait_ge(hidw_d, NC * (j - 1) + c + 1)
                    dve.tensor_tensor(hid[:, s], silu_g[:, s], bank(g0 + 3 * c + 1), ALU.mult).then_inc(hid_d, 1)
                    dve.wait_ge(hid_d, NC * j + c + 1)
                    dve.wait_ge(wb_f, NC * j + c + 1)
                    if not first:
                        dve.wait_ge(hlo_d, NC * (j - 1) + c + 1)
                    dve.tensor_tensor(hidw[:, s], hid[:, s], bank(g0 + 3 * c + 2), ALU.mult).then_inc(hidw_d, 1)

            mlp_dve(0, 2, True)
            with dve.Fori(0, HT // 2 - 1) as r:
                mlp_dve(2 * r + 1, 2 + 6, False)
                mlp_dve(2 * r + 2, 2, False)
            mlp_dve(HT - 1, 2 + 6, False)

            def add_mlp(t):
                dve.wait_ge(down_d, HT + t // 2 * 2 + 1)
                return dve.tensor_tensor(pre[:, t, :], acc_t[:, t, :], x_res[:, t, :], ALU.add)

            layer_norm(2, add_mlp, pre)

        @block.tensor
        def _(pe):
            def split_mm(dst, pairs, start=True):
                last = len(pairs) - 1
                for n, (lhs, rhs) in enumerate(pairs):
                    pe.matmul(dst, lhs[0], rhs[0], start=start and n == 0, stop=False, skip_group_check=True)
                    pe.matmul(dst, lhs[0], rhs[1], start=False, stop=False, skip_group_check=True)
                    mm = pe.matmul(dst, lhs[1], rhs[0], start=False, stop=n == last, skip_group_check=True)
                return mm

            pe.wait_ge(ld_ctx, 32)
            for m in range(DM):
                for c in range(NC):
                    pe.matmul(bank(NC * m + c), inw[:, m * P:(m + 1) * P], ctxT[:, c * CH:(c + 1) * CH],
                              start=True, stop=True).then_inc(filled, 1)

            def proj(g, i, which, c):
                s = slice(c * CH, (c + 1) * CH)
                split_mm(bank(g), [((wqk_hi[i][:, (which * DK + k) * P:(which * DK + k + 1) * P],
                                     wqk_lo[i][:, (which * DK + k) * P:(which * DK + k + 1) * P]),
                                    (xT_hi[:, k, s], xT_lo[:, k, s])) for k in range(DK)]).then_inc(filled, 1)

            def values(g, t2):
                for j in range(2):
                    tok = slice((2 * t2 + j) * P, (2 * t2 + j + 1) * P)
                    mm = split_mm(bank(g)[:, j * 2 * HD:(j + 1) * 2 * HD],
                                  [((xT_hi[:, k, tok], xT_lo[:, k, tok]),
                                    (wv_hi[:, k * 2 * HD:(k + 1) * 2 * HD], wv_lo[:, k * 2 * HD:(k + 1) * 2 * HD]))
                                   for k in range(DK)], start=j == 0)
                mm.then_inc(filled, 1)

            def scores(g, b):
                for t in range(2):
                    qs = slice(b * SEQ + t * P, b * SEQ + (t + 1) * P)
                    ks = slice(b * SEQ, b * SEQ + (t + 1) * P)
                    dst = bank(g)[:, 0:P] if t == 0 else bank(g)[:, P:3 * P]
                    mm = split_mm(dst, [((q_hi[:, qs], q_lo[:, qs]), (k_hi[:, ks], k_lo[:, ks]))], start=t == 0)
                mm.then_inc(filled, 1)

            def turn_probs(g, b):
                for t in range(3):
                    mm = pe.transpose(bank(g)[:, t * P:(t + 1) * P], prob[:, b, t * P:(t + 1) * P], ident[:, :])
                mm.then_inc(filled, 1)

            def context(g, i, c):
                for j in range(2):
                    b = 2 * c + j
                    e = slice(i * HD, (i + 1) * HD)
                    split_mm(bank(g)[:, j * SEQ:(j + 1) * SEQ],
                             [((v_hi[:, 2 * b, e], v_lo[:, 2 * b, e]),
                               (pT_hi[:, b, 0:2 * P], pT_lo[:, b, 0:2 * P]))], start=j == 0)
                    mm = split_mm(bank(g)[:, j * SEQ + P:(j + 1) * SEQ],
                                  [((v_hi[:, 2 * b + 1, e], v_lo[:, 2 * b + 1, e]),
                                    (pT_hi[:, b, 2 * P:], pT_lo[:, b, 2 * P:]))], start=False)
                mm.then_inc(filled, 1)

            def out_projection(i, signal):
                for t in range(NT):
                    s = slice(t * P, (t + 1) * P)
                    mm = split_mm(acc_t[:, t, :], [((z_hi[:, s], z_lo[:, s]), (wo_hi[i][:, :], wo_lo[i][:, :]))],
                                  start=False)
                    if signal:
                        mm.then_inc(out_proj, 1)

            pe.wait_ge(x_lo_s, DK)
            pe.wait_ge(wqk_s, 1)
            for c in range(NC):
                pe.wait_ge(pre_read, 1 + c)
                proj(4 + c, 0, 0, c)
            for c in range(NC):
                pe.wait_ge(pre_read, 3 + c)
                proj(6 + c, 0, 1, c)
            pe.wait_ge(wv_s, 1)
            for t in range(4):
                pe.wait_ge(bank_read, 1 + t)
                values(8 + t, t)
            pe.wait_ge(u_done, 2)
            pe.wait_ge(ld_xw, 32)
            for c in range(NC):
                pe.wait_ge(bank_read, 5 + c)
                for m in range(DM):
                    mm = pe.matmul(bank(12 + c)[0:XDBL, :], xw[:, m, :], u[:, m, c * CH:(c + 1) * CH],
                                   start=m == 0, stop=m == DM - 1)
                mm.then_inc(filled, 1)
            pe.wait_ge(pre_read, 6)
            pe.wait_ge(bank_read, 8)
            for m in range(DM):
                for c in range(NC):
                    pe.matmul(bank(14 + NC * m + c), dtw[:, m * P:(m + 1) * P], xdbl[0:RANK, c * CH:(c + 1) * CH],
                              start=True, stop=True).then_inc(filled, 1)
            for b in range(BATCH):
                pe.wait_ge(pre_read, 7 + b)
                scores(18 + b, b)

            def pair_pe(p, last):
                for i in range(2):
                    a = 2 * p + i
                    gb = PRE_UNITS + HALF_UNITS * i
                    before = PRE_ATTN + PAIR_UNITS * p + HALF_UNITS * i - 3
                    nxt = not (last and i == 1)
                    pt, z = (P_U, Z_U) if nxt else (P_U - 2, Z_U - 4)
                    if nxt:
                        pe.wait_ge(wqk_s, a + 2)
                        for c in range(NC):
                            pe.wait_ge(bank_read, before + Q_U + c)
                            proj(gb + Q_U + c, 1 - i, 0, c)
                    for b in range(BATCH):
                        pe.wait_ge(bank_read, before + pt + b)
                        pe.wait_ge(probs_ready, 8 * a + 2 * b + 2)
                        turn_probs(gb + pt + b, b)
                    if nxt:
                        for c in range(NC):
                            pe.wait_ge(bank_read, before + K_U + c)
                            proj(gb + K_U + c, 1 - i, 1, c)
                    for c in range(NC):
                        pe.wait_ge(bank_read, before + z + c if nxt else before + pt + 2 * c + 5)
                        context(gb + z + c, i, c)
                    if nxt:
                        for b in range(BATCH):
                            pe.wait_ge(bank_read, before + S_U + b)
                            scores(gb + S_U + b, b)
                    else:
                        pe.wait_ge(bank_read, before + z + 5)
                    pe.wait_ge(wo_s, a + 1)
                    out_projection(i, last and i == 1)
                if not last:
                    pe.wait_ge(wv_s, p + 2)
                    for t in range(4):
                        pe.wait_ge(bank_read, PRE_ATTN + PAIR_UNITS * p + V_U + t - 3)
                        values(PRE_UNITS + V_U + t, t)

            pe.wait_ge(acc_zero, 1)
            pe.wait_ge(consts, 5)
            with pe.Fori(0, PAIRS - 1) as p:
                pair_pe(p, False)
            pair_pe(PAIRS - 1, True)

            total_attn = PRE_ATTN + PAIR_UNITS * (PAIRS - 1) + 2 * HALF_UNITS - 8
            pe.wait_ge(bank_read, total_attn)
            pe.wait_ge(gated, NT)
            for t in range(NT):
                b, l = t // 2, t % 2
                for m in range(DM):
                    mm = pe.transpose(bank(t // 2)[:, (t % 2) * D + m * P:(t % 2) * D + (m + 1) * P],
                                      y[:, m, b * SEQ + l * P:b * SEQ + (l + 1) * P], ident[:, :])
                mm.then_inc(turned, 1)
            for n in range(NC * DK):
                k, c = n % DK, n // DK
                for j in range(4):
                    t = 4 * c + j
                    if k == 0:
                        pe.wait_ge(ln_out, NT + t + 1)
                    mm = pe.transpose(bank(n)[:, j * P:(j + 1) * P], x_res[:, t, k * P:(k + 1) * P], ident[:, :])
                mm.then_inc(x2_turned, 1)
            pe.wait_ge(rw_s, 1)
            pe.wait_ge(x2_lo, NC * DK)
            for t in range(NT):
                s = slice(t * P, (t + 1) * P)
                mm = split_mm(bank(0)[:, t * NR:(t + 1) * NR],
                              [((xT_hi[:, k, s], xT_lo[:, k, s]), (rw_hi[:, k, :], rw_lo[:, k, :]))
                               for k in range(DK)], start=t == 0)
            mm.then_inc(logit, 1)
            pe.wait_ge(soft, 2 * (TAPS - 1) + 18 + 5 + 2 * NT + 5)
            for t in range(NT):
                mm = pe.transpose(bank(1)[0:NSEL, t * P // 2:(t + 1) * P // 2].bitcast(BF16), wpart[:, t, :],
                                  ident_b[:, :])
            mm.then_inc(wt_turned, 1)
            pe.wait_ge(consts, 15)
            pe.wait_ge(wt_done, 1)
            pe.wait_ge(acc_zero, 2)

            def gate_up(j, i, g0, first):
                pe.wait_ge(gu_s, j + 1)
                for c in range(NC):
                    s = slice(c * CH, (c + 1) * CH)
                    for which, done in ((0, gate_f), (1, up_f)):
                        if which == 0 and not first:
                            pe.wait_ge(hidw_d, NC * (j - 1) + c + 1)
                        if which == 1 and c == 0 and not first:
                            pe.wait_ge(silu_d, NC * (j - 1) + 2)
                        if which == 1 and c == 1:
                            pe.wait_ge(silu_d, NC * j + 1)
                        split_mm(bank(g0 + 3 * c + which),
                                 [((gu_hi[i][:, (2 * which + k) * P:(2 * which + k + 1) * P],
                                    gu_lo[i][:, (2 * which + k) * P:(2 * which + k + 1) * P]),
                                   (xT_hi[:, k, s], xT_lo[:, k, s])) for k in range(DK)]).then_inc(done, 1)
                    if c == 0 and not first:
                        pe.wait_ge(hid_d, NC * (j - 1) + 2)
                    if c == 1:
                        pe.wait_ge(hid_d, NC * j + 1)
                    pe.matmul(bank(g0 + 3 * c + 2), sel[:, bass.ds(j * P, P)], wT[:, s], start=True, stop=True)\
                      .then_inc(wb_f, 1)

            def down(j, i, signal_tiles):
                pe.wait_ge(dn_s, j + 1)
                for t in range(NT):
                    if t % 4 == 0:
                        pe.wait_ge(hlo_d, NC * j + t // 4 + 1)
                    s = slice(t * P, (t + 1) * P)
                    mm = split_mm(acc_t[:, t, :], [((h_hi[i][:, s], h_lo[i][:, s]),
                                                    (dn_hi[i][:, :], dn_lo[i][:, :]))], start=False)
                    if signal_tiles:
                        mm.then_inc(down_d, 1)
                if not signal_tiles:
                    mm.then_inc(down_d, 1)

            gate_up(0, 0, 2, True)
            with pe.Fori(0, HT // 2 - 1) as r:
                gate_up(2 * r + 1, 1, 2 + 6, False)
                down(2 * r, 0, False)
                gate_up(2 * r + 2, 0, 2, False)
                down(2 * r + 1, 1, False)
            gate_up(HT - 1, 1, 2 + 6, False)
            down(HT - 2, 0, False)
            down(HT - 1, 1, True)


def kernel(x, ctx_1024, L0_attn_W_Q, L0_attn_W_K, L0_attn_W_V, L0_attn_W_O, L0_xattn_in_proj_w, L0_xattn_conv_w,
           L0_xattn_conv_b, L0_xattn_x_proj_w, L0_xattn_dt_proj_w, L0_xattn_dt_proj_b, L0_xattn_A_log, L0_xattn_D,
           L0_ffn_router_w, L0_ffn_gate_w, L0_ffn_up_w, L0_ffn_down_w, L0_ffn_shared_gate_w, L0_ffn_shared_up_w,
           L0_ffn_shared_down_w, L0_ffn_se_gate_w):
    import numpy as np
    import concourse.bacc as bacc
    from concourse.bass_utils import run_bass_kernel_spmd as run

    def parts(w, n):
        return np.asarray(w).T.reshape(n, P, -1).transpose(1, 0, 2)

    xf = np.asarray(x).reshape(TOK, D)
    heads = lambda w: np.asarray(w).transpose(0, 2, 1).reshape(HEADS, DK, P, HD)
    wq, wk, wv = heads(L0_attn_W_Q), heads(L0_attn_W_K), heads(L0_attn_W_V)
    wqk = np.stack([wq, wk], 1).transpose(0, 3, 1, 2, 4).reshape(HEADS, P, 4 * P)
    wv = wv.reshape(PAIRS, 2, DK, P, HD).transpose(0, 3, 2, 1, 4).reshape(PAIRS, P, 4 * P)
    wo = np.asarray(L0_attn_W_O).transpose(0, 2, 1)
    chan = np.concatenate([np.asarray(L0_xattn_conv_w)[:, 0, :], np.asarray(L0_xattn_conv_b)[:, None],
                           np.asarray(L0_xattn_dt_proj_b)[:, None], np.asarray(L0_xattn_D)[:, None],
                           np.asarray(L0_xattn_A_log)], 1).reshape(DM, P, -1).transpose(1, 0, 2)
    router = np.concatenate([np.asarray(L0_ffn_router_w), np.asarray(L0_ffn_se_gate_w),
                             np.zeros((1, D), np.float32)], 0)
    pad = np.zeros((HT * P - HID, D), np.float32)
    gw = np.concatenate([np.asarray(L0_ffn_gate_w).reshape(-1, D), np.asarray(L0_ffn_shared_gate_w), pad], 0)
    uw = np.concatenate([np.asarray(L0_ffn_up_w).reshape(-1, D), np.asarray(L0_ffn_shared_up_w), pad], 0)
    dw = np.concatenate([np.asarray(L0_ffn_down_w).transpose(0, 2, 1).reshape(-1, D),
                         np.asarray(L0_ffn_shared_down_w).T, pad], 0)
    turn = lambda w: w.reshape(HT, P, DK, P).transpose(0, 3, 2, 1).reshape(HT, P, DK * P)
    wf = np.concatenate([turn(gw), turn(uw), dw.reshape(HT, P, D)], 2)
    arrays = {
        "xT": parts(xf, DK), "x": xf.reshape(NT, P, D).transpose(1, 0, 2),
        "ctxT": np.asarray(ctx_1024).reshape(TOK, CTX).T, "inw": np.asarray(L0_xattn_in_proj_w).T,
        "xw": parts(L0_xattn_x_proj_w, DM), "dtw": np.asarray(L0_xattn_dt_proj_w).T, "chan": chan,
        "wqk": wqk, "wv": wv, "wo": wo, "rw": parts(router, DK), "wf": wf,
    }
    nc = bacc.Bacc("TRN2", target_bir_lowering=False, num_devices=1)
    feed, ins = {}, {}
    for name, a in arrays.items():
        feed[f"in_{name}"] = np.ascontiguousarray(a)
        ins[name] = nc.dram_tensor(f"in_{name}", a.shape, F32, kind="ExternalInput").ap()
    out = nc.dram_tensor("out_0", (TOK, D), F32, kind="ExternalOutput").ap()
    decoder_layer(nc, ins, out)
    r = run(nc, [feed], core_ids=[0])
    return r.results[0]["out_0"].reshape(BATCH, SEQ, D)
```

```python
from contextlib import ExitStack

import concourse.bass as bass
from concourse import mybir

F32 = mybir.dt.float32
F32R = mybir.dt.float32r
BF16 = mybir.dt.bfloat16
ALU = mybir.AluOpType
ACT = mybir.ActivationFunctionType
AX = mybir.AxisListType

P = 128
BATCH, SEQ, D = 4, 256, 256
TOK = BATCH * SEQ
NT = TOK // P
DK = D // P
CH = 512
NC = TOK // CH
HEADS, HD = 16, 128
PAIRS = HEADS // 2
QSCALE = -1.0 / float(HD) ** 0.5
MASKED = 1.0e30
CTX = 128
DI = 256
DM = DI // P
STATES, TAPS, RANK = 16, 4, 8
XDBL = RANK + 2 * STATES
EXPERTS, EI, SI = 16, 176, 704
GROUPS = (EXPERTS * EI + SI) // EI
HID = GROUPS * EI
HT = -(-HID // P)
TOPK = 4
NR = EXPERTS + 2
NSEL = 96
EPS = 1e-5
LP_LEAD = 0.005232687917294774
LP = LP_LEAD ** 0.125
LP_QUADS = ((-2.3216868949994938, 0.43240693469890085), (1.0093577160564058, 1.106062565110738),
            (-1.424736015210064, 2.702104075306238), (-0.08225193417593676, 3.2574693061961))

PRE_UNITS = 22
PRE_ATTN = 12
PAIR_UNITS, HALF_UNITS = 32, 14
Q_U, P_U, K_U, Z_U, S_U, V_U = 0, 2, 6, 8, 10, 28
PRE_HI, PAIR_HI, HALF_HI = 8, 24, 10


def decoder_layer(nc, ins, out):
    with ExitStack() as ctx:
        def sb(name, shape, dt=F32):
            return ctx.enter_context(nc.sbuf_tensor(name, shape, dt))

        def sem(name):
            return ctx.enter_context(nc.semaphore(name))

        xT_hi = sb("xT_hi", [P, DK, TOK], F32R)
        xT_lo = sb("xT_lo", [P, DK, TOK], F32R)
        x_res = sb("x_res", [P, NT, D])
        stage = sb("stage", [P, DK, TOK])
        wqk_raw = sb("wqk_raw", [P, 4 * P])
        wv_raw = sb("wv_raw", [P, 4 * P])
        wo_raw = sb("wo_raw", [P, D])
        wqk_hi = [sb(f"wqk_hi{i}", [P, 4 * P], F32R) for i in range(2)]
        wqk_lo = [sb(f"wqk_lo{i}", [P, 4 * P], F32R) for i in range(2)]
        wv_hi = sb("wv_hi", [P, 4 * P], F32R)
        wv_lo = sb("wv_lo", [P, 4 * P], F32R)
        wo_hi = [sb(f"wo_hi{i}", [P, D], F32R) for i in range(2)]
        wo_lo = [sb(f"wo_lo{i}", [P, D], F32R) for i in range(2)]
        q_hi, q_lo = sb("q_hi", [P, TOK], F32R), sb("q_lo", [P, TOK], F32R)
        k_hi, k_lo = sb("k_hi", [P, TOK], F32R), sb("k_lo", [P, TOK], F32R)
        z_hi, z_lo = sb("z_hi", [P, TOK], F32R), sb("z_lo", [P, TOK], F32R)
        v_hi = sb("v_hi", [P, NT, 2 * HD], F32R)
        v_lo = sb("v_lo", [P, NT, 2 * HD], F32R)
        prob = sb("prob", [P, BATCH, 3 * P])
        pT_hi = sb("pT_hi", [P, BATCH, 3 * P], F32R)
        pT_lo = sb("pT_lo", [P, BATCH, 3 * P], F32R)
        smin = sb("smin", [P, BATCH, 2])
        ssum = sb("ssum", [P, BATCH, 2])
        sinv = sb("sinv", [P, BATCH, 2])
        mask = sb("mask", [P, 2 * P])
        ident = sb("ident", [P, P])
        ident_b = sb("ident_b", [P, P], BF16)
        inw = sb("inw", [P, DI])
        xw = sb("xw", [P, DM, XDBL])
        dtw = sb("dtw", [RANK, DI])
        chan = sb("chan", [P, DM, TAPS + 3 + STATES])
        bc = sb("bc", [P, 4 * TOK])
        b_all = bc[:, 0:2 * TOK].rearrange("p (i t) -> p i t", t=TOK)
        c_all = bc[:, 2 * TOK:].rearrange("p (i t) -> p i t", t=TOK)
        n_pad = DM * BATCH * (SEQ + TAPS - 1)
        padded = bc[:, 0:n_pad].rearrange("p (m b s) -> p m b s", m=DM, b=BATCH)
        ctxT = bc[:, n_pad:n_pad + TOK]
        u = sb("u", [P, DM, TOK])
        xdbl = sb("xdbl", [XDBL, TOK])
        dt = sb("dt", [P, DM, TOK])
        dtu = sb("dtu", [P, DM, TOK])
        y = sb("y", [P, DM, TOK])
        lp_bias = sb("lp_bias", [P, len(LP_QUADS)])
        a_neg = sb("a_neg", [P, DM, STATES])
        da = sb("da", [P, DM, BATCH, SEQ])
        dbu = sb("dbu", [P, DM, TOK])
        state = sb("state", [P, DM, TOK])
        stats = sb("stats", [P, NT, 6])
        mv = sb("mv", [P, NT, 2])
        veps = sb("veps", [P, NT])
        rstd = sb("rstd", [P, NT])
        negmean = sb("negmean", [P, NT])
        nbias = sb("nbias", [P, NT])
        mhalf = sb("mhalf", [P, NT])
        rw_raw = sb("rw_raw", [P, DK, NR])
        rw_hi, rw_lo = sb("rw_hi", [P, DK, NR], F32R), sb("rw_lo", [P, DK, NR], F32R)
        lmax = sb("lmax", [P, NT])
        lsub = sb("lsub", [P, NT, EXPERTS])
        lsum = sb("lsum", [P, NT])
        linv = sb("linv", [P, NT])
        probs = sb("probs", [P, NT, EXPERTS + 8])
        picked = sb("picked", [P, NT, EXPERTS + 8])
        top = sb("top", [P, NT, 8])
        gate = sb("gate", [P, NT])
        wr = sb("wr", [P, NT, GROUPS])
        wpart = sb("wpart", [P, NT, NSEL], BF16)
        wT = sb("wT", [NSEL, TOK], BF16)
        sel = sb("sel", [NSEL, HT * P], BF16)
        h_hi, h_lo = [q_hi, k_hi], [q_lo, k_lo]
        f_raw = [prob[:, 2 * i:2 * i + 2, :].rearrange("p b s -> p (b s)") for i in range(2)]
        gu_hi, gu_lo = wqk_hi, wqk_lo
        dn_hi, dn_lo = wo_hi, wo_lo
        silu_g, hid = da[:, 0].rearrange("p b s -> p (b s)"), dbu[:, 0, :]
        hidw = state[:, 0, :]

        logit_sb = xdbl[0:NR, :]
        def silu_x1(t):
            return da[:, t // 4].rearrange("p b s -> p (b s)")[:, (t % 4) * D:(t % 4 + 1) * D]

        pre = stage[:, :, :].rearrange("p a t -> p (a t)").rearrange("p (t d) -> p t d", d=D)
        prod = [None] + [w[:, 1, :].rearrange("p (b s) -> p b s", s=SEQ) for w in (dt, dtu, state)]
        soft_v, soft_e = da, dbu
        squares = [state, stage, dtu, state]
        conv = [dtu[:, 0, :], dbu[:, 1, :]]

        acc = ctx.enter_context(nc.psum_tensor("acc", [P, NT * D], F32))
        ring = ctx.enter_context(nc.psum_tensor("ring", [P, 4, CH], F32))
        acc_t = acc[:, :].rearrange("p (t d) -> p t d", d=D)

        def bank(g):
            return ring[:, g % 4, :]

        bc_dram = nc.dram_tensor("bc_dram", [2 * STATES, TOK], F32, kind="Internal").ap()

        filled = sem("filled")
        pre_read = sem("pre_read")
        bank_read = sem("bank_read")
        hi_done = sem("hi_done")
        exp_done = sem("exp_done")
        inv_done = sem("inv_done")
        probs_ready = sem("probs_ready")
        ld_x, ld_xres, ld_ctx = sem("ld_x"), sem("ld_xres"), sem("ld_ctx")
        ld_chan, ld_xw, ld_rw = sem("ld_chan"), sem("ld_xw"), sem("ld_rw")
        ld_wqk, ld_wv, ld_wo = sem("ld_wqk"), sem("ld_wv"), sem("ld_wo")
        x_hi_s, x_lo_s = sem("x_hi_s"), sem("x_lo_s")
        wqk_h, wv_h, wo_h = sem("wqk_h"), sem("wv_h"), sem("wo_h")
        wqk_s, wv_s, wo_s = sem("wqk_s"), sem("wv_s"), sem("wo_s")
        consts = sem("consts")
        lp_const = sem("lp_const")
        pad_zero, acc_open, acc_set = sem("pad_zero"), sem("acc_open"), sem("acc_set")
        tap_prod = sem("tap_prod")
        conv_taps = [sem("conv_taps0"), sem("conv_taps1")]
        u_done, a_exp, a_done = sem("u_done"), sem("a_exp"), sem("a_done")
        bc_stored, ld_sel, dt_done, dtu_done = sem("bc_stored"), sem("ld_sel"), sem("dt_done"), sem("dtu_done")
        soft_abs, soft_x, soft_pos = sem("soft_abs"), sem("soft_x"), sem("soft_pos")
        squared = [sem("squared0"), sem("squared1")]
        quads = [sem("quads0"), sem("quads1")]
        bc_load = [sem("bc_load0"), sem("bc_load1")]
        da_done, dbu_done = sem("da_done"), sem("dbu_done")
        scanned, cmul, y_added = sem("scanned"), sem("cmul"), sem("y_added")
        out_proj = sem("out_proj")
        ln_in, ln_stat, ln_mv = sem("ln_in"), sem("ln_stat"), sem("ln_mv")
        ln_eps, ln_rstd, ln_bias = sem("ln_eps"), sem("ln_rstd"), sem("ln_bias")
        x1_done, x2_v, x2_a = sem("x1_done"), sem("x2_v"), sem("x2_a")
        out_first, out_second = sem("out_first"), sem("out_second")
        silu_z, gated, turned = sem("silu_z"), sem("gated"), sem("turned")
        x2_turned, x2_hi, x2_lo = sem("x2_turned"), sem("x2_hi"), sem("x2_lo")
        logit_t, logit_read = sem("logit_t"), sem("logit_read")
        rw_h, rw_s, logit = sem("rw_h"), sem("rw_s"), sem("logit")
        route, route_e, route_v = sem("route"), sem("route_e"), sem("route_v")
        wt_turned, wt_done = sem("wt_turned"), sem("wt_done")
        ld_f = [sem("ld_f0"), sem("ld_f1")]
        gu_h, gu_s, dn_h, dn_s = sem("gu_h"), sem("gu_s"), sem("dn_h"), sem("dn_s")
        gate_f, up_f, wb_f = sem("gate_f"), sem("up_f"), sem("wb_f")
        silu_d, hid_d, hidw_d = sem("silu_d"), sem("hid_d"), sem("hidw_d")
        hhi_d, hlo_d = sem("hhi_d"), sem("hlo_d")
        down_d = sem("down_d")
        stored = sem("stored")

        block = ctx.enter_context(nc.Block())

        @block.sync
        def _(sp):
            sp.dma_start(ctxT[:, :], ins["ctxT"]).then_inc(ld_ctx, 16)
            sp.dma_start(inw[:, :], ins["inw"]).then_inc(ld_ctx, 16)
            sp.dma_start(chan[:, :, :], ins["chan"]).then_inc(ld_chan, 16)
            sp.dma_start(stage[:, :, :], ins["xT"]).then_inc(ld_x, 16)
            sp.dma_start(wqk_raw[:, :], ins["wqk"][0, :, :]).then_inc(ld_wqk, 16)
            sp.dma_start(wv_raw[:, :], ins["wv"][0, :, :]).then_inc(ld_wv, 16)
            sp.dma_start(xw[:, :, :], ins["xw"]).then_inc(ld_xw, 16)
            sp.dma_start(dtw[:, :], ins["dtw"]).then_inc(ld_xw, 16)
            sp.dma_start(wo_raw[:, :], ins["wo"][0, :, :]).then_inc(ld_wo, 16)
            sp.dma_start(x_res[:, :, :], ins["x"]).then_inc(ld_xres, 16)
            sp.dma_start(rw_raw[:, :, :], ins["rw"]).then_inc(ld_rw, 16)
            sp.wait_ge(wqk_s, 1)
            sp.dma_start(wqk_raw[:, :], ins["wqk"][1, :, :]).then_inc(ld_wqk, 16)
            sp.wait_ge(pre_read, 6)
            sp.dma_start(bc_dram, xdbl[RANK:XDBL, :]).then_inc(bc_stored, 16)
            sp.wait_ge(bc_stored, 16)

            def load_bc(n, i):
                sp.dma_start(b_all[:, i, :], bc_dram[bass.ds(n, 1), :].to_broadcast([P, TOK])).then_inc(bc_load[i], 16)
                sp.dma_start(c_all[:, i, :], bc_dram[bass.ds(n + STATES, 1), :].to_broadcast([P, TOK]))\
                  .then_inc(bc_load[i], 16)

            for i in range(2):
                load_bc(i, i)

            def pair_loads(p, first, last):
                for i in range(2):
                    a = 2 * p + i
                    if not last:
                        sp.wait_ge(wqk_s, a + 2)
                        sp.dma_start(wqk_raw[:, :], ins["wqk"][bass.ds(a + 2, 1), :, :].rearrange("h p n -> (h p) n"))\
                          .then_inc(ld_wqk, 16)
                    if not (last and i == 1):
                        sp.wait_ge(wo_s, a + 1)
                        sp.dma_start(wo_raw[:, :], ins["wo"][bass.ds(a + 1, 1), :, :].rearrange("h p n -> (h p) n"))\
                          .then_inc(ld_wo, 16)
                    if i == 0 and not last:
                        sp.wait_ge(wv_s, p + 1)
                        sp.dma_start(wv_raw[:, :], ins["wv"][bass.ds(p + 1, 1), :, :].rearrange("h p n -> (h p) n"))\
                          .then_inc(ld_wv, 16)
                    if not (first and i == 0) and not (last and i == 1):
                        n = 2 * p - 1 + i
                        sp.wait_ge(dbu_done, 2 * n + 2)
                        sp.wait_ge(cmul, 2 * n + 2)
                        load_bc(n + 2, 1 - i)

            pair_loads(0, True, False)
            with sp.Fori(1, PAIRS - 1) as p:
                pair_loads(p, False, False)
            pair_loads(PAIRS - 1, False, True)
            sp.wait_ge(consts, 11)
            for r in range(32, NSEL, 32):
                sp.dma_start(sel[r:r + 32, :], sel[0:32, :]).then_inc(ld_sel, 16)
            sp.wait_ge(filled, PRE_UNITS + PAIR_UNITS * (PAIRS - 1) + HALF_UNITS + BATCH)
            for i in range(2):
                sp.dma_start(f_raw[i], ins["wf"][i, :, :]).then_inc(ld_f[i], 16)

            def mlp_load(j, i):
                sp.wait_ge(dn_s, j - 1)
                sp.dma_start(f_raw[i], ins["wf"][bass.ds(j, 1), :, :].rearrange("h p n -> (h p) n"))\
                  .then_inc(ld_f[i], 16)

            with sp.Fori(0, HT // 2 - 1) as r:
                for i in range(2):
                    mlp_load(2 * r + 2 + i, i)
            for t in range(NT):
                if t < 4:
                    sp.wait_ge(out_first, t + 1)
                else:
                    sp.wait_ge(out_second, t - 3)
                sp.dma_start(out[t * P:(t + 1) * P, :], pre[:, t, :]).then_inc(stored, 16)
            sp.wait_ge(stored, 16 * NT)

        @block.gpsimd
        def _(pool):
            pool.memset(ident[:, :], 0.0).then_inc(consts, 1)
            pool.memset(mask[:, :], 0.0).then_inc(consts, 1)
            pool.memset(padded[:, :, :, 0:TAPS - 1], 0.0).then_inc(pad_zero, 1)
            pool.wait_ge(consts, 2)
            pool.affine_select(out=ident[:, :], in_=ident[:, :], compare_op=ALU.not_equal, fill=1.0,
                               base=0, pattern=[[-1, P]], channel_multiplier=1).then_inc(consts, 1)
            pool.affine_select(out=mask[:, P:2 * P], in_=mask[:, P:2 * P], compare_op=ALU.is_ge,
                               fill=MASKED, base=0, pattern=[[-1, P]], channel_multiplier=1).then_inc(consts, 1)
            pool.wait_ge(consts, 4)
            pool.tensor_scalar(ident_b[:, :], ident[:, :], 1.0, 0.0, ALU.mult, ALU.add).then_inc(consts, 1)

            for k, (root, _) in enumerate(LP_QUADS):
                pool.memset(lp_bias[:, k:k + 1], LP * root).then_inc(lp_const, 1)

            def split(raw, hi, lo, hi_sem, lo_sem, n):
                pool.nop(nofuse=True)
                pool.tensor_scalar(hi, raw, 1.0, 0.0, ALU.mult, ALU.add).then_inc(hi_sem, 1)
                pool.wait_ge(hi_sem, n)
                pool.tensor_tensor(lo, raw, hi.bitcast(F32), ALU.subtract).then_inc(lo_sem, 1)

            pool.wait_ge(ld_wqk, 16)
            split(wqk_raw[:, :], wqk_hi[0][:, :], wqk_lo[0][:, :], wqk_h, wqk_s, 1)
            pool.wait_ge(ld_wv, 16)
            split(wv_raw[:, :], wv_hi[:, :], wv_lo[:, :], wv_h, wv_s, 1)
            pool.wait_ge(pre_read, NC * DM)
            pool.wait_ge(pad_zero, 1)
            dst = conv[1].rearrange("p (b s) -> p b s", s=SEQ)
            pool.tensor_scalar(dst, padded[:, 1, :, 0:SEQ], chan[:, 1, 0:1], 1.0, ALU.mult, ALU.mult)\
                .then_inc(conv_taps[1], 1)
            for k in range(1, TAPS):
                pool.wait_ge(tap_prod, k)
                pool.wait_ge(conv_taps[1], k)
                pool.tensor_tensor(dst, dst, prod[k], ALU.add).then_inc(conv_taps[1], 1)
            pool.wait_ge(ld_wqk, 32)
            split(wqk_raw[:, :], wqk_hi[1][:, :], wqk_lo[1][:, :], wqk_h, wqk_s, 2)
            pool.wait_ge(ld_wo, 16)
            split(wo_raw[:, :], wo_hi[0][:, :], wo_lo[0][:, :], wo_h, wo_s, 1)
            for m in range(DM):
                pool.wait_ge(u_done, m + 1)
                pool.tensor_scalar(y[:, m, :], u[:, m, :], chan[:, m, TAPS + 2:TAPS + 3], 1.0,
                                   ALU.mult, ALU.mult).then_inc(y_added, 1)

            def late_constants():
                pool.memset(mhalf[:, :], -0.5).then_inc(consts, 1)
                pool.memset(probs[:, :, EXPERTS:EXPERTS + 8], -1.0).then_inc(consts, 1)
                pool.memset(wpart[:, :, :], 0.0).then_inc(consts, 1)
                pool.memset(sel[0:32, :], 1.0).then_inc(consts, 1)
                pool.wait_ge(consts, 9)
                pool.affine_select(out=sel[0:32, :], in_=sel[0:32, :], compare_op=ALU.is_ge, fill=0.0,
                                   base=0, pattern=[[1, HT * P]], channel_multiplier=-EI).then_inc(consts, 1)
                pool.wait_ge(consts, 10)
                pool.affine_select(out=sel[0:32, :], in_=sel[0:32, :], compare_op=ALU.is_ge, fill=0.0,
                                   base=EI - 1, pattern=[[-1, HT * P]], channel_multiplier=EI).then_inc(consts, 1)

            def make_dbu(n, i, m):
                pool.wait_ge(bc_load[i], 16 * (n - i) + 32)
                pool.wait_ge(scanned, 2 * n + m + 1)
                pool.tensor_tensor(dbu[:, m, :], dtu[:, m, :], b_all[:, i, :], ALU.mult).then_inc(dbu_done, 1)

            def add_y(n, m):
                pool.wait_ge(cmul, 2 * n + m + 1)
                pool.wait_ge(y_added, 2 * n + m + 1)
                pool.tensor_tensor(y[:, m, :], y[:, m, :], state[:, m, :], ALU.add).then_inc(y_added, 1)

            def pair_pool(p, first, last):
                for i in range(2):
                    a, n = 2 * p + i, 2 * p - 1 + i
                    if not first:
                        make_dbu(n + 1, i, 0)
                    if not (last and i == 1):
                        pool.wait_ge(filled, PRE_UNITS + PAIR_UNITS * p + HALF_UNITS * i + 1)
                        pool.wait_ge(ld_wo, 16 * (a + 2))
                        split(wo_raw[:, :], wo_hi[1 - i][:, :], wo_lo[1 - i][:, :], wo_h, wo_s, a + 2)
                    if not first:
                        add_y(n, 0)
                    if not last:
                        pool.wait_ge(ld_wqk, 16 * (a + 3))
                        split(wqk_raw[:, :], wqk_hi[i][:, :], wqk_lo[i][:, :], wqk_h, wqk_s, a + 3)
                    if i == 0 and not last:
                        pool.wait_ge(ld_wv, 16 * (p + 2))
                        split(wv_raw[:, :], wv_hi[:, :], wv_lo[:, :], wv_h, wv_s, p + 2)
                    if first and i == 0:
                        for m in range(DM):
                            last_quad = squares[3][:, m, :]
                            pool.wait_ge(squared[m], 4)
                            pool.tensor_scalar(last_quad, last_quad, 1.0, LP * LP * LP_QUADS[3][1], ALU.mult, ALU.add)\
                                .then_inc(squared[m], 1)
                        for m in range(DM):
                            pool.wait_ge(squared[m], 5)
                            pool.wait_ge(quads[m], 3)
                            pool.tensor_tensor(dt[:, m, :], dt[:, m, :], squares[3][:, m, :], ALU.mult)\
                                .then_inc(quads[m], 1)
                        for m in range(DM):
                            pool.wait_ge(soft_pos, m + 1)
                            pool.wait_ge(quads[m], 4)
                            pool.tensor_tensor(dt[:, m, :], dt[:, m, :], soft_v[:, m].rearrange("p b s -> p (b s)"),
                                               ALU.add).then_inc(dt_done, 1)
                        for m in range(DM):
                            pool.wait_ge(dt_done, m + 1)
                            pool.tensor_tensor(dtu[:, m, :], dt[:, m, :], u[:, m, :], ALU.mult).then_inc(dtu_done, 1)
                            pool.wait_ge(dtu_done, m + 1)
                            make_dbu(0, 0, m)
                    elif first:
                        for m in range(DM):
                            make_dbu(1, 1, m)
                            add_y(0, m)
                    else:
                        make_dbu(n + 1, i, 1)
                        add_y(n, 1)

            pool.wait_ge(ld_rw, 16)
            split(rw_raw[:, :, :], rw_hi[:, :, :], rw_lo[:, :, :], rw_h, rw_s, 1)
            late_constants()
            pair_pool(0, True, False)
            with pool.Fori(1, PAIRS - 1) as p:
                pair_pool(p, False, False)
            pair_pool(PAIRS - 1, False, True)
            def norm_scale(n, g):
                t = slice(4 * g, 4 * g + 4)
                pool.wait_ge(ln_mv, NT * n + 4 * g + 4)
                pool.tensor_scalar(veps[:, t], mv[:, t, 1], 1.0, EPS, ALU.mult, ALU.add).then_inc(ln_eps, 1)
                pool.tensor_scalar(negmean[:, t], mv[:, t, 0], -1.0, 0.0, ALU.mult, ALU.add).then_inc(ln_eps, 1)
                pool.wait_ge(ln_eps, 4 * n + 2 * g + 2)
                pool.tensor_tensor(rstd[:, t], veps[:, t], mhalf[:, t], ALU.pow).then_inc(ln_rstd, 1)
                pool.wait_ge(ln_rstd, 2 * n + g + 1)
                pool.tensor_tensor(nbias[:, t], negmean[:, t], rstd[:, t], ALU.mult).then_inc(ln_bias, 1)

            def split_gate_up(j, i):
                pool.wait_ge(ld_f[i], 8 * j + 16 - 8 * i)
                split(f_raw[i][:, 0:4 * P], gu_hi[i][:, :], gu_lo[i][:, :], gu_h, gu_s, j + 1)

            def split_down(j, i):
                split(f_raw[i][:, 4 * P:], dn_hi[i][:, :], dn_lo[i][:, :], dn_h, dn_s, j + 1)

            def lo_h(j, i):
                for c in range(NC):
                    s = slice(c * CH, (c + 1) * CH)
                    pool.wait_ge(hhi_d, NC * j + c + 1)
                    pool.tensor_tensor(h_lo[i][:, s], hidw[:, s], h_hi[i][:, s].bitcast(F32), ALU.subtract)\
                        .then_inc(hlo_d, 1)

            for g in range(2):
                norm_scale(0, g)
            split_gate_up(0, 0)
            split_down(0, 0)
            for g in range(2):
                norm_scale(1, g)
            split_gate_up(1, 1)
            split_down(1, 1)
            lo_h(0, 0)
            with pool.Fori(0, HT // 2 - 1) as r:
                for i in range(2):
                    j = 2 * r + i
                    pool.wait_ge(up_f, NC * (j + 1))
                    split_gate_up(j + 2, i)
                    lo_h(j + 1, 1 - i)
                    pool.wait_ge(down_d, j + 1)
                    split_down(j + 2, i)
            lo_h(HT - 1, 1)
            for g in range(2):
                norm_scale(2, g)

        @block.scalar
        def _(act):
            def drain_in_proj(m):
                for c in range(NC):
                    g = NC * m + c
                    act.wait_ge(filled, g + 1)
                    act.activation(padded[:, m, 2 * c:2 * c + 2, TAPS - 1:],
                                   bank(g).rearrange("p (b s) -> p b s", s=SEQ), ACT.Copy).then_inc(pre_read, 1)

            drain_in_proj(0)
            act.wait_ge(ld_x, 16)
            for k in range(DK):
                act.activation(xT_hi[:, k, :], stage[:, k, :], ACT.Copy).then_inc(x_hi_s, 1)
            drain_in_proj(1)

            def hi(dst, g, n_units, scale=1.0, cols=CH):
                act.wait_ge(filled, n_units)
                act.activation(dst, bank(g)[:, 0:cols], ACT.Copy, scale=scale).then_inc(hi_done, 1)

            def hi_qk(dst, g, n, c, scale):
                hi(dst[:, c * CH:(c + 1) * CH], g, n + 1, scale)

            def silu_u(m):
                act.wait_ge(conv_taps[m], TAPS)
                act.activation(u[:, m, :], conv[m], ACT.Silu, bias=chan[:, m, TAPS:TAPS + 1]).then_inc(u_done, 1)

            act.wait_ge(pad_zero, 1)
            act.wait_ge(pre_read, NC * DM)
            for k in range(1, TAPS):
                act.activation(prod[k], padded[:, 1, :, k:k + SEQ], ACT.Copy, scale=chan[:, 1, k:k + 1])\
                   .then_inc(tap_prod, 1)
            for c in range(NC):
                hi_qk(q_hi, 4 + c, 4 + c, c, QSCALE)
            for c in range(NC):
                hi_qk(k_hi, 6 + c, 6 + c, c, 1.0)
            silu_u(0)
            for t in range(4):
                hi(v_hi[:, 2 * t:2 * t + 2, :].rearrange("p t e -> p (t e)"), 8 + t, 9 + t)
                if t == 0:
                    silu_u(1)
            def exps(n):
                for b in range(BATCH):
                    act.wait_ge(bank_read, n + b + 1)
                    act.activation(prob[:, b, 0:P], prob[:, b, 0:P], ACT.Exp, bias=smin[:, b, 0:1], scale=-1.0,
                                   accum_out=ssum[:, b, 0:1]).then_inc(exp_done, 1)
                    act.activation(prob[:, b, P:], prob[:, b, P:], ACT.Exp, bias=smin[:, b, 1:2], scale=-1.0,
                                   accum_out=ssum[:, b, 1:2]).then_inc(exp_done, 1)

            def make_da(n, m):
                act.wait_ge(scanned, 2 * n + m + 1)
                act.activation(da[:, m, :, 1:], dt[:, m, :].rearrange("p (b s) -> p b s", s=SEQ)[:, :, 1:],
                               ACT.Exp, scale=a_neg[:, m, bass.ds(n, 1)]).then_inc(da_done, 1)

            for c in range(NC):
                act.wait_ge(filled, 13 + c)
                act.activation(xdbl[:, c * CH:(c + 1) * CH], bank(12 + c)[0:XDBL, :], ACT.Copy).then_inc(pre_read, 1)
            exps(8)
            act.activation(a_neg[:, :, :], chan[:, :, TAPS + 3:], ACT.Exp).then_inc(a_exp, 1)
            for m in range(DM):
                for c in range(NC):
                    g = 18 + NC * m + c
                    act.wait_ge(filled, g + 1)
                    act.activation(soft_v[:, m, 2 * c:2 * c + 2, :].rearrange("p b s -> p (b s)"), bank(g),
                                   ACT.Identity, bias=chan[:, m, TAPS + 1:TAPS + 2]).then_inc(pre_read, 1)
            for m in range(DM):
                act.wait_ge(soft_abs, m + 1)
                act.activation(soft_e[:, m, :], soft_e[:, m, :], ACT.Exp, scale=-1.0).then_inc(soft_x, 1)

            def soft_square(k):
                for m in range(DM):
                    act.wait_ge(soft_x, m + 1)
                    if k == 3:
                        act.wait_ge(quads[m], 1)
                    act.activation(squares[k][:, m, :], soft_e[:, m, :], ACT.Square, scale=LP,
                                   bias=lp_bias[:, k:k + 1]).then_inc(squared[m], 1)

            def pair_act(p, first, last):
                for i in range(2):
                    base = PRE_UNITS + PAIR_UNITS * p + HALF_UNITS * i
                    gb = PRE_UNITS + HALF_UNITS * i
                    n = 2 * p - 1 + i
                    nxt = not (last and i == 1)
                    if last and i == 1:
                        pt, z = P_U - 2, Z_U - 4
                    else:
                        pt, z = P_U, Z_U
                    if nxt:
                        for c in range(NC):
                            hi_qk(q_hi, gb + Q_U + c, base + Q_U + c, c, QSCALE)
                    if first and i == 0:
                        act.wait_ge(lp_const, len(LP_QUADS))
                        soft_square(0)
                    for b in range(BATCH):
                        hi(pT_hi[:, b, :], gb + pt + b, base + pt + b + 1, cols=3 * P)
                    if first and i == 0:
                        soft_square(1)
                    elif first:
                        act.wait_ge(a_done, 1)
                        act.wait_ge(dt_done, 2)
                        make_da(0, 0)
                    else:
                        make_da(n, 1)
                    if nxt:
                        for c in range(NC):
                            hi_qk(k_hi, gb + K_U + c, base + K_U + c, c, 1.0)
                    if first and i == 0:
                        soft_square(2)
                        soft_square(3)
                    if not first:
                        make_da(n + 1, 0)
                    elif i == 1:
                        make_da(0, 1)
                    for c in range(NC):
                        hi_qk(z_hi, gb + z + c, base + z + c, c, 1.0)
                    if first and i == 0:
                        for m in range(DM):
                            v = soft_v[:, m].rearrange("p b s -> p (b s)")
                            act.wait_ge(soft_abs, m + 1)
                            act.activation(v, v, ACT.Relu).then_inc(soft_pos, 1)
                    if nxt:
                        exps(PRE_ATTN + PAIR_UNITS * p + HALF_UNITS * i + S_U)
                    if first and i == 1:
                        make_da(1, 0)
                if not last:
                    for t in range(4):
                        hi(v_hi[:, 2 * t:2 * t + 2, :].rearrange("p t e -> p (t e)"),
                           PRE_UNITS + V_U + t, PRE_UNITS + PAIR_UNITS * p + V_U + t + 1)

            pair_act(0, True, False)
            with act.Fori(1, PAIRS - 1) as p:
                pair_act(p, False, False)
            pair_act(PAIRS - 1, False, True)
            make_da(STATES - 1, 1)

            def normed(n, t, src, dst, func, done):
                act.wait_ge(ln_bias, 2 * n + t // 4 + 1)
                act.activation(dst, src[:, t, :], func, scale=rstd[:, t:t + 1], bias=nbias[:, t:t + 1])\
                   .then_inc(done, 1)

            act.wait_ge(scanned, 2 + 2 * STATES)
            for t in range(NT):
                normed(0, t, acc_t, silu_x1(t), ACT.Silu, silu_z)
            for t in range(NT):
                normed(0, t, acc_t, x_res[:, t, :], ACT.Identity, x1_done)
            for t in (4, 5):
                normed(1, t, pre, x_res[:, t, :], ACT.Identity, x2_a)
            for n in range(NC * DK):
                act.wait_ge(x2_turned, n + 1)
                act.activation(xT_hi[:, n % DK, (n // DK) * CH:(n // DK + 1) * CH], bank(n), ACT.Copy)\
                   .then_inc(x2_hi, 1)
            for c in range(NC):
                act.wait_ge(logit_t, c + 1)
                act.activation(logit_sb[:, c * CH:(c + 1) * CH], acc[0:NR, c * CH:(c + 1) * CH], ACT.Copy)\
                   .then_inc(logit_read, 1)
            act.wait_ge(route, 2)
            act.activation(probs[:, :, 0:EXPERTS], lsub[:, :, :], ACT.Exp).then_inc(route_e, 1)
            act.activation(gate[:, :], gate[:, :], ACT.Exp).then_inc(route_e, 1)

            def silu_gate(j, g0, first):
                for c in range(NC):
                    s = slice(c * CH, (c + 1) * CH)
                    act.wait_ge(gate_f, NC * j + c + 1)
                    if not first:
                        act.wait_ge(hid_d, NC * (j - 1) + c + 1)
                    act.activation(silu_g[:, s], bank(g0 + 3 * c), ACT.Silu).then_inc(silu_d, 1)

            def hi_h(j, i):
                for c in range(NC):
                    s = slice(c * CH, (c + 1) * CH)
                    act.wait_ge(hidw_d, NC * j + c + 1)
                    act.activation(h_hi[i][:, s], hidw[:, s], ACT.Copy).then_inc(hhi_d, 1)

            silu_gate(0, 2, True)
            act.wait_ge(wt_turned, 1)
            act.activation(wT[:, :], acc[0:NSEL, 3 * CH:].bitcast(BF16), ACT.Copy).then_inc(wt_done, 1)
            hi_h(0, 0)
            with act.Fori(0, HT // 2 - 1) as r:
                silu_gate(2 * r + 1, 2 + 6, False)
                hi_h(2 * r + 1, 1)
                silu_gate(2 * r + 2, 2, False)
                hi_h(2 * r + 2, 0)
            silu_gate(HT - 1, 2 + 6, False)
            hi_h(HT - 1, 1)
            for t in range(4):
                normed(2, t, acc_t, pre[:, t, :], ACT.Identity, out_first)

        @block.vector
        def _(dve):
            def tap(k):
                src, weight = padded[:, 0, :, k:k + SEQ], chan[:, 0, k:k + 1]
                dst = conv[0].rearrange("p (b s) -> p b s", s=SEQ)
                if k == 0:
                    dve.tensor_scalar(dst, src, weight, None, ALU.mult).then_inc(conv_taps[0], 1)
                else:
                    dve.wait_ge(conv_taps[0], k)
                    dve.scalar_tensor_tensor(out=dst, in0=src, scalar=weight, in1=dst, op0=ALU.mult, op1=ALU.add)\
                       .then_inc(conv_taps[0], 1)

            dve.wait_ge(ld_chan, 16)
            dve.wait_ge(pre_read, NC)
            dve.wait_ge(pad_zero, 1)
            tap(0)
            dve.wait_ge(ld_x, 16)
            for k in range(DK):
                dve.wait_ge(x_hi_s, k + 1)
                dve.tensor_tensor(xT_lo[:, k, :], stage[:, k, :], xT_hi[:, k, :].bitcast(F32), ALU.subtract)\
                   .then_inc(x_lo_s, 1)
            for k in range(1, TAPS):
                tap(k)

            def lo(dst, hi_part, g, n_hi, scale=None, cols=CH):
                dve.wait_ge(hi_done, n_hi)
                if scale is None:
                    dve.tensor_tensor(dst, bank(g)[:, 0:cols], hi_part.bitcast(F32), ALU.subtract).then_inc(bank_read, 1)
                else:
                    dve.scalar_tensor_tensor(out=dst, in0=bank(g)[:, 0:cols], scalar=scale, in1=hi_part.bitcast(F32),
                                             op0=ALU.mult, op1=ALU.subtract).then_inc(bank_read, 1)

            def lo_qk(dst, src, g, n, c, scale=None):
                s = slice(c * CH, (c + 1) * CH)
                lo(dst[:, s], src[:, s], g, n + 1, scale)

            def lo_v(t, g, n):
                lo(v_lo[:, 2 * t:2 * t + 2, :].rearrange("p t e -> p (t e)"),
                   v_hi[:, 2 * t:2 * t + 2, :].rearrange("p t e -> p (t e)"), g, n + 1)

            for c in range(NC):
                lo_qk(q_lo, q_hi, 4 + c, c, c, QSCALE)
            for c in range(NC):
                lo_qk(k_lo, k_hi, 6 + c, 2 + c, c)
            for t in range(4):
                lo_v(t, 8 + t, 4 + t)

            def softplus_quad(k):
                for m in range(DM):
                    dve.wait_ge(squared[m], k + 1)
                    if k:
                        dve.wait_ge(quads[m], k)
                    dve.scalar_tensor_tensor(out=dt[:, m, :], in0=squares[k][:, m, :], scalar=LP * LP * LP_QUADS[k][1],
                                             in1=dt[:, m, :] if k else soft_e[:, m, :], op0=ALU.add, op1=ALU.mult)\
                       .then_inc(quads[m], 1)

            def mask_scores(b, g, n_units):
                dve.wait_ge(filled, n_units)
                dve.nop(nofuse=True)
                dve.tensor_tensor_reduce(prob[:, b, 0:P], bank(g)[:, 0:P], mask[:, P:], 1.0, 3.0e38, ALU.add, ALU.min,
                                         smin[:, b, 0:1])
                dve.tensor_tensor_reduce(prob[:, b, P:], bank(g)[:, P:3 * P], mask[:, :], 1.0, 3.0e38, ALU.add, ALU.min,
                                         smin[:, b, 1:2]).then_inc(bank_read, 1)

            def normalise(n):
                for b in range(BATCH):
                    dve.wait_ge(exp_done, 8 * n + 2 * b + 2)
                    dve.reciprocal(sinv[:, b, :], ssum[:, b, :]).then_inc(inv_done, 1)
                for b in range(BATCH):
                    dve.wait_ge(inv_done, BATCH * n + b + 1)
                    dve.tensor_scalar(prob[:, b, 0:P], prob[:, b, 0:P], sinv[:, b, 0:1], None, ALU.mult)\
                       .then_inc(probs_ready, 1)
                    dve.tensor_scalar(prob[:, b, P:], prob[:, b, P:], sinv[:, b, 1:2], None, ALU.mult)\
                       .then_inc(probs_ready, 1)

            def scan(n, m):
                dve.wait_ge(da_done, 2 * n + m + 1)
                dve.wait_ge(dbu_done, 2 * n + m + 1)
                dve.wait_ge(y_added, 2 * n + m + 1)
                dve.tensor_tensor_scan(state[:, m, :], da[:, m].rearrange("p b s -> p (b s)"), dbu[:, m, :], 0.0,
                                       ALU.mult, ALU.add).then_inc(scanned, 1)

            def times_c(n, i, m):
                dve.wait_ge(scanned, 2 * n + m + 3)
                dve.wait_ge(bc_load[i], 16 * (n - i) + 32)
                dve.tensor_tensor(state[:, m, :], state[:, m, :], c_all[:, i, :], ALU.mult).then_inc(cmul, 1)

            dve.wait_ge(ld_xres, 16)
            dve.wait_ge(acc_open, 1)
            dve.tensor_copy(acc[:, :], x_res[:, :, :].rearrange("p t d -> p (t d)")).then_inc(acc_set, 1)
            dve.wait_ge(consts, 4)
            for b in range(BATCH):
                mask_scores(b, 14 + b, 15 + b)
            dve.wait_ge(a_exp, 1)
            dve.tensor_scalar(a_neg[:, :, :], a_neg[:, :, :], -1.0, None, ALU.mult).then_inc(a_done, 1)
            normalise(0)
            for m in range(DM):
                v = soft_v[:, m].rearrange("p b s -> p (b s)")
                dve.wait_ge(pre_read, 8 + 2 * m)
                dve.scalar_tensor_tensor(out=soft_e[:, m, :], in0=v, scalar=-1.0, in1=v, op0=ALU.mult,
                                         op1=ALU.max).then_inc(soft_abs, 1)

            def pair_dve(p, first, last):
                for i in range(2):
                    base = PRE_UNITS + PAIR_UNITS * p + HALF_UNITS * i
                    hbase = PRE_HI + PAIR_HI * p + HALF_HI * i
                    gb = PRE_UNITS + HALF_UNITS * i
                    n = 2 * p - 1 + i
                    nxt = not (last and i == 1)
                    pt, z, hp, hz = (P_U, Z_U, 2, 8) if nxt else (P_U - 2, Z_U - 4, 0, 4)
                    if nxt:
                        for c in range(NC):
                            lo_qk(q_lo, q_hi, gb + Q_U + c, hbase + c, c, QSCALE)
                    if first and i == 0:
                        softplus_quad(0)
                    for b in range(BATCH):
                        lo(pT_lo[:, b, :], pT_hi[:, b, :], gb + pt + b, hbase + hp + b + 1, cols=3 * P)
                    if first and i == 0:
                        softplus_quad(1)
                    elif first:
                        dve.wait_ge(dt_done, 2)
                        dve.memset(da[:, :, :, 0:1], 0.0).then_inc(scanned, 2)
                    elif i == 1:
                        times_c(n, 0, 0)
                    if nxt:
                        for c in range(NC):
                            lo_qk(k_lo, k_hi, gb + K_U + c, hbase + 6 + c, c)
                    if first and i == 0:
                        softplus_quad(2)
                    elif first:
                        scan(0, 0)
                    else:
                        scan(n, 1)
                    for c in range(NC):
                        lo_qk(z_lo, z_hi, gb + z + c, hbase + hz + c, c)
                    if first and i == 1:
                        times_c(0, 0, 0)
                        scan(0, 1)
                    if nxt:
                        for b in range(BATCH):
                            mask_scores(b, gb + S_U + b, base + S_U + b + 1)
                    if not first:
                        times_c(n, 1 - i, 1)
                        scan(n + 1, 0)
                        if i == 1:
                            times_c(n + 1, i, 0)
                    if first and i == 1:
                        times_c(0, 0, 1)
                    if nxt:
                        normalise(2 * p + i + 1)
                if not last:
                    for t in range(4):
                        lo_v(t, PRE_UNITS + V_U + t, PRE_HI + PAIR_HI * p + 20 + t)
                if first:
                    scan(1, 0)
                    times_c(1, 1, 0)

            pair_dve(0, True, False)
            with dve.Fori(1, PAIRS - 1) as p:
                pair_dve(p, False, False)
            pair_dve(PAIRS - 1, False, True)

            def moments(n, g, src, add=None):
                for t in range(4 * g, 4 * g + 6):
                    if add and t < 4 * g + 4:
                        add(t).then_inc(ln_in, 1)
                    if 4 * g + 1 <= t <= 4 * g + 4:
                        if add:
                            dve.wait_ge(ln_in, t)
                        elif n == 0:
                            dve.wait_ge(out_proj, (t - 1) // 2 * 2 + 2)
                        else:
                            dve.wait_ge(down_d, HT - 1 + (t - 1) // 2 * 2 + 2)
                        dve.bn_stats(stats[:, t - 1, :], src[:, t - 1, :]).then_inc(ln_stat, 1)
                    if t >= 4 * g + 2:
                        dve.wait_ge(ln_stat, NT * n + t - 1)
                        dve.bn_aggr(mv[:, t - 2, :], stats[:, t - 2, :]).then_inc(ln_mv, 1)

            def normed(n, t, src, dst, done):
                dve.wait_ge(ln_rstd, 2 * n + t // 4 + 1)
                dve.tensor_scalar(dst[:, t, :], src[:, t, :], mv[:, t, 0:1], rstd[:, t:t + 1],
                                  ALU.subtract, ALU.mult).then_inc(done, 1)

            for g in range(2):
                moments(0, g, acc_t)
            scan(STATES - 1, 1)
            times_c(STATES - 1, 1, 1)
            for m in range(DM):
                dve.wait_ge(cmul, 2 * STATES - 1 + m)
                dve.wait_ge(y_added, 2 * STATES - 1 + m)
                dve.tensor_tensor(y[:, m, :], y[:, m, :], state[:, m, :], ALU.add).then_inc(y_added, 1)
            dve.wait_ge(y_added, 2 + 2 * STATES)
            for t in range(NT):
                b, m = t // DM, t % DM
                dve.wait_ge(silu_z, t + 1)
                dve.tensor_tensor(y[:, m, b * SEQ:(b + 1) * SEQ], y[:, m, b * SEQ:(b + 1) * SEQ], silu_x1(t),
                                  ALU.mult).then_inc(gated, 1)

            def add_scan(t):
                dve.wait_ge(x1_done, t + 1)
                dve.wait_ge(turned, t // 2 * 2 + 2)
                return dve.tensor_tensor(pre[:, t, :], bank(t // 2)[:, (t % 2) * D:(t % 2 + 1) * D], x_res[:, t, :],
                                         ALU.add)

            for g in range(2):
                moments(1, g, pre, add_scan)
            for t in (0, 1, 2, 3, 6, 7):
                normed(1, t, pre, x_res, x2_v)
            for n in range(NC * DK):
                dve.wait_ge(x2_hi, n + 1)
                s = slice((n // DK) * CH, (n // DK + 1) * CH)
                dve.tensor_tensor(xT_lo[:, n % DK, s], bank(n), xT_hi[:, n % DK, s].bitcast(F32), ALU.subtract)\
                   .then_inc(x2_lo, 1)

            dve.wait_ge(logit, 1)
            dve.wait_ge(consts, 8)
            logits = acc[:, 2 * CH:2 * CH + NT * NR].rearrange("p (t e) -> p t e", e=NR)
            dve.tensor_reduce(lmax[:, :], logits[:, :, 0:EXPERTS], AX.X, ALU.max).then_inc(route_v, 1)
            dve.tensor_scalar(gate[:, :], logits[:, :, EXPERTS], -1.0, 80.0, ALU.mult, ALU.min).then_inc(route, 1)
            dve.wait_ge(route_v, 1)
            dve.tensor_tensor(lsub[:, :, :], logits[:, :, 0:EXPERTS],
                              lmax[:, :].unsqueeze(2).to_broadcast([P, NT, EXPERTS]), ALU.subtract).then_inc(route, 1)
            dve.wait_ge(route_e, 2)
            dve.tensor_reduce(lsum[:, :], probs[:, :, 0:EXPERTS], AX.X, ALU.add).then_inc(route_v, 1)
            dve.tensor_scalar(gate[:, :], gate[:, :], 1.0, None, ALU.add).then_inc(route, 1)
            dve.wait_ge(route_v, 2)
            dve.reciprocal(linv[:, :], lsum[:, :]).then_inc(route_v, 1)
            dve.wait_ge(route, 3)
            for g in range(EXPERTS, GROUPS):
                dve.reciprocal(wr[:, :, g], gate[:, :]).then_inc(route, 1)
            dve.wait_ge(route_v, 3)
            dve.tensor_tensor(probs[:, :, 0:EXPERTS], probs[:, :, 0:EXPERTS],
                              linv[:, :].unsqueeze(2).to_broadcast([P, NT, EXPERTS]), ALU.mult).then_inc(route_v, 1)
            dve.wait_ge(route_v, 4)
            for t in range(NT):
                dve.max(top[:, t, :], probs[:, t, 0:EXPERTS]).then_inc(route_v, 1)
            dve.wait_ge(route_v, 4 + NT)
            dve.memset(top[:, :, TOPK:], -1.0).then_inc(route_v, 1)
            dve.wait_ge(route_v, 5 + NT)
            for t in range(NT):
                dve.match_replace(picked[:, t, :], top[:, t, :], probs[:, t, :], -2.0).then_inc(route_v, 1)
            dve.wait_ge(route_v, 5 + 2 * NT)
            dve.scalar_tensor_tensor(out=wr[:, :, 0:EXPERTS], in0=picked[:, :, 0:EXPERTS], scalar=-2.0,
                                     in1=probs[:, :, 0:EXPERTS], op0=ALU.is_equal, op1=ALU.mult).then_inc(route, 1)
            s0 = 5 + 2 * NT
            dve.wait_ge(route, 3 + (GROUPS - EXPERTS) + 1)
            for part in range(3):
                dst = wpart[:, :, 32 * part:32 * part + GROUPS]
                dve.tensor_copy(dst, wr[:, :, :]).then_inc(route_v, 1)
                s0 += 1
                dve.wait_ge(route_v, s0)
                if part < 2:
                    dve.tensor_tensor(wr[:, :, :], wr[:, :, :], dst, ALU.subtract).then_inc(route_v, 1)
                    s0 += 1
                    dve.wait_ge(route_v, s0)

            def mlp_dve(j, g0, first):
                for c in range(NC):
                    s = slice(c * CH, (c + 1) * CH)
                    dve.wait_ge(silu_d, NC * j + c + 1)
                    dve.wait_ge(up_f, NC * j + c + 1)
                    if not first:
                        dve.wait_ge(hidw_d, NC * (j - 1) + c + 1)
                    dve.tensor_tensor(hid[:, s], silu_g[:, s], bank(g0 + 3 * c + 1), ALU.mult).then_inc(hid_d, 1)
                    dve.wait_ge(hid_d, NC * j + c + 1)
                    dve.wait_ge(wb_f, NC * j + c + 1)
                    if not first:
                        dve.wait_ge(hlo_d, NC * (j - 1) + c + 1)
                    dve.tensor_tensor(hidw[:, s], hid[:, s], bank(g0 + 3 * c + 2), ALU.mult).then_inc(hidw_d, 1)

            mlp_dve(0, 2, True)
            dve.wait_ge(acc_open, 2)
            dve.tensor_copy(acc[:, :], x_res[:, :, :].rearrange("p t d -> p (t d)")).then_inc(acc_set, 1)
            with dve.Fori(0, HT // 2 - 1) as r:
                mlp_dve(2 * r + 1, 2 + 6, False)
                mlp_dve(2 * r + 2, 2, False)
            mlp_dve(HT - 1, 2 + 6, False)

            for g in range(2):
                moments(2, g, acc_t)
            for t in range(4, NT):
                normed(2, t, acc_t, pre, out_second)

        @block.tensor
        def _(pe):
            def split_mm(dst, pairs, start=True):
                last = len(pairs) - 1
                for n, (lhs, rhs) in enumerate(pairs):
                    pe.matmul(dst, lhs[0], rhs[0], start=start and n == 0, stop=False, skip_group_check=True)
                    pe.matmul(dst, lhs[0], rhs[1], start=False, stop=False, skip_group_check=True)
                    mm = pe.matmul(dst, lhs[1], rhs[0], start=False, stop=n == last, skip_group_check=True)
                return mm

            def open_acc():
                for n in range(4 * NC * DK):
                    mm = pe.matmul(acc[:, n * P:(n + 1) * P], ident_b[:, :], ident_b[:, :], start=n % 4 == 0,
                                   stop=n % 4 == 3, skip_group_check=True)
                mm.then_inc(acc_open, 1)

            pe.wait_ge(consts, 5)
            open_acc()
            pe.wait_ge(ld_ctx, 32)
            for m in range(DM):
                for c in range(NC):
                    pe.matmul(bank(NC * m + c), inw[:, m * P:(m + 1) * P], ctxT[:, c * CH:(c + 1) * CH],
                              start=True, stop=True).then_inc(filled, 1)

            def proj(g, i, which, c):
                s = slice(c * CH, (c + 1) * CH)
                split_mm(bank(g), [((wqk_hi[i][:, (which * DK + k) * P:(which * DK + k + 1) * P],
                                     wqk_lo[i][:, (which * DK + k) * P:(which * DK + k + 1) * P]),
                                    (xT_hi[:, k, s], xT_lo[:, k, s])) for k in range(DK)]).then_inc(filled, 1)

            def values(g, t2):
                for j in range(2):
                    tok = slice((2 * t2 + j) * P, (2 * t2 + j + 1) * P)
                    mm = split_mm(bank(g)[:, j * 2 * HD:(j + 1) * 2 * HD],
                                  [((xT_hi[:, k, tok], xT_lo[:, k, tok]),
                                    (wv_hi[:, k * 2 * HD:(k + 1) * 2 * HD], wv_lo[:, k * 2 * HD:(k + 1) * 2 * HD]))
                                   for k in range(DK)], start=j == 0)
                mm.then_inc(filled, 1)

            def scores(g, b):
                for t in range(2):
                    qs = slice(b * SEQ + t * P, b * SEQ + (t + 1) * P)
                    ks = slice(b * SEQ, b * SEQ + (t + 1) * P)
                    dst = bank(g)[:, 0:P] if t == 0 else bank(g)[:, P:3 * P]
                    mm = split_mm(dst, [((q_hi[:, qs], q_lo[:, qs]), (k_hi[:, ks], k_lo[:, ks]))], start=t == 0)
                mm.then_inc(filled, 1)

            def turn_probs(g, b):
                for t in range(3):
                    mm = pe.transpose(bank(g)[:, t * P:(t + 1) * P], prob[:, b, t * P:(t + 1) * P], ident[:, :])
                mm.then_inc(filled, 1)

            def context(g, i, c):
                for j in range(2):
                    b = 2 * c + j
                    e = slice(i * HD, (i + 1) * HD)
                    split_mm(bank(g)[:, j * SEQ:(j + 1) * SEQ],
                             [((v_hi[:, 2 * b, e], v_lo[:, 2 * b, e]),
                               (pT_hi[:, b, 0:2 * P], pT_lo[:, b, 0:2 * P]))], start=j == 0)
                    mm = split_mm(bank(g)[:, j * SEQ + P:(j + 1) * SEQ],
                                  [((v_hi[:, 2 * b + 1, e], v_lo[:, 2 * b + 1, e]),
                                    (pT_hi[:, b, 2 * P:], pT_lo[:, b, 2 * P:]))], start=False)
                mm.then_inc(filled, 1)

            def out_projection(i, signal):
                for t in range(NT):
                    s = slice(t * P, (t + 1) * P)
                    mm = split_mm(acc_t[:, t, :], [((z_hi[:, s], z_lo[:, s]), (wo_hi[i][:, :], wo_lo[i][:, :]))],
                                  start=False)
                    if signal:
                        mm.then_inc(out_proj, 1)

            pe.wait_ge(x_lo_s, DK)
            pe.wait_ge(wqk_s, 1)
            for c in range(NC):
                pe.wait_ge(pre_read, 1 + c)
                proj(4 + c, 0, 0, c)
            for c in range(NC):
                pe.wait_ge(pre_read, 3 + c)
                proj(6 + c, 0, 1, c)
            pe.wait_ge(wv_s, 1)
            for t in range(4):
                pe.wait_ge(bank_read, 1 + t)
                values(8 + t, t)
            pe.wait_ge(u_done, 2)
            pe.wait_ge(ld_xw, 32)
            for c in range(NC):
                pe.wait_ge(bank_read, 5 + c)
                for m in range(DM):
                    mm = pe.matmul(bank(12 + c)[0:XDBL, :], xw[:, m, :], u[:, m, c * CH:(c + 1) * CH],
                                   start=m == 0, stop=m == DM - 1)
                mm.then_inc(filled, 1)
            pe.wait_ge(bank_read, 8)
            for b in range(BATCH):
                if b >= 2:
                    pe.wait_ge(pre_read, 3 + b)
                scores(14 + b, b)
            pe.wait_ge(pre_read, 6)
            for m in range(DM):
                for c in range(NC):
                    pe.wait_ge(bank_read, 9 + NC * m + c)
                    pe.matmul(bank(18 + NC * m + c), dtw[:, m * P:(m + 1) * P], xdbl[0:RANK, c * CH:(c + 1) * CH],
                              start=True, stop=True).then_inc(filled, 1)

            def pair_pe(p, first, last):
                for i in range(2):
                    a = 2 * p + i
                    gb = PRE_UNITS + HALF_UNITS * i
                    before = PRE_ATTN + PAIR_UNITS * p + HALF_UNITS * i - 3
                    nxt = not (last and i == 1)
                    pt, z = (P_U, Z_U) if nxt else (P_U - 2, Z_U - 4)
                    if nxt:
                        pe.wait_ge(wqk_s, a + 2)
                        for c in range(NC):
                            if first and i == 0:
                                pe.wait_ge(pre_read, 7 + c)
                            pe.wait_ge(bank_read, before + Q_U + c)
                            proj(gb + Q_U + c, 1 - i, 0, c)
                    for b in range(BATCH):
                        if first and i == 0 and b < 2:
                            pe.wait_ge(pre_read, 9 + b)
                        pe.wait_ge(bank_read, before + pt + b)
                        pe.wait_ge(probs_ready, 8 * a + 2 * b + 2)
                        turn_probs(gb + pt + b, b)
                    if nxt:
                        for c in range(NC):
                            pe.wait_ge(bank_read, before + K_U + c)
                            proj(gb + K_U + c, 1 - i, 1, c)
                    for c in range(NC):
                        pe.wait_ge(bank_read, before + z + c if nxt else before + pt + 2 * c + 5)
                        context(gb + z + c, i, c)
                    if nxt:
                        for b in range(BATCH):
                            pe.wait_ge(bank_read, before + S_U + b)
                            scores(gb + S_U + b, b)
                    else:
                        pe.wait_ge(bank_read, before + z + 5)
                    if first and i == 0:
                        pe.wait_ge(acc_set, 1)
                    pe.wait_ge(wo_s, a + 1)
                    out_projection(i, last and i == 1)
                if not last:
                    pe.wait_ge(wv_s, p + 2)
                    for t in range(4):
                        pe.wait_ge(bank_read, PRE_ATTN + PAIR_UNITS * p + V_U + t - 3)
                        values(PRE_UNITS + V_U + t, t)

            pair_pe(0, True, False)
            with pe.Fori(1, PAIRS - 1) as p:
                pair_pe(p, False, False)
            pair_pe(PAIRS - 1, False, True)

            total_attn = PRE_ATTN + PAIR_UNITS * (PAIRS - 1) + 2 * HALF_UNITS - 8
            pe.wait_ge(bank_read, total_attn)
            for t in range(NT):
                b, l = t // 2, t % 2
                pe.wait_ge(gated, DM * b + DM)
                for m in range(DM):
                    mm = pe.transpose(bank(t // 2)[:, (t % 2) * D + m * P:(t % 2) * D + (m + 1) * P],
                                      y[:, m, b * SEQ + l * P:b * SEQ + (l + 1) * P], ident[:, :])
                mm.then_inc(turned, 1)
            pe.wait_ge(ln_in, NT)
            for n in range(NC * DK):
                k, c = n % DK, n // DK
                for j in range(4):
                    if k == 0:
                        if c == 1 and j < 2:
                            pe.wait_ge(x2_a, j + 1)
                        else:
                            pe.wait_ge(x2_v, 2 * c + j + 1)
                    mm = pe.transpose(bank(n)[:, j * P:(j + 1) * P], x_res[:, 4 * c + j, k * P:(k + 1) * P],
                                      ident[:, :])
                mm.then_inc(x2_turned, 1)
            pe.wait_ge(rw_s, 1)
            for c in range(NC):
                pe.wait_ge(x2_lo, DK * (c + 1))
                s = slice(c * CH, (c + 1) * CH)
                split_mm(acc[0:NR, s], [((rw_hi[:, k, :], rw_lo[:, k, :]), (xT_hi[:, k, s], xT_lo[:, k, s]))
                                        for k in range(DK)]).then_inc(logit_t, 1)
            for t in range(NT):
                if t % 4 == 0:
                    pe.wait_ge(logit_read, t // 4 + 1)
                mm = pe.transpose(acc[:, 2 * CH + t * NR:2 * CH + (t + 1) * NR], logit_sb[:, t * P:(t + 1) * P],
                                  ident[0:NR, 0:NR])
            mm.then_inc(logit, 1)

            def turn_weights():
                pe.wait_ge(route_v, 5 + 2 * NT + 5)
                for t in range(NT):
                    mm = pe.transpose(acc[0:NSEL, 3 * CH + t * P // 2:3 * CH + (t + 1) * P // 2].bitcast(BF16),
                                      wpart[:, t, :], ident_b[:, :])
                mm.then_inc(wt_turned, 1)
                pe.wait_ge(ld_sel, 32)
                pe.wait_ge(wt_done, 1)

            def gate_up(j, i, g0, first):
                pe.wait_ge(gu_s, j + 1)
                for c in range(NC):
                    s = slice(c * CH, (c + 1) * CH)
                    for which, done in ((0, gate_f), (1, up_f)):
                        if which == 0 and not first:
                            pe.wait_ge(hidw_d, NC * (j - 1) + c + 1)
                        if which == 1 and c == 0 and not first:
                            pe.wait_ge(silu_d, NC * (j - 1) + 2)
                        if which == 1 and c == 1:
                            pe.wait_ge(silu_d, NC * j + 1)
                        split_mm(bank(g0 + 3 * c + which),
                                 [((gu_hi[i][:, (2 * which + k) * P:(2 * which + k + 1) * P],
                                    gu_lo[i][:, (2 * which + k) * P:(2 * which + k + 1) * P]),
                                   (xT_hi[:, k, s], xT_lo[:, k, s])) for k in range(DK)]).then_inc(done, 1)
                    if not first:
                        spread(j, g0, c, False)
                if first:
                    turn_weights()
                    for c in range(NC):
                        spread(j, g0, c, True)

            def spread(j, g0, c, first):
                if c == 0 and not first:
                    pe.wait_ge(hid_d, NC * (j - 1) + 2)
                if c == 1:
                    pe.wait_ge(hid_d, NC * j + 1)
                pe.matmul(bank(g0 + 3 * c + 2), sel[:, bass.ds(j * P, P)], wT[:, c * CH:(c + 1) * CH],
                          start=True, stop=True).then_inc(wb_f, 1)

            def down(j, i, signal_tiles):
                pe.wait_ge(dn_s, j + 1)
                for t in range(NT):
                    if t % 4 == 0:
                        pe.wait_ge(hlo_d, NC * j + t // 4 + 1)
                    s = slice(t * P, (t + 1) * P)
                    mm = split_mm(acc_t[:, t, :], [((h_hi[i][:, s], h_lo[i][:, s]),
                                                    (dn_hi[i][:, :], dn_lo[i][:, :]))], start=False)
                    if signal_tiles:
                        mm.then_inc(down_d, 1)
                if not signal_tiles:
                    mm.then_inc(down_d, 1)

            gate_up(0, 0, 2, True)
            open_acc()
            gate_up(1, 1, 2 + 6, False)
            pe.wait_ge(acc_set, 2)
            with pe.Fori(0, HT // 2 - 1) as r:
                down(2 * r, 0, False)
                gate_up(2 * r + 2, 0, 2, False)
                down(2 * r + 1, 1, False)
                gate_up(2 * r + 3, 1, 2 + 6, False)
            down(HT - 2, 0, False)
            down(HT - 1, 1, True)


def kernel(x, ctx_1024, L0_attn_W_Q, L0_attn_W_K, L0_attn_W_V, L0_attn_W_O, L0_xattn_in_proj_w, L0_xattn_conv_w,
           L0_xattn_conv_b, L0_xattn_x_proj_w, L0_xattn_dt_proj_w, L0_xattn_dt_proj_b, L0_xattn_A_log, L0_xattn_D,
           L0_ffn_router_w, L0_ffn_gate_w, L0_ffn_up_w, L0_ffn_down_w, L0_ffn_shared_gate_w, L0_ffn_shared_up_w,
           L0_ffn_shared_down_w, L0_ffn_se_gate_w):
    import numpy as np
    import concourse.bacc as bacc
    from concourse.bass_utils import run_bass_kernel_spmd as run

    def parts(w, n):
        return np.asarray(w).T.reshape(n, P, -1).transpose(1, 0, 2)

    xf = np.asarray(x).reshape(TOK, D)
    heads = lambda w: np.asarray(w).transpose(0, 2, 1).reshape(HEADS, DK, P, HD)
    wq, wk, wv = heads(L0_attn_W_Q), heads(L0_attn_W_K), heads(L0_attn_W_V)
    wqk = np.stack([wq, wk], 1).transpose(0, 3, 1, 2, 4).reshape(HEADS, P, 4 * P)
    wv = wv.reshape(PAIRS, 2, DK, P, HD).transpose(0, 3, 2, 1, 4).reshape(PAIRS, P, 4 * P)
    wo = np.asarray(L0_attn_W_O).transpose(0, 2, 1)
    chan = np.concatenate([np.asarray(L0_xattn_conv_w)[:, 0, :], np.asarray(L0_xattn_conv_b)[:, None],
                           np.asarray(L0_xattn_dt_proj_b)[:, None], np.asarray(L0_xattn_D)[:, None],
                           np.asarray(L0_xattn_A_log)], 1).reshape(DM, P, -1).transpose(1, 0, 2)
    router = np.concatenate([np.asarray(L0_ffn_router_w), np.asarray(L0_ffn_se_gate_w),
                             np.zeros((1, D), np.float32)], 0)
    pad = np.zeros((HT * P - HID, D), np.float32)
    gw = np.concatenate([np.asarray(L0_ffn_gate_w).reshape(-1, D), np.asarray(L0_ffn_shared_gate_w), pad], 0)
    uw = np.concatenate([np.asarray(L0_ffn_up_w).reshape(-1, D), np.asarray(L0_ffn_shared_up_w), pad], 0)
    dw = np.concatenate([np.asarray(L0_ffn_down_w).transpose(0, 2, 1).reshape(-1, D),
                         np.asarray(L0_ffn_shared_down_w).T, pad], 0)
    turn = lambda w: w.reshape(HT, P, DK, P).transpose(0, 3, 2, 1).reshape(HT, P, DK * P)
    wf = np.concatenate([turn(gw), turn(uw), dw.reshape(HT, P, D)], 2)
    arrays = {
        "xT": parts(xf, DK), "x": xf.reshape(NT, P, D).transpose(1, 0, 2),
        "ctxT": np.asarray(ctx_1024).reshape(TOK, CTX).T, "inw": np.asarray(L0_xattn_in_proj_w).T,
        "xw": parts(L0_xattn_x_proj_w, DM), "dtw": np.asarray(L0_xattn_dt_proj_w).T, "chan": chan,
        "wqk": wqk, "wv": wv, "wo": wo, "rw": parts(router, DK), "wf": wf,
    }
    nc = bacc.Bacc("TRN2", target_bir_lowering=False, num_devices=1)
    feed, ins = {}, {}
    for name, a in arrays.items():
        feed[f"in_{name}"] = np.ascontiguousarray(a)
        ins[name] = nc.dram_tensor(f"in_{name}", a.shape, F32, kind="ExternalInput").ap()
    out = nc.dram_tensor("out_0", (TOK, D), F32, kind="ExternalOutput").ap()
    decoder_layer(nc, ins, out)
    r = run(nc, [feed], core_ids=[0])
    return r.results[0]["out_0"].reshape(BATCH, SEQ, D)
```

```python
from contextlib import ExitStack

import concourse.bass as bass
from concourse import mybir

F32 = mybir.dt.float32
F32R = mybir.dt.float32r
BF16 = mybir.dt.bfloat16
ALU = mybir.AluOpType
ACT = mybir.ActivationFunctionType
AX = mybir.AxisListType

P = 128
BATCH, SEQ, D = 4, 256, 256
TOK = BATCH * SEQ
NT = TOK // P
DK = D // P
CH = 512
NC = TOK // CH
HEADS, HD = 16, 128
PAIRS = HEADS // 2
QSCALE = -1.0 / float(HD) ** 0.5
MASKED = 1.0e30
CTX = 128
DI = 256
DM = DI // P
STATES, TAPS, RANK = 16, 4, 8
XDBL = RANK + 2 * STATES
EXPERTS, EI, SI = 16, 176, 704
GROUPS = (EXPERTS * EI + SI) // EI
HID = GROUPS * EI
HT = -(-HID // P)
TOPK = 4
NR = EXPERTS + 2
NSEL = 96
SPREAD_TILES = 2
BLOCK = 16
EPS = 1e-5
LP_LEAD = 0.005232687917294774
LP = LP_LEAD ** 0.125
LP_QUADS = ((-2.3216868949994938, 0.43240693469890085), (1.0093577160564058, 1.106062565110738),
            (-1.424736015210064, 2.702104075306238), (-0.08225193417593676, 3.2574693061961))

PRE_UNITS = 22
PRE_ATTN = 12
PAIR_UNITS, HALF_UNITS = 32, 14
Q_U, P_U, K_U, Z_U, S_U, V_U = 0, 2, 6, 8, 10, 28
PRE_HI, PAIR_HI, HALF_HI = 8, 24, 10


def decoder_layer(nc, ins, out):
    with ExitStack() as ctx:
        def sb(name, shape, dt=F32):
            return ctx.enter_context(nc.sbuf_tensor(name, shape, dt))

        def sem(name):
            return ctx.enter_context(nc.semaphore(name))

        xT_hi = sb("xT_hi", [P, DK, TOK], F32R)
        xT_lo = sb("xT_lo", [P, DK, TOK], F32R)
        x_res = sb("x_res", [P, NT, D])
        stage = sb("stage", [P, DK, TOK])
        wqk_raw = sb("wqk_raw", [P, 4 * P])
        wv_raw = sb("wv_raw", [P, 4 * P])
        wo_raw = sb("wo_raw", [P, D])
        wqk_hi = [sb(f"wqk_hi{i}", [P, 4 * P], F32R) for i in range(2)]
        wqk_lo = [sb(f"wqk_lo{i}", [P, 4 * P], F32R) for i in range(2)]
        wv_hi = sb("wv_hi", [P, 4 * P], F32R)
        wv_lo = sb("wv_lo", [P, 4 * P], F32R)
        wo_hi = [sb(f"wo_hi{i}", [P, D], F32R) for i in range(2)]
        wo_lo = [sb(f"wo_lo{i}", [P, D], F32R) for i in range(2)]
        q_hi, q_lo = sb("q_hi", [P, TOK], F32R), sb("q_lo", [P, TOK], F32R)
        k_hi, k_lo = sb("k_hi", [P, TOK], F32R), sb("k_lo", [P, TOK], F32R)
        z_hi, z_lo = sb("z_hi", [P, TOK], F32R), sb("z_lo", [P, TOK], F32R)
        v_hi = sb("v_hi", [P, NT, 2 * HD], F32R)
        v_lo = sb("v_lo", [P, NT, 2 * HD], F32R)
        prob = sb("prob", [P, BATCH, 3 * P])
        pT_hi = sb("pT_hi", [P, BATCH, 3 * P], F32R)
        pT_lo = sb("pT_lo", [P, BATCH, 3 * P], F32R)
        smin = sb("smin", [P, BATCH, 2])
        ssum = sb("ssum", [P, BATCH, 2])
        sinv = sb("sinv", [P, BATCH, 2])
        mask = sb("mask", [P, 2 * P])
        ident = sb("ident", [P, P])
        ident_b = sb("ident_b", [P, P], BF16)
        inw = sb("inw", [P, DI])
        xw = sb("xw", [P, DM, XDBL])
        dtw = sb("dtw", [RANK, DI])
        chan = sb("chan", [P, DM, TAPS + 3 + STATES])
        bc = sb("bc", [P, 4 * TOK])
        b_all = bc[:, 0:2 * TOK].rearrange("p (i t) -> p i t", t=TOK)
        c_all = bc[:, 2 * TOK:].rearrange("p (i t) -> p i t", t=TOK)
        n_pad = DM * BATCH * (SEQ + TAPS - 1)
        padded = bc[:, 0:n_pad].rearrange("p (m b s) -> p m b s", m=DM, b=BATCH)
        ctxT = bc[:, n_pad:n_pad + TOK]
        u = sb("u", [P, DM, TOK])
        xdbl = sb("xdbl", [XDBL, TOK])
        dt = sb("dt", [P, DM, TOK])
        dtu = sb("dtu", [P, DM, TOK])
        y = sb("y", [P, DM, TOK])
        idle = sb("idle", [P, 1])
        lp_bias = sb("lp_bias", [P, len(LP_QUADS)])
        a_neg = sb("a_neg", [P, DM, STATES])
        da = sb("da", [P, DM, BATCH, SEQ])
        dbu = sb("dbu", [P, DM, TOK])
        state = sb("state", [P, DM, TOK])
        stats = sb("stats", [P, NT, 6])
        mv = sb("mv", [P, NT, 2])
        veps = sb("veps", [P, NT])
        rstd = sb("rstd", [P, NT])
        negmean = sb("negmean", [P, NT])
        nbias = sb("nbias", [P, NT])
        mhalf = sb("mhalf", [P, NT])
        rw_raw = sb("rw_raw", [P, DK, NR])
        rw_hi, rw_lo = sb("rw_hi", [P, DK, NR], F32R), sb("rw_lo", [P, DK, NR], F32R)
        lmax = sb("lmax", [P, NT])
        lsub = sb("lsub", [P, NT, EXPERTS])
        lsum = sb("lsum", [P, NT])
        linv = sb("linv", [P, NT])
        probs = sb("probs", [P, NT, EXPERTS + 8])
        picked = sb("picked", [P, NT, EXPERTS + 8])
        top = sb("top", [P, NT, 8])
        gate = sb("gate", [P, NT])
        wr = sb("wr", [P, NT, GROUPS])
        wpart = sb("wpart", [P, NT, NSEL], BF16)
        wT = sb("wT", [NSEL, TOK], BF16)
        sel = sb("sel", [NSEL, SPREAD_TILES * P + 32], BF16)
        w_groups = sb("w_groups", [GROUPS, TOK])
        w_unit = [bc[:, 0:TOK], bc[:, TOK:2 * TOK]]
        h_hi, h_lo = [q_hi, k_hi], [q_lo, k_lo]
        f_raw = [prob[:, 2 * i:2 * i + 2, :].rearrange("p b s -> p (b s)") for i in range(2)]
        gu_hi, gu_lo = wqk_hi, wqk_lo
        dn_hi, dn_lo = wo_hi, wo_lo
        silu_g, hid = da[:, 0].rearrange("p b s -> p (b s)"), dbu[:, 0, :]
        hidw = state[:, 0, :]

        logit_sb = xdbl[0:NR, :]
        def silu_x1(t):
            return da[:, t // 4].rearrange("p b s -> p (b s)")[:, (t % 4) * D:(t % 4 + 1) * D]

        pre = stage[:, :, :].rearrange("p a t -> p (a t)").rearrange("p (t d) -> p t d", d=D)
        prod = [None] + [w[:, 1, :].rearrange("p (b s) -> p b s", s=SEQ) for w in (dt, dtu, state)]
        soft_v, soft_e = da, dbu
        squares = [state, stage, dtu, state]
        conv = [dtu[:, 0, :], dbu[:, 1, :]]

        acc = ctx.enter_context(nc.psum_tensor("acc", [P, NT * D], F32))
        ring = ctx.enter_context(nc.psum_tensor("ring", [P, 4, CH], F32))
        acc_t = acc[:, :].rearrange("p (t d) -> p t d", d=D)

        def bank(g):
            return ring[:, g % 4, :]

        bc_dram = nc.dram_tensor("bc_dram", [2 * STATES, TOK], F32, kind="Internal").ap()

        w_blocks = nc.dram_tensor("w_blocks", [HT * P // BLOCK, TOK], F32, kind="Internal").ap()

        filled = sem("filled")
        pre_read = sem("pre_read")
        bank_read = sem("bank_read")
        hi_done = sem("hi_done")
        exp_done = sem("exp_done")
        inv_done = sem("inv_done")
        probs_ready = sem("probs_ready")
        ld_x, ld_xres, ld_ctx = sem("ld_x"), sem("ld_xres"), sem("ld_ctx")
        ld_chan, ld_xw, ld_rw = sem("ld_chan"), sem("ld_xw"), sem("ld_rw")
        ld_wqk, ld_wv, ld_wo = sem("ld_wqk"), sem("ld_wv"), sem("ld_wo")
        x_hi_s, x_lo_s = sem("x_hi_s"), sem("x_lo_s")
        wqk_h, wv_h, wo_h = sem("wqk_h"), sem("wv_h"), sem("wo_h")
        wqk_s, wv_s, wo_s = sem("wqk_s"), sem("wv_s"), sem("wo_s")
        consts = sem("consts")
        lp_const = sem("lp_const")
        pad_zero, acc_open, acc_set = sem("pad_zero"), sem("acc_open"), sem("acc_set")
        tap_prod = sem("tap_prod")
        conv_taps = [sem("conv_taps0"), sem("conv_taps1")]
        u_done, a_exp, a_done = sem("u_done"), sem("a_exp"), sem("a_done")
        bc_stored, ld_sel, dt_done, dtu_done = sem("bc_stored"), sem("ld_sel"), sem("dt_done"), sem("dtu_done")
        quad_sum = sem("quad_sum")
        soft_abs, soft_x = sem("soft_abs"), sem("soft_x")
        squared = [sem("squared0"), sem("squared1")]
        quads = [sem("quads0"), sem("quads1")]
        bc_load = [sem("bc_load0"), sem("bc_load1")]
        da_done, dbu_done = sem("da_done"), sem("dbu_done")
        scanned, cmul, y_added = sem("scanned"), sem("cmul"), sem("y_added")
        y_last = sem("y_last")
        out_proj = sem("out_proj")
        ln_stat, ln_mv = sem("ln_stat"), sem("ln_mv")
        ln_eps, ln_rstd, ln_bias = sem("ln_eps"), sem("ln_rstd"), sem("ln_bias")
        x1_a, x1_v, x2_v, x2_a = sem("x1_a"), sem("x1_v"), sem("x2_v"), sem("x2_a")
        out_a, out_v = sem("out_a"), sem("out_v")
        silu_z, gated, turned = sem("silu_z"), sem("gated"), sem("turned")
        x2_turned, x2_hi, x2_lo = sem("x2_turned"), sem("x2_hi"), sem("x2_lo")
        logit_t, logit_read = sem("logit_t"), sem("logit_read")
        rw_h, rw_s, logit = sem("rw_h"), sem("rw_s"), sem("logit")
        route, route_e, route_v = sem("route"), sem("route_e"), sem("route_v")
        wt_turned, wt_done = sem("wt_turned"), sem("wt_done")
        groups_f, groups_d, w_stored = sem("groups_f"), sem("groups_d"), sem("w_stored")
        ld_w = [sem("ld_w0"), sem("ld_w1")]
        ld_f = [sem("ld_f0"), sem("ld_f1")]
        gu_h, gu_s, dn_h, dn_s = sem("gu_h"), sem("gu_s"), sem("dn_h"), sem("dn_s")
        gate_f, up_f, wb_f = sem("gate_f"), sem("up_f"), sem("wb_f")
        silu_d, hid_d, hidw_d = sem("silu_d"), sem("hid_d"), sem("hidw_d")
        hhi_d, hlo_d = sem("hhi_d"), sem("hlo_d")
        down_d = sem("down_d")
        stored = sem("stored")

        block = ctx.enter_context(nc.Block())

        @block.sync
        def _(sp):
            sp.dma_start(ctxT[:, :], ins["ctxT"]).then_inc(ld_ctx, 16)
            sp.dma_start(inw[:, :], ins["inw"]).then_inc(ld_ctx, 16)
            sp.dma_start(chan[:, :, :], ins["chan"]).then_inc(ld_chan, 16)
            sp.dma_start(stage[:, :, :], ins["xT"]).then_inc(ld_x, 16)
            sp.dma_start(wqk_raw[:, :], ins["wqk"][0, :, :]).then_inc(ld_wqk, 16)
            sp.dma_start(wv_raw[:, :], ins["wv"][0, :, :]).then_inc(ld_wv, 16)
            sp.dma_start(xw[:, :, :], ins["xw"]).then_inc(ld_xw, 16)
            sp.dma_start(dtw[:, :], ins["dtw"]).then_inc(ld_xw, 16)
            sp.dma_start(wo_raw[:, :], ins["wo"][0, :, :]).then_inc(ld_wo, 16)
            sp.dma_start(x_res[:, :, :], ins["x"]).then_inc(ld_xres, 16)
            sp.dma_start(rw_raw[:, :, :], ins["rw"]).then_inc(ld_rw, 16)
            sp.wait_ge(wqk_s, 1)
            sp.dma_start(wqk_raw[:, :], ins["wqk"][1, :, :]).then_inc(ld_wqk, 16)
            sp.wait_ge(pre_read, 6)
            sp.dma_start(bc_dram, xdbl[RANK:XDBL, :]).then_inc(bc_stored, 16)
            sp.wait_ge(bc_stored, 16)

            def load_bc(n, i):
                sp.dma_start(b_all[:, i, :], bc_dram[bass.ds(n, 1), :].to_broadcast([P, TOK])).then_inc(bc_load[i], 16)
                sp.dma_start(c_all[:, i, :], bc_dram[bass.ds(n + STATES, 1), :].to_broadcast([P, TOK]))\
                  .then_inc(bc_load[i], 16)

            for i in range(2):
                load_bc(i, i)

            def pair_loads(p, first, last):
                for i in range(2):
                    a = 2 * p + i
                    if not last:
                        sp.wait_ge(wqk_s, a + 2)
                        sp.dma_start(wqk_raw[:, :], ins["wqk"][bass.ds(a + 2, 1), :, :].rearrange("h p n -> (h p) n"))\
                          .then_inc(ld_wqk, 16)
                    if not (last and i == 1):
                        sp.wait_ge(wo_s, a + 1)
                        sp.dma_start(wo_raw[:, :], ins["wo"][bass.ds(a + 1, 1), :, :].rearrange("h p n -> (h p) n"))\
                          .then_inc(ld_wo, 16)
                    if i == 0 and not last:
                        sp.wait_ge(wv_s, p + 1)
                        sp.dma_start(wv_raw[:, :], ins["wv"][bass.ds(p + 1, 1), :, :].rearrange("h p n -> (h p) n"))\
                          .then_inc(ld_wv, 16)
                    if not (first and i == 0) and not (last and i == 1):
                        n = 2 * p - 1 + i
                        sp.wait_ge(dbu_done, 2 * n + 2)
                        sp.wait_ge(cmul, 2 * n + 2)
                        load_bc(n + 2, 1 - i)

            pair_loads(0, True, False)
            with sp.Fori(1, PAIRS - 1) as p:
                pair_loads(p, False, False)
            pair_loads(PAIRS - 1, False, True)
            sp.wait_ge(consts, 13)
            for r in range(32, NSEL, 32):
                sp.dma_start(sel[r:r + 32, :], sel[0:32, :]).then_inc(ld_sel, 16)
            sp.wait_ge(filled, PRE_UNITS + PAIR_UNITS * (PAIRS - 1) + HALF_UNITS + BATCH)
            for i in range(2):
                sp.dma_start(f_raw[i], ins["wf"][i, :, :]).then_inc(ld_f[i], 16)

            def mlp_load(j, i):
                sp.wait_ge(dn_s, j - 1)
                sp.dma_start(f_raw[i], ins["wf"][bass.ds(j, 1), :, :].rearrange("h p n -> (h p) n"))\
                  .then_inc(ld_f[i], 16)

            sp.wait_ge(groups_d, NC)
            sp.dma_start(w_blocks[0:HID // BLOCK, :].rearrange("(g k) t -> g k t", g=GROUPS),
                         w_groups[:, :].unsqueeze(1).to_broadcast([GROUPS, EI // BLOCK, TOK])).then_inc(w_stored, 16)
            sp.dma_start(w_blocks[HID // BLOCK:, :], w_groups[0:(HT * P - HID) // BLOCK, :]).then_inc(w_stored, 16)
            sp.wait_ge(w_stored, 32)
            with sp.Fori(0, HT // 2 - 1) as r:
                for i in range(2):
                    j = 2 * r + 2 + i
                    mlp_load(j, i)
                    sp.wait_ge(hidw_d, NC * (j - 1))
                    sp.dma_start(w_unit[i],
                                 w_blocks[bass.ds(j * (P // BLOCK), P // BLOCK), :].unsqueeze(1)
                                 .to_broadcast([P // BLOCK, BLOCK, TOK])).then_inc(ld_w[i], 16)
            for t in range(NT):
                if t in (4, 5):
                    sp.wait_ge(out_v, t - 3)
                else:
                    sp.wait_ge(out_a, t + 1 if t < 4 else t - 1)
                sp.dma_start(out[t * P:(t + 1) * P, :], pre[:, t, :]).then_inc(stored, 16)
            sp.wait_ge(stored, 16 * NT)

        @block.gpsimd
        def _(pool):
            pool.memset(ident[:, :], 0.0).then_inc(consts, 1)
            pool.memset(mask[:, :], 0.0).then_inc(consts, 1)
            pool.memset(padded[:, :, :, 0:TAPS - 1], 0.0).then_inc(pad_zero, 1)
            pool.wait_ge(consts, 2)
            pool.affine_select(out=ident[:, :], in_=ident[:, :], compare_op=ALU.not_equal, fill=1.0,
                               base=0, pattern=[[-1, P]], channel_multiplier=1).then_inc(consts, 1)
            pool.affine_select(out=mask[:, P:2 * P], in_=mask[:, P:2 * P], compare_op=ALU.is_ge,
                               fill=MASKED, base=0, pattern=[[-1, P]], channel_multiplier=1).then_inc(consts, 1)
            pool.wait_ge(consts, 4)
            pool.tensor_scalar(ident_b[:, :], ident[:, :], 1.0, 0.0, ALU.mult, ALU.add).then_inc(consts, 1)

            for k, (root, _) in enumerate(LP_QUADS):
                pool.memset(lp_bias[:, k:k + 1], LP * root).then_inc(lp_const, 1)

            def split(raw, hi, lo, hi_sem, lo_sem, n):
                pool.nop(nofuse=True)
                pool.tensor_scalar(hi, raw, 1.0, 0.0, ALU.mult, ALU.add).then_inc(hi_sem, 1)
                pool.wait_ge(hi_sem, n)
                pool.tensor_tensor(lo, raw, hi.bitcast(F32), ALU.subtract).then_inc(lo_sem, 1)

            pool.wait_ge(ld_wqk, 16)
            split(wqk_raw[:, :], wqk_hi[0][:, :], wqk_lo[0][:, :], wqk_h, wqk_s, 1)
            pool.wait_ge(ld_wv, 16)
            split(wv_raw[:, :], wv_hi[:, :], wv_lo[:, :], wv_h, wv_s, 1)
            pool.wait_ge(pre_read, NC * DM)
            pool.wait_ge(pad_zero, 1)
            dst = conv[1].rearrange("p (b s) -> p b s", s=SEQ)
            pool.tensor_scalar(dst, padded[:, 1, :, 0:SEQ], chan[:, 1, 0:1], 1.0, ALU.mult, ALU.mult)\
                .then_inc(conv_taps[1], 1)
            for k in range(1, TAPS):
                pool.wait_ge(tap_prod, k)
                pool.wait_ge(conv_taps[1], k)
                pool.tensor_tensor(dst, dst, prod[k], ALU.add).then_inc(conv_taps[1], 1)
            pool.wait_ge(ld_wqk, 32)
            split(wqk_raw[:, :], wqk_hi[1][:, :], wqk_lo[1][:, :], wqk_h, wqk_s, 2)
            pool.wait_ge(ld_wo, 16)
            split(wo_raw[:, :], wo_hi[0][:, :], wo_lo[0][:, :], wo_h, wo_s, 1)
            for m in range(DM):
                pool.wait_ge(u_done, m + 1)
                pool.tensor_scalar(y[:, m, :], u[:, m, :], chan[:, m, TAPS + 2:TAPS + 3], 1.0,
                                   ALU.mult, ALU.mult).then_inc(y_added, 1)

            def late_constants():
                pool.memset(mhalf[:, :], -0.5).then_inc(consts, 1)
                pool.memset(probs[:, :, EXPERTS:EXPERTS + 8], -1.0).then_inc(consts, 1)
                pool.memset(wpart[:, :, :], 0.0).then_inc(consts, 1)
                units, groups = slice(0, SPREAD_TILES * P), slice(SPREAD_TILES * P, SPREAD_TILES * P + 32)
                pool.memset(sel[0:32, units], 1.0).then_inc(consts, 1)
                pool.memset(sel[0:32, groups], 0.0).then_inc(consts, 1)
                pool.wait_ge(consts, 10)
                pool.affine_select(out=sel[0:32, units], in_=sel[0:32, units], compare_op=ALU.is_ge, fill=0.0,
                                   base=0, pattern=[[1, SPREAD_TILES * P]], channel_multiplier=-EI)\
                    .then_inc(consts, 1)
                pool.wait_ge(consts, 11)
                pool.affine_select(out=sel[0:32, units], in_=sel[0:32, units], compare_op=ALU.is_ge, fill=0.0,
                                   base=EI - 1, pattern=[[-1, SPREAD_TILES * P]], channel_multiplier=EI)\
                    .then_inc(consts, 1)
                pool.wait_ge(consts, 12)
                pool.affine_select(out=sel[0:32, groups], in_=sel[0:32, groups], compare_op=ALU.not_equal, fill=1.0,
                                   base=0, pattern=[[-1, 32]], channel_multiplier=1).then_inc(consts, 1)

            def make_dbu(n, i, m):
                pool.wait_ge(bc_load[i], 16 * (n - i) + 32)
                pool.wait_ge(scanned, 2 * n + m + 1)
                pool.tensor_tensor(dbu[:, m, :], dtu[:, m, :], b_all[:, i, :], ALU.mult).then_inc(dbu_done, 1)

            def add_y(n, m):
                pool.wait_ge(cmul, 2 * n + m + 1)
                pool.wait_ge(y_added, 2 * n + m + 1)
                pool.tensor_tensor(y[:, m, :], y[:, m, :], state[:, m, :], ALU.add).then_inc(y_added, 1)

            def pair_pool(p, first, last):
                for i in range(2):
                    a, n = 2 * p + i, 2 * p - 1 + i
                    if not first:
                        make_dbu(n + 1, i, 0)
                    if not last:
                        pool.wait_ge(filled, PRE_UNITS + PAIR_UNITS * p + HALF_UNITS * i + 1)
                        pool.wait_ge(ld_wqk, 16 * (a + 3))
                        split(wqk_raw[:, :], wqk_hi[i][:, :], wqk_lo[i][:, :], wqk_h, wqk_s, a + 3)
                    if not first:
                        add_y(n, 0)
                    if not (last and i == 1):
                        pool.wait_ge(filled, PRE_UNITS + PAIR_UNITS * p + HALF_UNITS * i + P_U + 1)
                        pool.wait_ge(ld_wo, 16 * (a + 2))
                        split(wo_raw[:, :], wo_hi[1 - i][:, :], wo_lo[1 - i][:, :], wo_h, wo_s, a + 2)
                    if i == 0 and not last:
                        pool.wait_ge(ld_wv, 16 * (p + 2))
                        split(wv_raw[:, :], wv_hi[:, :], wv_lo[:, :], wv_h, wv_s, p + 2)
                    if first and i == 0:
                        for m in range(DM):
                            quad = squares[2][:, m, :]
                            pool.wait_ge(squared[m], 3)
                            pool.tensor_scalar(quad, quad, 1.0, LP * LP * LP_QUADS[2][1], ALU.mult, ALU.add)\
                                .then_inc(quad_sum, 1)
                        for m in range(DM):
                            pool.wait_ge(quad_sum, m + 1)
                            pool.wait_ge(quads[m], 2)
                            pool.tensor_tensor(dt[:, m, :], dt[:, m, :], squares[2][:, m, :], ALU.mult)\
                                .then_inc(quads[m], 1)
                        for m in range(DM):
                            pool.wait_ge(dt_done, m + 1)
                            pool.tensor_tensor(dtu[:, m, :], dt[:, m, :], u[:, m, :], ALU.mult).then_inc(dtu_done, 1)
                            pool.wait_ge(dtu_done, m + 1)
                            make_dbu(0, 0, m)
                    elif first:
                        for m in range(DM):
                            make_dbu(1, 1, m)
                            add_y(0, m)
                    else:
                        make_dbu(n + 1, i, 1)
                        add_y(n, 1)

            pool.wait_ge(ld_rw, 16)
            split(rw_raw[:, :, :], rw_hi[:, :, :], rw_lo[:, :, :], rw_h, rw_s, 1)
            late_constants()
            pair_pool(0, True, False)
            with pool.Fori(1, PAIRS - 1) as p:
                pair_pool(p, False, False)
            pair_pool(PAIRS - 1, False, True)
            def norm_scale(n, g):
                t = slice(4 * g, 4 * g + 4)
                pool.wait_ge(ln_mv, NT * n + 4 * g + 4)
                pool.tensor_scalar(veps[:, t], mv[:, t, 1], 1.0, EPS, ALU.mult, ALU.add).then_inc(ln_eps, 1)
                pool.tensor_scalar(negmean[:, t], mv[:, t, 0], -1.0, 0.0, ALU.mult, ALU.add).then_inc(ln_eps, 1)
                pool.wait_ge(ln_eps, 4 * n + 2 * g + 2)
                pool.tensor_tensor(rstd[:, t], veps[:, t], mhalf[:, t], ALU.pow).then_inc(ln_rstd, 1)
                pool.wait_ge(ln_rstd, 2 * n + g + 1)
                pool.tensor_tensor(nbias[:, t], negmean[:, t], rstd[:, t], ALU.mult).then_inc(ln_bias, 1)

            def split_gate_up(j, i):
                pool.wait_ge(ld_f[i], 8 * j + 16 - 8 * i)
                split(f_raw[i][:, 0:4 * P], gu_hi[i][:, :], gu_lo[i][:, :], gu_h, gu_s, j + 1)

            def split_down(j, i):
                split(f_raw[i][:, 4 * P:], dn_hi[i][:, :], dn_lo[i][:, :], dn_h, dn_s, j + 1)

            def lo_h(j, i):
                for c in range(NC):
                    s = slice(c * CH, (c + 1) * CH)
                    pool.wait_ge(hhi_d, NC * j + c + 1)
                    pool.tensor_tensor(h_lo[i][:, s], hidw[:, s], h_hi[i][:, s].bitcast(F32), ALU.subtract)\
                        .then_inc(hlo_d, 1)

            for g in range(2):
                norm_scale(0, g)
            add_y(STATES - 1, 0)
            split_gate_up(0, 0)
            split_down(0, 0)
            for g in range(2):
                norm_scale(1, g)
            split_gate_up(1, 1)
            split_down(1, 1)
            lo_h(0, 0)
            with pool.Fori(0, HT // 2 - 1) as r:
                for i in range(2):
                    j = 2 * r + i
                    pool.wait_ge(up_f, NC * (j + 1))
                    split_gate_up(j + 2, i)
                    lo_h(j + 1, 1 - i)
                    pool.wait_ge(down_d, j + 1)
                    split_down(j + 2, i)
            lo_h(HT - 1, 1)
            for g in range(2):
                norm_scale(2, g)

        @block.scalar
        def _(act):
            def drain_in_proj(m):
                for c in range(NC):
                    g = NC * m + c
                    act.wait_ge(filled, g + 1)
                    act.activation(padded[:, m, 2 * c:2 * c + 2, TAPS - 1:],
                                   bank(g).rearrange("p (b s) -> p b s", s=SEQ), ACT.Copy).then_inc(pre_read, 1)

            drain_in_proj(0)
            act.wait_ge(ld_x, 16)
            for c in range(NC):
                for k in range(DK):
                    s = slice(c * CH, (c + 1) * CH)
                    act.activation(xT_hi[:, k, s], stage[:, k, s], ACT.Copy).then_inc(x_hi_s, 1)
            drain_in_proj(1)

            def hi(dst, g, n_units, scale=1.0, cols=CH):
                act.wait_ge(filled, n_units)
                act.activation(dst, bank(g)[:, 0:cols], ACT.Copy, scale=scale).then_inc(hi_done, 1)

            def hi_qk(dst, g, n, c, scale):
                hi(dst[:, c * CH:(c + 1) * CH], g, n + 1, scale)

            def silu_u(m):
                act.wait_ge(conv_taps[m], TAPS)
                act.activation(u[:, m, :], conv[m], ACT.Silu, bias=chan[:, m, TAPS:TAPS + 1]).then_inc(u_done, 1)

            act.wait_ge(pad_zero, 1)
            act.wait_ge(pre_read, NC * DM)
            for k in range(1, TAPS):
                act.activation(prod[k], padded[:, 1, :, k:k + SEQ], ACT.Copy, scale=chan[:, 1, k:k + 1])\
                   .then_inc(tap_prod, 1)
            for c in range(NC):
                hi_qk(q_hi, 4 + c, 4 + c, c, QSCALE)
            for c in range(NC):
                hi_qk(k_hi, 6 + c, 6 + c, c, 1.0)
            silu_u(0)
            for t in range(4):
                hi(v_hi[:, 2 * t:2 * t + 2, :].rearrange("p t e -> p (t e)"), 8 + t, 9 + t)
                if t == 0:
                    silu_u(1)
            def exps(n):
                for b in range(BATCH):
                    act.wait_ge(bank_read, n + b + 1)
                    act.activation(prob[:, b, 0:P], prob[:, b, 0:P], ACT.Exp, bias=smin[:, b, 0:1], scale=-1.0,
                                   accum_out=ssum[:, b, 0:1]).then_inc(exp_done, 1)
                    act.activation(prob[:, b, P:], prob[:, b, P:], ACT.Exp, bias=smin[:, b, 1:2], scale=-1.0,
                                   accum_out=ssum[:, b, 1:2]).then_inc(exp_done, 1)

            def make_da(n, m):
                act.wait_ge(scanned, 2 * n + m + 1)
                act.activation(da[:, m, :, 1:], dt[:, m, :].rearrange("p (b s) -> p b s", s=SEQ)[:, :, 1:],
                               ACT.Exp, scale=a_neg[:, m, bass.ds(n, 1)]).then_inc(da_done, 1)

            for c in range(NC):
                act.wait_ge(filled, 13 + c)
                act.activation(xdbl[:, c * CH:(c + 1) * CH], bank(12 + c)[0:XDBL, :], ACT.Copy).then_inc(pre_read, 1)
            exps(8)
            act.activation(a_neg[:, :, :], chan[:, :, TAPS + 3:], ACT.Exp).then_inc(a_exp, 1)
            for m in range(DM):
                for c in range(NC):
                    g = 18 + NC * m + c
                    act.wait_ge(filled, g + 1)
                    act.activation(soft_v[:, m, 2 * c:2 * c + 2, :].rearrange("p b s -> p (b s)"), bank(g),
                                   ACT.Identity, bias=chan[:, m, TAPS + 1:TAPS + 2]).then_inc(pre_read, 1)
            for m in range(DM):
                act.wait_ge(soft_abs, m + 1)
                act.activation(soft_e[:, m, :], soft_e[:, m, :], ACT.Exp, scale=-1.0).then_inc(soft_x, 1)

            def soft_square(k):
                for m in range(DM):
                    act.wait_ge(soft_x, m + 1)
                    if k == 3:
                        act.wait_ge(quads[m], 1)
                    act.activation(squares[k][:, m, :], soft_e[:, m, :], ACT.Square, scale=LP,
                                   bias=lp_bias[:, k:k + 1]).then_inc(squared[m], 1)

            def pair_act(p, first, last):
                for i in range(2):
                    base = PRE_UNITS + PAIR_UNITS * p + HALF_UNITS * i
                    gb = PRE_UNITS + HALF_UNITS * i
                    n = 2 * p - 1 + i
                    nxt = not (last and i == 1)
                    if last and i == 1:
                        pt, z = P_U - 2, Z_U - 4
                    else:
                        pt, z = P_U, Z_U
                    if nxt:
                        for c in range(NC):
                            hi_qk(q_hi, gb + Q_U + c, base + Q_U + c, c, QSCALE)
                    for b in range(BATCH):
                        hi(pT_hi[:, b, :], gb + pt + b, base + pt + b + 1, cols=3 * P)
                    if first and i == 0:
                        act.wait_ge(lp_const, len(LP_QUADS))
                        soft_square(0)
                    elif not first:
                        make_da(n, 1)
                    if nxt:
                        for c in range(NC):
                            hi_qk(k_hi, gb + K_U + c, base + K_U + c, c, 1.0)
                    if first and i == 0:
                        soft_square(1)
                    if not first:
                        make_da(n + 1, 0)
                    for c in range(NC):
                        hi_qk(z_hi, gb + z + c, base + z + c, c, 1.0)
                    if first and i == 1:
                        act.wait_ge(a_done, 1)
                        for m in range(DM):
                            make_da(0, m)
                    if first and i == 0:
                        soft_square(2)
                    if nxt:
                        exps(PRE_ATTN + PAIR_UNITS * p + HALF_UNITS * i + S_U)
                    if first and i == 0:
                        soft_square(3)
                    if first and i == 1:
                        make_da(1, 0)
                if not last:
                    for t in range(4):
                        hi(v_hi[:, 2 * t:2 * t + 2, :].rearrange("p t e -> p (t e)"),
                           PRE_UNITS + V_U + t, PRE_UNITS + PAIR_UNITS * p + V_U + t + 1)

            pair_act(0, True, False)
            with act.Fori(1, PAIRS - 1) as p:
                pair_act(p, False, False)
            pair_act(PAIRS - 1, False, True)
            make_da(STATES - 1, 1)

            def normed(n, t, src, dst, func, done):
                act.wait_ge(ln_bias, 2 * n + t // 4 + 1)
                act.activation(dst, src[:, t, :], func, scale=rstd[:, t:t + 1], bias=nbias[:, t:t + 1])\
                   .then_inc(done, 1)

            act.activation(idle[:, :], lp_bias[:, 0:1], ACT.Silu)
            act.wait_ge(scanned, 1 + 2 * STATES)
            for t in range(4):
                normed(0, t, acc_t, silu_x1(t), ACT.Silu, silu_z)
            for t in range(2):
                normed(0, t, acc_t, acc_t[:, t, :], ACT.Identity, x1_a)
            act.wait_ge(scanned, 2 + 2 * STATES)
            for t in range(4, NT):
                normed(0, t, acc_t, silu_x1(t), ACT.Silu, silu_z)
            for t in range(2, 6):
                normed(0, t, acc_t, acc_t[:, t, :], ACT.Identity, x1_a)
            for n in range(NC * DK):
                if n == 0:
                    for t in range(4):
                        normed(1, t, acc_t, x_res[:, t, :], ACT.Identity, x2_a)
                if n == 2:
                    for t in (4, 5):
                        normed(1, t, acc_t, x_res[:, t, :], ACT.Identity, x2_a)
                act.wait_ge(x2_turned, n + 1)
                act.activation(xT_hi[:, n % DK, (n // DK) * CH:(n // DK + 1) * CH], bank(n), ACT.Copy)\
                   .then_inc(x2_hi, 1)
            for c in range(NC):
                act.wait_ge(logit_t, c + 1)
                act.activation(logit_sb[:, c * CH:(c + 1) * CH], acc[0:NR, c * CH:(c + 1) * CH], ACT.Copy)\
                   .then_inc(logit_read, 1)
            act.wait_ge(route, 2)
            act.activation(probs[:, :, 0:EXPERTS], lsub[:, :, :], ACT.Exp).then_inc(route_e, 1)
            act.activation(gate[:, :], gate[:, :], ACT.Exp).then_inc(route_e, 1)

            def silu_gate(j, g0, step, first):
                for c in range(NC):
                    s = slice(c * CH, (c + 1) * CH)
                    act.wait_ge(gate_f, NC * j + c + 1)
                    if not first:
                        act.wait_ge(hid_d, NC * (j - 1) + c + 1)
                    act.activation(silu_g[:, s], bank(g0 + step * c), ACT.Silu).then_inc(silu_d, 1)

            def hi_h(j, i):
                for c in range(NC):
                    s = slice(c * CH, (c + 1) * CH)
                    act.wait_ge(hidw_d, NC * j + c + 1)
                    act.activation(h_hi[i][:, s], hidw[:, s], ACT.Copy).then_inc(hhi_d, 1)

            silu_gate(0, 2, 3, True)
            act.wait_ge(wt_turned, 1)
            act.activation(wT[:, :], acc[0:NSEL, 3 * CH:].bitcast(BF16), ACT.Copy).then_inc(wt_done, 1)
            for c in range(NC):
                act.wait_ge(groups_f, c + 1)
                act.activation(w_groups[:, c * CH:(c + 1) * CH], acc[0:GROUPS, c * CH:(c + 1) * CH], ACT.Copy)\
                   .then_inc(groups_d, 1)
            hi_h(0, 0)
            silu_gate(1, 2 + 6, 3, False)
            hi_h(1, 1)
            with act.Fori(0, HT // 2 - 1) as r:
                for i in range(2):
                    silu_gate(2 * r + 2 + i, 2, 2, False)
                    hi_h(2 * r + 2 + i, i)
            for t in (0, 1, 2, 3, 6, 7):
                normed(2, t, acc_t, pre[:, t, :], ACT.Identity, out_a)

        @block.vector
        def _(dve):
            def tap(k):
                src, weight = padded[:, 0, :, k:k + SEQ], chan[:, 0, k:k + 1]
                dst = conv[0].rearrange("p (b s) -> p b s", s=SEQ)
                if k == 0:
                    dve.tensor_scalar(dst, src, weight, None, ALU.mult).then_inc(conv_taps[0], 1)
                else:
                    dve.wait_ge(conv_taps[0], k)
                    dve.scalar_tensor_tensor(out=dst, in0=src, scalar=weight, in1=dst, op0=ALU.mult, op1=ALU.add)\
                       .then_inc(conv_taps[0], 1)

            dve.wait_ge(ld_chan, 16)
            dve.wait_ge(pre_read, NC)
            dve.wait_ge(pad_zero, 1)
            tap(0)
            dve.wait_ge(ld_x, 16)
            for c in range(NC):
                for k in range(DK):
                    s = slice(c * CH, (c + 1) * CH)
                    dve.wait_ge(x_hi_s, DK * c + k + 1)
                    dve.tensor_tensor(xT_lo[:, k, s], stage[:, k, s], xT_hi[:, k, s].bitcast(F32), ALU.subtract)\
                       .then_inc(x_lo_s, 1)
            for k in range(1, TAPS):
                tap(k)

            def lo(dst, hi_part, g, n_hi, scale=None, cols=CH):
                dve.wait_ge(hi_done, n_hi)
                if scale is None:
                    dve.tensor_tensor(dst, bank(g)[:, 0:cols], hi_part.bitcast(F32), ALU.subtract).then_inc(bank_read, 1)
                else:
                    dve.scalar_tensor_tensor(out=dst, in0=bank(g)[:, 0:cols], scalar=scale, in1=hi_part.bitcast(F32),
                                             op0=ALU.mult, op1=ALU.subtract).then_inc(bank_read, 1)

            def lo_qk(dst, src, g, n, c, scale=None):
                s = slice(c * CH, (c + 1) * CH)
                lo(dst[:, s], src[:, s], g, n + 1, scale)

            def lo_v(t, g, n):
                lo(v_lo[:, 2 * t:2 * t + 2, :].rearrange("p t e -> p (t e)"),
                   v_hi[:, 2 * t:2 * t + 2, :].rearrange("p t e -> p (t e)"), g, n + 1)

            for c in range(NC):
                lo_qk(q_lo, q_hi, 4 + c, c, c, QSCALE)
            for c in range(NC):
                lo_qk(k_lo, k_hi, 6 + c, 2 + c, c)
            for t in range(4):
                lo_v(t, 8 + t, 4 + t)

            def softplus_quad(k):
                for m in range(DM):
                    dve.wait_ge(squared[m], k + 1)
                    if k:
                        dve.wait_ge(quads[m], k)
                    dve.scalar_tensor_tensor(out=dt[:, m, :], in0=squares[k][:, m, :], scalar=LP * LP * LP_QUADS[k][1],
                                             in1=dt[:, m, :] if k else soft_e[:, m, :], op0=ALU.add, op1=ALU.mult)\
                       .then_inc(quads[m], 1)

            def softplus_end():
                for m in range(DM):
                    dve.wait_ge(quads[m], len(LP_QUADS))
                    dve.scalar_tensor_tensor(out=dt[:, m, :], in0=soft_v[:, m].rearrange("p b s -> p (b s)"),
                                             scalar=0.0, in1=dt[:, m, :], op0=ALU.max, op1=ALU.add).then_inc(dt_done, 1)

            def mask_scores(b, g, n_units):
                dve.wait_ge(filled, n_units)
                dve.nop(nofuse=True)
                dve.tensor_tensor_reduce(prob[:, b, 0:P], bank(g)[:, 0:P], mask[:, P:], 1.0, 3.0e38, ALU.add, ALU.min,
                                         smin[:, b, 0:1])
                dve.tensor_tensor_reduce(prob[:, b, P:], bank(g)[:, P:3 * P], mask[:, :], 1.0, 3.0e38, ALU.add, ALU.min,
                                         smin[:, b, 1:2]).then_inc(bank_read, 1)

            def normalise(n):
                for b in range(BATCH):
                    dve.wait_ge(exp_done, 8 * n + 2 * b + 2)
                    dve.reciprocal(sinv[:, b, :], ssum[:, b, :]).then_inc(inv_done, 1)
                for b in range(BATCH):
                    dve.wait_ge(inv_done, BATCH * n + b + 1)
                    dve.tensor_scalar(prob[:, b, 0:P], prob[:, b, 0:P], sinv[:, b, 0:1], None, ALU.mult)\
                       .then_inc(probs_ready, 1)
                    dve.tensor_scalar(prob[:, b, P:], prob[:, b, P:], sinv[:, b, 1:2], None, ALU.mult)\
                       .then_inc(probs_ready, 1)

            def scan(n, m):
                dve.wait_ge(da_done, 2 * n + m + 1)
                dve.wait_ge(dbu_done, 2 * n + m + 1)
                dve.wait_ge(y_added, 2 * n + m + 1)
                dve.tensor_tensor_scan(state[:, m, :], da[:, m].rearrange("p b s -> p (b s)"), dbu[:, m, :], 0.0,
                                       ALU.mult, ALU.add).then_inc(scanned, 1)

            def times_c(n, i, m):
                dve.wait_ge(scanned, 2 * n + m + 3)
                dve.wait_ge(bc_load[i], 16 * (n - i) + 32)
                dve.tensor_tensor(state[:, m, :], state[:, m, :], c_all[:, i, :], ALU.mult).then_inc(cmul, 1)

            dve.wait_ge(ld_xres, 16)
            dve.wait_ge(acc_open, 1)
            dve.tensor_copy(acc[:, :], x_res[:, :, :].rearrange("p t d -> p (t d)")).then_inc(acc_set, 1)
            dve.wait_ge(consts, 4)
            for b in range(BATCH):
                mask_scores(b, 14 + b, 15 + b)
            dve.wait_ge(a_exp, 1)
            dve.tensor_scalar(a_neg[:, :, :], a_neg[:, :, :], -1.0, None, ALU.mult).then_inc(a_done, 1)
            normalise(0)
            for m in range(DM):
                v = soft_v[:, m].rearrange("p b s -> p (b s)")
                dve.wait_ge(pre_read, 8 + 2 * m)
                dve.scalar_tensor_tensor(out=soft_e[:, m, :], in0=v, scalar=-1.0, in1=v, op0=ALU.mult,
                                         op1=ALU.max).then_inc(soft_abs, 1)

            def pair_dve(p, first, last):
                for i in range(2):
                    base = PRE_UNITS + PAIR_UNITS * p + HALF_UNITS * i
                    hbase = PRE_HI + PAIR_HI * p + HALF_HI * i
                    gb = PRE_UNITS + HALF_UNITS * i
                    n = 2 * p - 1 + i
                    nxt = not (last and i == 1)
                    pt, z, hp, hz = (P_U, Z_U, 2, 8) if nxt else (P_U - 2, Z_U - 4, 0, 4)
                    if nxt:
                        for c in range(NC):
                            lo_qk(q_lo, q_hi, gb + Q_U + c, hbase + c, c, QSCALE)
                    for b in range(BATCH):
                        lo(pT_lo[:, b, :], pT_hi[:, b, :], gb + pt + b, hbase + hp + b + 1, cols=3 * P)
                    if first and i == 0:
                        softplus_quad(0)
                    elif first:
                        softplus_quad(3)
                        softplus_end()
                        dve.wait_ge(dt_done, 2)
                        dve.memset(da[:, :, :, 0:1], 0.0).then_inc(scanned, 2)
                    elif i == 1:
                        times_c(n, 0, 0)
                    if nxt:
                        for c in range(NC):
                            lo_qk(k_lo, k_hi, gb + K_U + c, hbase + 6 + c, c)
                    if first and i == 0:
                        softplus_quad(1)
                    elif not first:
                        scan(n, 1)
                    for c in range(NC):
                        lo_qk(z_lo, z_hi, gb + z + c, hbase + hz + c, c)
                    if nxt:
                        for b in range(BATCH):
                            mask_scores(b, gb + S_U + b, base + S_U + b + 1)
                    if not first:
                        times_c(n, 1 - i, 1)
                        scan(n + 1, 0)
                        if i == 1:
                            times_c(n + 1, i, 0)
                    if first and i == 1:
                        for m in range(DM):
                            scan(0, m)
                            times_c(0, 0, m)
                    if i == 1 and not last:
                        for t in range(2):
                            lo_v(t, PRE_UNITS + V_U + t, PRE_HI + PAIR_HI * p + 20 + t)
                    if nxt:
                        normalise(2 * p + i + 1)
                if not last:
                    for t in range(2, 4):
                        lo_v(t, PRE_UNITS + V_U + t, PRE_HI + PAIR_HI * p + 20 + t)
                if first:
                    scan(1, 0)
                    times_c(1, 1, 0)

            pair_dve(0, True, False)
            with dve.Fori(1, PAIRS - 1) as p:
                pair_dve(p, False, False)
            pair_dve(PAIRS - 1, False, True)

            def moments(n, g, ready, count):
                for t in range(4 * g, 4 * g + 5):
                    if t < 4 * g + 4:
                        ready_tiles = t // 2 * 2 + 2
                        dve.wait_ge(ready, count + ready_tiles)
                        dve.bn_stats(stats[:, t, :], acc_t[:, t, :]).then_inc(ln_stat, 1)
                    if t > 4 * g:
                        dve.wait_ge(ln_stat, NT * n + t)
                        dve.bn_aggr(mv[:, t - 1, :], stats[:, t - 1, :]).then_inc(ln_mv, 1)

            def normed(n, t, src, dst, done):
                dve.wait_ge(ln_rstd, 2 * n + t // 4 + 1)
                dve.tensor_scalar(dst[:, t, :], src[:, t, :], mv[:, t, 0:1], rstd[:, t:t + 1],
                                  ALU.subtract, ALU.mult).then_inc(done, 1)

            for g in range(2):
                moments(0, g, out_proj, 0)
            scan(STATES - 1, 1)
            times_c(STATES - 1, 1, 1)
            dve.wait_ge(cmul, 2 * STATES)
            dve.wait_ge(y_added, 2 * STATES)
            dve.tensor_tensor(y[:, 1, :], y[:, 1, :], state[:, 1, :], ALU.add).then_inc(y_last, 1)
            dve.wait_ge(y_last, 1)
            for t in (1, 3, 0, 2, 4, 5, 6, 7):
                b, m = t // DM, t % DM
                if t == 0:
                    dve.wait_ge(y_added, 2 * STATES + 1)
                dve.wait_ge(silu_z, t + 1)
                dve.tensor_tensor(y[:, m, b * SEQ:(b + 1) * SEQ], y[:, m, b * SEQ:(b + 1) * SEQ], silu_x1(t),
                                  ALU.mult).then_inc(gated, 1)

            for t in (6, 7):
                normed(0, t, acc_t, acc_t, x1_v)
            for g in range(2):
                moments(1, g, turned, 0)
            for n in range(NC * DK):
                if n == 1:
                    for t in (6, 7):
                        normed(1, t, acc_t, x_res, x2_v)
                dve.wait_ge(x2_hi, n + 1)
                s = slice((n // DK) * CH, (n // DK + 1) * CH)
                dve.tensor_tensor(xT_lo[:, n % DK, s], bank(n), xT_hi[:, n % DK, s].bitcast(F32), ALU.subtract)\
                   .then_inc(x2_lo, 1)

            dve.wait_ge(logit, 1)
            dve.wait_ge(consts, 8)
            logits = acc[:, 2 * CH:2 * CH + NT * NR].rearrange("p (t e) -> p t e", e=NR)
            dve.tensor_reduce(lmax[:, :], logits[:, :, 0:EXPERTS], AX.X, ALU.max).then_inc(route_v, 1)
            dve.tensor_scalar(gate[:, :], logits[:, :, EXPERTS], -1.0, 80.0, ALU.mult, ALU.min).then_inc(route, 1)
            dve.wait_ge(route_v, 1)
            dve.tensor_tensor(lsub[:, :, :], logits[:, :, 0:EXPERTS],
                              lmax[:, :].unsqueeze(2).to_broadcast([P, NT, EXPERTS]), ALU.subtract).then_inc(route, 1)
            dve.wait_ge(route_e, 2)
            dve.tensor_reduce(lsum[:, :], probs[:, :, 0:EXPERTS], AX.X, ALU.add).then_inc(route_v, 1)
            dve.tensor_scalar(gate[:, :], gate[:, :], 1.0, None, ALU.add).then_inc(route, 1)
            dve.wait_ge(route_v, 2)
            dve.reciprocal(linv[:, :], lsum[:, :]).then_inc(route_v, 1)
            dve.wait_ge(route, 3)
            dve.reciprocal(wr[:, :, EXPERTS:], gate[:, :].unsqueeze(2).to_broadcast([P, NT, GROUPS - EXPERTS]))\
               .then_inc(route, 1)
            dve.wait_ge(route_v, 3)
            dve.tensor_tensor(probs[:, :, 0:EXPERTS], probs[:, :, 0:EXPERTS],
                              linv[:, :].unsqueeze(2).to_broadcast([P, NT, EXPERTS]), ALU.mult).then_inc(route_v, 1)
            dve.wait_ge(route_v, 4)
            for t in range(NT):
                dve.max(top[:, t, :], probs[:, t, 0:EXPERTS]).then_inc(route_v, 1)
            dve.wait_ge(route_v, 4 + NT)
            dve.memset(top[:, :, TOPK:], -1.0).then_inc(route_v, 1)
            dve.wait_ge(route_v, 5 + NT)
            for t in range(NT):
                dve.match_replace(picked[:, t, :], top[:, t, :], probs[:, t, :], -2.0).then_inc(route_v, 1)
            dve.wait_ge(route_v, 5 + 2 * NT)
            dve.scalar_tensor_tensor(out=wr[:, :, 0:EXPERTS], in0=picked[:, :, 0:EXPERTS], scalar=-2.0,
                                     in1=probs[:, :, 0:EXPERTS], op0=ALU.is_equal, op1=ALU.mult).then_inc(route, 1)
            s0 = 5 + 2 * NT
            dve.wait_ge(route, 5)
            for part in range(3):
                dst = wpart[:, :, 32 * part:32 * part + GROUPS]
                dve.tensor_copy(dst, wr[:, :, :]).then_inc(route_v, 1)
                s0 += 1
                dve.wait_ge(route_v, s0)
                if part < 2:
                    dve.tensor_tensor(wr[:, :, :], wr[:, :, :], dst, ALU.subtract).then_inc(route_v, 1)
                    s0 += 1
                    dve.wait_ge(route_v, s0)

            def mlp_dve(j, g0, i, first):
                step = 3 if i is None else 2
                for c in range(NC):
                    s = slice(c * CH, (c + 1) * CH)
                    dve.wait_ge(silu_d, NC * j + c + 1)
                    dve.wait_ge(up_f, NC * j + c + 1)
                    if not first:
                        dve.wait_ge(hidw_d, NC * (j - 1) + c + 1)
                    dve.tensor_tensor(hid[:, s], silu_g[:, s], bank(g0 + step * c + 1), ALU.mult).then_inc(hid_d, 1)
                    dve.wait_ge(hid_d, NC * j + c + 1)
                    if i is None:
                        dve.wait_ge(wb_f, NC * j + c + 1)
                        weights = bank(g0 + 3 * c + 2)
                    else:
                        dve.wait_ge(ld_w[i], 8 * (j - i))
                        weights = w_unit[i][:, s]
                    if not first:
                        dve.wait_ge(hlo_d, NC * (j - 1) + c + 1)
                    dve.tensor_tensor(hidw[:, s], hid[:, s], weights, ALU.mult).then_inc(hidw_d, 1)

            mlp_dve(0, 2, None, True)
            dve.wait_ge(acc_open, 2)
            dve.tensor_copy(acc[:, :], x_res[:, :, :].rearrange("p t d -> p (t d)")).then_inc(acc_set, 1)
            mlp_dve(1, 2 + 6, None, False)
            with dve.Fori(0, HT // 2 - 1) as r:
                for i in range(2):
                    mlp_dve(2 * r + 2 + i, 2, i, False)

            for g in range(2):
                moments(2, g, down_d, HT - 1)
            for t in (4, 5):
                normed(2, t, acc_t, pre, out_v)

        @block.tensor
        def _(pe):
            def split_mm(dst, pairs, start=True):
                last = len(pairs) - 1
                for n, (lhs, rhs) in enumerate(pairs):
                    pe.matmul(dst, lhs[0], rhs[0], start=start and n == 0, stop=False, skip_group_check=True)
                    pe.matmul(dst, lhs[0], rhs[1], start=False, stop=False, skip_group_check=True)
                    mm = pe.matmul(dst, lhs[1], rhs[0], start=False, stop=n == last, skip_group_check=True)
                return mm

            def open_acc():
                for n in range(4 * NC * DK):
                    mm = pe.matmul(acc[:, n * P:(n + 1) * P], ident_b[:, :], ident_b[:, :], start=n % 4 == 0,
                                   stop=n % 4 == 3, skip_group_check=True)
                mm.then_inc(acc_open, 1)

            pe.wait_ge(consts, 5)
            open_acc()
            pe.wait_ge(ld_ctx, 32)
            for m in range(DM):
                for c in range(NC):
                    pe.matmul(bank(NC * m + c), inw[:, m * P:(m + 1) * P], ctxT[:, c * CH:(c + 1) * CH],
                              start=True, stop=True).then_inc(filled, 1)

            def proj(g, i, which, c):
                s = slice(c * CH, (c + 1) * CH)
                split_mm(bank(g), [((wqk_hi[i][:, (which * DK + k) * P:(which * DK + k + 1) * P],
                                     wqk_lo[i][:, (which * DK + k) * P:(which * DK + k + 1) * P]),
                                    (xT_hi[:, k, s], xT_lo[:, k, s])) for k in range(DK)]).then_inc(filled, 1)

            def values(g, t2):
                for j in range(2):
                    tok = slice((2 * t2 + j) * P, (2 * t2 + j + 1) * P)
                    mm = split_mm(bank(g)[:, j * 2 * HD:(j + 1) * 2 * HD],
                                  [((xT_hi[:, k, tok], xT_lo[:, k, tok]),
                                    (wv_hi[:, k * 2 * HD:(k + 1) * 2 * HD], wv_lo[:, k * 2 * HD:(k + 1) * 2 * HD]))
                                   for k in range(DK)], start=j == 0)
                mm.then_inc(filled, 1)

            def scores(g, b):
                for t in range(2):
                    qs = slice(b * SEQ + t * P, b * SEQ + (t + 1) * P)
                    ks = slice(b * SEQ, b * SEQ + (t + 1) * P)
                    dst = bank(g)[:, 0:P] if t == 0 else bank(g)[:, P:3 * P]
                    mm = split_mm(dst, [((q_hi[:, qs], q_lo[:, qs]), (k_hi[:, ks], k_lo[:, ks]))], start=t == 0)
                mm.then_inc(filled, 1)

            def turn_probs(g, b):
                for t in range(3):
                    mm = pe.transpose(bank(g)[:, t * P:(t + 1) * P], prob[:, b, t * P:(t + 1) * P], ident[:, :])
                mm.then_inc(filled, 1)

            def context(g, i, c):
                for j in range(2):
                    b = 2 * c + j
                    e = slice(i * HD, (i + 1) * HD)
                    split_mm(bank(g)[:, j * SEQ:(j + 1) * SEQ],
                             [((v_hi[:, 2 * b, e], v_lo[:, 2 * b, e]),
                               (pT_hi[:, b, 0:2 * P], pT_lo[:, b, 0:2 * P]))], start=j == 0)
                    mm = split_mm(bank(g)[:, j * SEQ + P:(j + 1) * SEQ],
                                  [((v_hi[:, 2 * b + 1, e], v_lo[:, 2 * b + 1, e]),
                                    (pT_hi[:, b, 2 * P:], pT_lo[:, b, 2 * P:]))], start=False)
                mm.then_inc(filled, 1)

            def out_projection(i, first_tile, end, signal):
                for t in range(first_tile, end):
                    s = slice(t * P, (t + 1) * P)
                    mm = split_mm(acc_t[:, t, :], [((z_hi[:, s], z_lo[:, s]), (wo_hi[i][:, :], wo_lo[i][:, :]))],
                                  start=False)
                    if signal:
                        mm.then_inc(out_proj, 1)

            pe.wait_ge(wqk_s, 1)
            for c in range(NC):
                pe.wait_ge(x_lo_s, DK * (c + 1))
                pe.wait_ge(pre_read, 1 + c)
                proj(4 + c, 0, 0, c)
            for c in range(NC):
                pe.wait_ge(pre_read, 3 + c)
                proj(6 + c, 0, 1, c)
            pe.wait_ge(wv_s, 1)
            for t in range(4):
                pe.wait_ge(bank_read, 1 + t)
                values(8 + t, t)
            pe.wait_ge(u_done, 2)
            pe.wait_ge(ld_xw, 32)
            for c in range(NC):
                pe.wait_ge(bank_read, 5 + c)
                for m in range(DM):
                    mm = pe.matmul(bank(12 + c)[0:XDBL, :], xw[:, m, :], u[:, m, c * CH:(c + 1) * CH],
                                   start=m == 0, stop=m == DM - 1)
                mm.then_inc(filled, 1)
            pe.wait_ge(bank_read, 8)
            for b in range(BATCH):
                if b >= 2:
                    pe.wait_ge(pre_read, 3 + b)
                scores(14 + b, b)
            pe.wait_ge(pre_read, 6)
            for m in range(DM):
                for c in range(NC):
                    pe.wait_ge(bank_read, 9 + NC * m + c)
                    pe.matmul(bank(18 + NC * m + c), dtw[:, m * P:(m + 1) * P], xdbl[0:RANK, c * CH:(c + 1) * CH],
                              start=True, stop=True).then_inc(filled, 1)

            def pair_pe(p, first, last):
                for i in range(2):
                    a = 2 * p + i
                    gb = PRE_UNITS + HALF_UNITS * i
                    before = PRE_ATTN + PAIR_UNITS * p + HALF_UNITS * i - 3
                    nxt = not (last and i == 1)
                    pt, z = (P_U, Z_U) if nxt else (P_U - 2, Z_U - 4)
                    if nxt:
                        pe.wait_ge(wqk_s, a + 2)
                        for c in range(NC):
                            if first and i == 0:
                                pe.wait_ge(pre_read, 7 + c)
                            pe.wait_ge(bank_read, before + Q_U + c)
                            proj(gb + Q_U + c, 1 - i, 0, c)
                    if not (first and i == 0):
                        out_projection(1 - i, NT // 2, NT, False)
                    for b in range(BATCH):
                        if first and i == 0 and b < 2:
                            pe.wait_ge(pre_read, 9 + b)
                        pe.wait_ge(bank_read, before + pt + b)
                        pe.wait_ge(probs_ready, 8 * a + 2 * b + 2)
                        turn_probs(gb + pt + b, b)
                    if nxt:
                        for c in range(NC):
                            pe.wait_ge(bank_read, before + K_U + c)
                            proj(gb + K_U + c, 1 - i, 1, c)
                    for c in range(NC):
                        pe.wait_ge(bank_read, before + z + c if nxt else before + pt + 2 * c + 5)
                        context(gb + z + c, i, c)
                    if nxt:
                        for b in range(BATCH):
                            pe.wait_ge(bank_read, before + S_U + b)
                            scores(gb + S_U + b, b)
                    else:
                        pe.wait_ge(bank_read, before + z + 5)
                    if first and i == 0:
                        pe.wait_ge(acc_set, 1)
                    pe.wait_ge(wo_s, a + 1)
                    out_projection(i, 0, NT // 2, last and i == 1)
                if not last:
                    pe.wait_ge(wv_s, p + 2)
                    for t in range(4):
                        pe.wait_ge(bank_read, PRE_ATTN + PAIR_UNITS * p + V_U + t - 3)
                        values(PRE_UNITS + V_U + t, t)

            pair_pe(0, True, False)
            with pe.Fori(1, PAIRS - 1) as p:
                pair_pe(p, False, False)
            pair_pe(PAIRS - 1, False, True)
            out_projection(1, NT // 2, NT, True)

            total_attn = PRE_ATTN + PAIR_UNITS * (PAIRS - 1) + 2 * HALF_UNITS - 8
            pe.wait_ge(bank_read, total_attn)
            for t in range(NT):
                b, l = t // 2, t % 2
                pe.wait_ge(gated, (3, 4, 6, 8)[b])
                if b < 3:
                    pe.wait_ge(x1_a, DM * b + DM)
                else:
                    pe.wait_ge(x1_v, 2)
                for m in range(DM):
                    mm = pe.matmul(acc_t[:, t, m * P:(m + 1) * P], y[:, m, b * SEQ + l * P:b * SEQ + (l + 1) * P],
                                   ident[:, :], start=False, stop=True, skip_group_check=True)
                mm.then_inc(turned, 1)
            for n in range(NC * DK):
                k, c = n % DK, n // DK
                for j in range(4):
                    if k == 0:
                        if 4 * c + j < 6:
                            pe.wait_ge(x2_a, 4 * c + j + 1)
                        else:
                            pe.wait_ge(x2_v, j - 1)
                    mm = pe.transpose(bank(n)[:, j * P:(j + 1) * P], x_res[:, 4 * c + j, k * P:(k + 1) * P],
                                      ident[:, :])
                mm.then_inc(x2_turned, 1)
            pe.wait_ge(rw_s, 1)
            for c in range(NC):
                pe.wait_ge(x2_lo, DK * (c + 1))
                s = slice(c * CH, (c + 1) * CH)
                split_mm(acc[0:NR, s], [((rw_hi[:, k, :], rw_lo[:, k, :]), (xT_hi[:, k, s], xT_lo[:, k, s]))
                                        for k in range(DK)]).then_inc(logit_t, 1)
            for t in range(NT):
                if t % 4 == 0:
                    pe.wait_ge(logit_read, t // 4 + 1)
                mm = pe.transpose(acc[:, 2 * CH + t * NR:2 * CH + (t + 1) * NR], logit_sb[:, t * P:(t + 1) * P],
                                  ident[0:NR, 0:NR])
            mm.then_inc(logit, 1)

            def turn_weights():
                pe.wait_ge(route_v, 5 + 2 * NT + 5)
                for t in range(NT):
                    mm = pe.transpose(acc[0:NSEL, 3 * CH + t * P // 2:3 * CH + (t + 1) * P // 2].bitcast(BF16),
                                      wpart[:, t, :], ident_b[:, :])
                mm.then_inc(wt_turned, 1)
                pe.wait_ge(ld_sel, 32)
                pe.wait_ge(wt_done, 1)
                for c in range(NC):
                    pe.matmul(acc[0:GROUPS, c * CH:(c + 1) * CH], sel[:, SPREAD_TILES * P:SPREAD_TILES * P + GROUPS],
                              wT[:, c * CH:(c + 1) * CH], start=True, stop=True).then_inc(groups_f, 1)

            def gate_up(j, i, g0, first):
                pe.wait_ge(gu_s, j + 1)
                for c in range(NC):
                    s = slice(c * CH, (c + 1) * CH)
                    for which, done in ((0, gate_f), (1, up_f)):
                        if which == 0 and not first:
                            pe.wait_ge(hidw_d, NC * (j - 1) + c + 1)
                        if which == 1 and c == 0 and not first:
                            pe.wait_ge(silu_d, NC * (j - 1) + 2)
                        if which == 1 and c == 1:
                            pe.wait_ge(silu_d, NC * j + 1)
                        split_mm(bank(g0 + 3 * c + which),
                                 [((gu_hi[i][:, (2 * which + k) * P:(2 * which + k + 1) * P],
                                    gu_lo[i][:, (2 * which + k) * P:(2 * which + k + 1) * P]),
                                   (xT_hi[:, k, s], xT_lo[:, k, s])) for k in range(DK)]).then_inc(done, 1)
                    if not first:
                        spread(j, g0, c, False)
                if first:
                    turn_weights()
                    for c in range(NC):
                        spread(j, g0, c, True)

            def spread(j, g0, c, first):
                if c == 0 and not first:
                    pe.wait_ge(hid_d, NC * (j - 1) + 2)
                if c == 1:
                    pe.wait_ge(hid_d, NC * j + 1)
                pe.matmul(bank(g0 + 3 * c + 2), sel[:, j * P:(j + 1) * P], wT[:, c * CH:(c + 1) * CH],
                          start=True, stop=True).then_inc(wb_f, 1)

            def gate_up_only(j, i):
                pe.wait_ge(gu_s, j + 1)
                for c in range(NC):
                    s = slice(c * CH, (c + 1) * CH)
                    for which, done in ((0, gate_f), (1, up_f)):
                        if c == 0:
                            pe.wait_ge(hidw_d, NC * (j - 1) + which + 1)
                        split_mm(bank(2 + 2 * c + which),
                                 [((gu_hi[i][:, (2 * which + k) * P:(2 * which + k + 1) * P],
                                    gu_lo[i][:, (2 * which + k) * P:(2 * which + k + 1) * P]),
                                   (xT_hi[:, k, s], xT_lo[:, k, s])) for k in range(DK)]).then_inc(done, 1)

            def down(j, i, signal_tiles):
                pe.wait_ge(dn_s, j + 1)
                for t in range(NT):
                    if t % 4 == 0:
                        pe.wait_ge(hlo_d, NC * j + t // 4 + 1)
                    s = slice(t * P, (t + 1) * P)
                    mm = split_mm(acc_t[:, t, :], [((h_hi[i][:, s], h_lo[i][:, s]),
                                                    (dn_hi[i][:, :], dn_lo[i][:, :]))], start=False)
                    if signal_tiles:
                        mm.then_inc(down_d, 1)
                if not signal_tiles:
                    mm.then_inc(down_d, 1)

            gate_up(0, 0, 2, True)
            pe.wait_ge(groups_d, NC)
            open_acc()
            gate_up(1, 1, 2 + 6, False)
            pe.wait_ge(acc_set, 2)
            with pe.Fori(0, HT // 2 - 1) as r:
                down(2 * r, 0, False)
                gate_up_only(2 * r + 2, 0)
                down(2 * r + 1, 1, False)
                gate_up_only(2 * r + 3, 1)
            down(HT - 2, 0, False)
            down(HT - 1, 1, True)


def kernel(x, ctx_1024, L0_attn_W_Q, L0_attn_W_K, L0_attn_W_V, L0_attn_W_O, L0_xattn_in_proj_w, L0_xattn_conv_w,
           L0_xattn_conv_b, L0_xattn_x_proj_w, L0_xattn_dt_proj_w, L0_xattn_dt_proj_b, L0_xattn_A_log, L0_xattn_D,
           L0_ffn_router_w, L0_ffn_gate_w, L0_ffn_up_w, L0_ffn_down_w, L0_ffn_shared_gate_w, L0_ffn_shared_up_w,
           L0_ffn_shared_down_w, L0_ffn_se_gate_w):
    import numpy as np
    import concourse.bacc as bacc
    from concourse.bass_utils import run_bass_kernel_spmd as run

    def parts(w, n):
        return np.asarray(w).T.reshape(n, P, -1).transpose(1, 0, 2)

    xf = np.asarray(x).reshape(TOK, D)
    heads = lambda w: np.asarray(w).transpose(0, 2, 1).reshape(HEADS, DK, P, HD)
    wq, wk, wv = heads(L0_attn_W_Q), heads(L0_attn_W_K), heads(L0_attn_W_V)
    wqk = np.stack([wq, wk], 1).transpose(0, 3, 1, 2, 4).reshape(HEADS, P, 4 * P)
    wv = wv.reshape(PAIRS, 2, DK, P, HD).transpose(0, 3, 2, 1, 4).reshape(PAIRS, P, 4 * P)
    wo = np.asarray(L0_attn_W_O).transpose(0, 2, 1)
    chan = np.concatenate([np.asarray(L0_xattn_conv_w)[:, 0, :], np.asarray(L0_xattn_conv_b)[:, None],
                           np.asarray(L0_xattn_dt_proj_b)[:, None], np.asarray(L0_xattn_D)[:, None],
                           np.asarray(L0_xattn_A_log)], 1).reshape(DM, P, -1).transpose(1, 0, 2)
    router = np.concatenate([np.asarray(L0_ffn_router_w), np.asarray(L0_ffn_se_gate_w),
                             np.zeros((1, D), np.float32)], 0)
    pad = np.zeros((HT * P - HID, D), np.float32)
    gw = np.concatenate([np.asarray(L0_ffn_gate_w).reshape(-1, D), np.asarray(L0_ffn_shared_gate_w), pad], 0)
    uw = np.concatenate([np.asarray(L0_ffn_up_w).reshape(-1, D), np.asarray(L0_ffn_shared_up_w), pad], 0)
    dw = np.concatenate([np.asarray(L0_ffn_down_w).transpose(0, 2, 1).reshape(-1, D),
                         np.asarray(L0_ffn_shared_down_w).T, pad], 0)
    turn = lambda w: w.reshape(HT, P, DK, P).transpose(0, 3, 2, 1).reshape(HT, P, DK * P)
    wf = np.concatenate([turn(gw), turn(uw), dw.reshape(HT, P, D)], 2)
    arrays = {
        "xT": parts(xf, DK), "x": xf.reshape(NT, P, D).transpose(1, 0, 2),
        "ctxT": np.asarray(ctx_1024).reshape(TOK, CTX).T, "inw": np.asarray(L0_xattn_in_proj_w).T,
        "xw": parts(L0_xattn_x_proj_w, DM), "dtw": np.asarray(L0_xattn_dt_proj_w).T, "chan": chan,
        "wqk": wqk, "wv": wv, "wo": wo, "rw": parts(router, DK), "wf": wf,
    }
    nc = bacc.Bacc("TRN2", target_bir_lowering=False, num_devices=1)
    feed, ins = {}, {}
    for name, a in arrays.items():
        feed[f"in_{name}"] = np.ascontiguousarray(a)
        ins[name] = nc.dram_tensor(f"in_{name}", a.shape, F32, kind="ExternalInput").ap()
    out = nc.dram_tensor("out_0", (TOK, D), F32, kind="ExternalOutput").ap()
    decoder_layer(nc, ins, out)
    r = run(nc, [feed], core_ids=[0])
    return r.results[0]["out_0"].reshape(BATCH, SEQ, D)
```
